# Optimizing a Trainium2 kernel written in Bass

```python
import numpy as np
import jax
import jax.numpy as jnp

def _softmax(x, axis=-1):
    return jax.nn.softmax(x, axis=axis)

def _gelu(x):
    return jax.nn.gelu(x, approximate=True)

def _silu(x):
    return jax.nn.silu(x)

def _sigmoid(x):
    return jax.nn.sigmoid(x)

def _layernorm(x, axis=-1, eps=1e-05):
    m = jnp.mean(x, axis=axis, keepdims=True)
    v = jnp.var(x, axis=axis, keepdims=True)
    return (x - m) / jnp.sqrt(v + eps)

def _scatter_add(tgt, idx, src, axis=0):
    return tgt.at[idx].add(src)

def _segment_sum(src, seg, n):
    return jax.ops.segment_sum(src, seg, n)
kernel_name = 'mk_adaln_ffn_d2_seqx_r8_590d56'

def setup_inputs(seed: int=0):
    np.random.seed(seed)
    _w = jnp.asarray

    def _rec_inputs():
        import jax
        import jax.numpy as jnp
        _rk = jax.random.key(seed)
        x = 7.22e-05 + 1 * jax.random.normal(jax.random.fold_in(_rk, 1), (16, 128, 256), jnp.float32)
        _lenS = 128 - jax.random.randint(jax.random.fold_in(_rk, 7), (16,), 0, max(1, 128 // 4) + 1, jnp.int32)
        _lenS2 = 128 - jax.random.randint(jax.random.fold_in(_rk, 8), (16,), 0, max(1, 128 // 4) + 1, jnp.int32)
        cond_2048 = jax.random.bernoulli(jax.random.fold_in(_rk, 11), 0.5063, (16, 256)).astype(jnp.float32)
        return (x, cond_2048)
    x, cond_2048 = _rec_inputs()

    def _L0_cond_setup():
        import jax, jax.numpy as jnp
        import numpy as np
        NH = 8
        NEG = -1e+30
        key = jax.random.key(seed)
        k1, k2, k3, k4 = jax.random.split(key, 4)
        B, D, T = (4, 128, 256)
        x = jax.random.normal(k1, (B, D, T), dtype=jnp.float32)
        mask = jax.random.randint(k2, (B, T), 0, 2).astype(jnp.float32)
        lim = float(np.sqrt(6.0 / (D + D)))
        Wq = jax.random.uniform(k3, (D, D), dtype=jnp.float32, minval=-lim, maxval=lim)
        Wo = jax.random.uniform(k4, (D, D), dtype=jnp.float32, minval=-lim, maxval=lim)
        return {'x': x, 'mask': mask, 'Wq': Wq, 'Wo': Wo}
    _L0_cond_all = _L0_cond_setup()
    _L0_cond_in = {k: v for k, v in _L0_cond_all.items() if k in ('Wq', 'Wo')}
    del _L0_cond_all

    def _L0_ffn_setup():
        import jax, jax.numpy as jnp
        import numpy as np
        HIDDEN = 256
        INTER = 688
        LUT_SIZE = 16

        def _ghost_linear(x, idx, lut):
            w = lut[idx]
            return jnp.einsum('bsh,oh->bso', x, w)
        key = jax.random.key(seed)
        k_x, k_lut, k_g, k_u, k_d = jax.random.split(key, 5)
        x = jax.random.normal(k_x, (2, 512, HIDDEN), dtype=jnp.float32)
        lut = jax.random.normal(k_lut, (LUT_SIZE,), dtype=jnp.float32) * 0.02
        gate_idx = jax.random.randint(k_g, (INTER, HIDDEN), 0, LUT_SIZE, dtype=jnp.int32)
        up_idx = jax.random.randint(k_u, (INTER, HIDDEN), 0, LUT_SIZE, dtype=jnp.int32)
        down_idx = jax.random.randint(k_d, (HIDDEN, INTER), 0, LUT_SIZE, dtype=jnp.int32)
        return {'x': x, 'lut': lut, 'gate_idx': gate_idx, 'up_idx': up_idx, 'down_idx': down_idx}
    _L0_ffn_all = _L0_ffn_setup()
    _L0_ffn_in = {k: v for k, v in _L0_ffn_all.items() if k in ('lut', 'gate_idx', 'up_idx', 'down_idx')}
    del _L0_ffn_all

    def _L1_cond_setup():
        import jax, jax.numpy as jnp
        import numpy as np
        HEADS = 16
        EPS = 1e-06

        def _rms_norm(x, g):
            xf = x.astype(jnp.float32)
            y = xf * jax.lax.rsqrt(jnp.mean(xf * xf, axis=-1, keepdims=True) + EPS)
            return y.astype(x.dtype) * g
        key = jax.random.key(seed)
        ks = jax.random.split(key, 6)
        b, n, dim, emb_dim = (4, 256, 256, 256)
        d_head = dim // HEADS
        return {'x': jax.random.normal(ks[0], (b, n, dim), jnp.float32), 'emb': jax.random.normal(ks[1], (b, 1, emb_dim), jnp.float32), 'W_emb': jax.random.normal(ks[2], (emb_dim, 2 * dim), jnp.float32) * emb_dim ** (-0.5), 'b_emb': jnp.zeros((2 * dim,), jnp.float32), 'g_norm': jnp.ones((dim,), jnp.float32), 'W_qkv': jax.random.normal(ks[3], (dim, 3 * dim), jnp.float32) * dim ** (-0.5), 'g_q': jnp.ones((d_head,), jnp.float32), 'g_k': jnp.ones((d_head,), jnp.float32), 'W_out': jax.random.normal(ks[4], (dim, dim), jnp.float32) * dim ** (-0.5)}
    _L1_cond_all = _L1_cond_setup()
    _L1_cond_in = {k: v for k, v in _L1_cond_all.items() if k in ('W_emb', 'b_emb', 'g_norm', 'W_qkv', 'g_q', 'g_k', 'W_out')}
    del _L1_cond_all

    def _L1_ffn_setup():
        import jax, jax.numpy as jnp
        import numpy as np
        D_MODEL = 256
        D_FF = 1024
        N_EXPERTS = 4
        B, S = (2, 256)
        key = jax.random.key(seed)
        ks = jax.random.split(key, 6)
        scale = 0.02
        return {'hidden_states': jax.random.normal(ks[0], (B, S, D_MODEL), dtype=jnp.float32), 'Wr': jax.random.normal(ks[1], (D_MODEL, N_EXPERTS), dtype=jnp.float32) * scale, 'br': jnp.zeros((N_EXPERTS,), dtype=jnp.float32), 'Wg': jax.random.normal(ks[2], (N_EXPERTS, D_MODEL, D_FF), dtype=jnp.float32) * scale, 'Wu': jax.random.normal(ks[3], (N_EXPERTS, D_MODEL, D_FF), dtype=jnp.float32) * scale, 'Wd': jax.random.normal(ks[4], (N_EXPERTS, D_FF, D_MODEL), dtype=jnp.float32) * scale}
    _L1_ffn_all = _L1_ffn_setup()
    _L1_ffn_in = {k: v for k, v in _L1_ffn_all.items() if k in ('Wr', 'br', 'Wg', 'Wu', 'Wd')}
    del _L1_ffn_all
    return {'x': x, 'cond_2048': cond_2048, 'L0_cond_Wq': _L0_cond_in['Wq'], 'L0_cond_Wo': _L0_cond_in['Wo'], 'L0_ffn_lut': _L0_ffn_in['lut'], 'L0_ffn_gate_idx': _L0_ffn_in['gate_idx'], 'L0_ffn_up_idx': _L0_ffn_in['up_idx'], 'L0_ffn_down_idx': _L0_ffn_in['down_idx'], 'L1_cond_W_emb': _L1_cond_in['W_emb'], 'L1_cond_b_emb': _L1_cond_in['b_emb'], 'L1_cond_g_norm': _L1_cond_in['g_norm'], 'L1_cond_W_qkv': _L1_cond_in['W_qkv'], 'L1_cond_g_q': _L1_cond_in['g_q'], 'L1_cond_g_k': _L1_cond_in['g_k'], 'L1_cond_W_out': _L1_cond_in['W_out'], 'L1_ffn_Wr': _L1_ffn_in['Wr'], 'L1_ffn_br': _L1_ffn_in['br'], 'L1_ffn_Wg': _L1_ffn_in['Wg'], 'L1_ffn_Wu': _L1_ffn_in['Wu'], 'L1_ffn_Wd': _L1_ffn_in['Wd']}

def reference(x, cond_2048, L0_cond_Wq, L0_cond_Wo, L0_ffn_lut, L0_ffn_gate_idx, L0_ffn_up_idx, L0_ffn_down_idx, L1_cond_W_emb, L1_cond_b_emb, L1_cond_g_norm, L1_cond_W_qkv, L1_cond_g_q, L1_cond_g_k, L1_cond_W_out, L1_ffn_Wr, L1_ffn_br, L1_ffn_Wg, L1_ffn_Wu, L1_ffn_Wd):
    import jax
    import jax.numpy as jnp

    def _L0_cond_ref(x, mask, Wq, Wo):
        import jax, jax.numpy as jnp
        import numpy as np
        NH = 8
        NEG = -1e+30
        B, D, T = x.shape
        dk = D // NH
        scale = 1.0 / jnp.sqrt(jnp.asarray(dk, x.dtype))
        xt = jnp.transpose(x, (0, 2, 1))
        q = xt @ Wq.T
        qh = q.reshape(B, T, NH, dk).transpose(0, 2, 1, 3)
        scores = scale * jnp.einsum('bhqd,bhkd->bhqk', qh, qh)
        cmask = mask[:, None, None, :]
        rmask = mask[:, None, :, None]
        logits = (scores * cmask + (1.0 - cmask) * NEG) * rmask
        attn = jax.nn.softmax(logits, axis=-1)
        ctx = jnp.einsum('bhqk,bhkd->bhqd', attn, qh)
        ctx = ctx.transpose(0, 2, 1, 3).reshape(B, T, D)
        out = ctx @ Wo.T
        return jnp.transpose(out, (0, 2, 1))

    def _L0_ffn_ref(x, lut, gate_idx, up_idx, down_idx):
        import jax, jax.numpy as jnp
        import numpy as np
        HIDDEN = 256
        INTER = 688
        LUT_SIZE = 16

        def _ghost_linear(x, idx, lut):
            w = lut[idx]
            return jnp.einsum('bsh,oh->bso', x, w)
        gate = _ghost_linear(x, gate_idx, lut)
        up = _ghost_linear(x, up_idx, lut)
        h = jax.nn.silu(gate) * up
        return _ghost_linear(h, down_idx, lut)

    def _L1_cond_ref(x, emb, W_emb, b_emb, g_norm, W_qkv, g_q, g_k, W_out):
        import jax, jax.numpy as jnp
        import numpy as np
        HEADS = 16
        EPS = 1e-06

        def _rms_norm(x, g):
            xf = x.astype(jnp.float32)
            y = xf * jax.lax.rsqrt(jnp.mean(xf * xf, axis=-1, keepdims=True) + EPS)
            return y.astype(x.dtype) * g
        b, n, dim = x.shape
        h = HEADS
        d = dim // h
        scale_shift = emb @ W_emb + b_emb
        scale, shift = jnp.split(scale_shift, 2, axis=-1)
        xn = _rms_norm(x, g_norm) * (1.0 + scale) + shift
        qkv = xn @ W_qkv
        qkv = qkv.reshape(b, n, 3, h, d)
        q, k, v = jnp.moveaxis(qkv, 2, 0)
        q = jnp.swapaxes(q, 1, 2)
        k = jnp.swapaxes(k, 1, 2)
        v = jnp.swapaxes(v, 1, 2)
        q = _rms_norm(q, g_q)
        k = _rms_norm(k, g_k)
        logits = jnp.einsum('bhqd,bhkd->bhqk', q, k) * d ** (-0.5)
        attn = jax.nn.softmax(logits, axis=-1)
        o = jnp.einsum('bhqk,bhkd->bhqd', attn, v)
        o = jnp.swapaxes(o, 1, 2).reshape(b, n, dim)
        return o + o @ W_out

    def _L1_ffn_ref(hidden_states, Wr, br, Wg, Wu, Wd):
        import jax, jax.numpy as jnp
        import numpy as np
        D_MODEL = 256
        D_FF = 1024
        N_EXPERTS = 4
        B, S = (2, 256)
        b, s, d = hidden_states.shape
        x = hidden_states.reshape(-1, d)
        logits = x @ Wr + br
        probs = jax.nn.softmax(logits, axis=-1)
        top_w, top_idx = jax.lax.top_k(probs, 1)
        g = jnp.einsum('td,edf->tef', x, Wg)
        u = jnp.einsum('td,edf->tef', x, Wu)
        h = jax.nn.silu(g) * u
        y = jnp.einsum('tef,efd->ted', h, Wd)
        sel = jnp.take_along_axis(y, top_idx[:, :, None], axis=1)[:, 0]
        out = sel * top_w
        return out.reshape(b, s, d)
    x = x + _L0_ffn_ref(_L0_cond_ref(x, cond_2048, L0_cond_Wq, L0_cond_Wo), L0_ffn_lut, L0_ffn_gate_idx, L0_ffn_up_idx, L0_ffn_down_idx)
    x = x + _L1_ffn_ref(_L1_cond_ref(x, cond_2048[:, None, :], L1_cond_W_emb, L1_cond_b_emb, L1_cond_g_norm, L1_cond_W_qkv, L1_cond_g_q, L1_cond_g_k, L1_cond_W_out), L1_ffn_Wr, L1_ffn_br, L1_ffn_Wg, L1_ffn_Wu, L1_ffn_Wd)
    return x

_drawn_inputs = setup_inputs


def setup_inputs(seed=0):
    import zlib

    import numpy as np

    out = dict(_drawn_inputs(seed))
    spreads = {'L1_cond_b_emb': (0.0, 0.1),
     'L1_cond_g_norm': (1.0, 0.2),
     'L1_cond_g_q': (1.0, 0.2),
     'L1_cond_g_k': (1.0, 0.2),
     'L1_ffn_br': (0.0, 0.1)}
    factors = {}
    for name, (base, spread) in spreads.items():
        noise = np.random.default_rng([zlib.crc32(name.encode()), seed]).standard_normal(out[name].shape)
        drawn = base * np.exp(spread * noise) if base else spread * noise
        out[name] = jnp.asarray(drawn.astype(out[name].dtype))
    for name, factor in factors.items():
        out[name] = (out[name] * factor).astype(out[name].dtype)
    return out
```

```python
from contextlib import ExitStack

import numpy as np

import concourse.bass as bass
from concourse import mybir

F32 = mybir.dt.float32
BF16 = mybir.dt.bfloat16
I32 = mybir.dt.int32
ALU = mybir.AluOpType
ACT = mybir.ActivationFunctionType
AX = mybir.AxisListType

P = 128
B, D, T = 16, 128, 256
KT = T // P
H0, DK0 = 8, 16
PAIRS = H0 // 2
SCALE0 = DK0 ** -0.5
INTER = 688
MT = -(-INTER // P)
MLAST = INTER - (MT - 1) * P
LUT = 16
H1, DK1 = 16, 16
EPS = 1e-6
E, FF = 4, 1024
FT = FF // P
TOK = B * D
CH = 512
TPC = CH // P
SLOTS = TOK // P + E - 1
ROW = 2 * T + 2
NEG = 1e30
DUMMY = 2 * TOK

GCOLS = KT * INTER
WCOLS = 2 * GCOLS + MT * T
LCH = 8
LW = WCOLS // LCH

C_ID, C_TRI, C_SQ, C_SK, C_EV, C_ROWS = 0, P, 2 * P, 2 * P + 1, 2 * P + 2, 2 * P + 3
C_N = C_ROWS + SLOTS


def constants():
    c = np.zeros((P, C_N), np.float32)
    p = np.arange(P)
    c[:, C_ID:C_ID + P] = np.eye(P)
    c[:, C_TRI:C_TRI + P] = p[:, None] < p[None, :]
    slot, r = p % 64 // 16, p % 64
    c[:, C_SQ] = np.where(slot == 2, -1, 0)
    c[:, C_SK] = np.where(slot == 1, -1, np.where((r == 48) | (r == 49), 1, 0))
    c[:, C_EV] = (r == 48) | (r == 49)
    c[:, C_ROWS:] = np.arange(SLOTS)
    return c


def program(nc, x, cond, condT, consts, wqT, woT, lut, idx_gu, idx_d, w_emb, b_emb, g_norm, w_qkv, g_q, g_k,
            w_out, w_outT, w_r, b_r, w_g, w_u, w_d, out, routed):
    with ExitStack() as ctx:
        def sb(name, shape, dt=F32):
            return ctx.enter_context(nc.sbuf_tensor(name, shape, dt))

        def sem(name):
            return ctx.enter_context(nc.semaphore(name))

        PA, PB, PC, PD = (ctx.enter_context(nc.psum_tensor(n, [P, 1024], F32)) for n in ("PA", "PB", "PC", "PD"))

        cst = sb("cst", [P, C_N])
        ident = cst[:, C_ID:C_ID + P]
        identb = sb("identb", [P, P], BF16)
        ones = sb("ones", [P, P])
        half_neg = sb("half_neg", [P, 64])
        ck = sb("ck", [P, KT, B])
        rows = sb("rows", [P, B, ROW])

        HALF = E * KT * FF
        arena = sb("arena", [P, 3 * HALF])
        at = [0]

        def f32(*shape):
            n = int(np.prod(shape))
            v = arena[:, at[0]:at[0] + n]
            at[0] += n
            return v

        def bf(*shape):
            n = int(np.prod(shape)) // 2
            v = arena[:, at[0]:at[0] + n].bitcast(BF16)
            at[0] += n
            return v

        def hi_lo(k):
            v = arena[:, k * HALF:(k + 1) * HALF].bitcast(BF16)
            return v[:, 0:HALF], v[:, HALF:2 * HALF]

        (wg_hi, wg_lo), (wu_hi, wu_lo), (wd_hi, wd_lo) = hi_lo(0), hi_lo(1), hi_lo(2)

        xall = f32(B, T).rearrange("p (b t) -> p b t", b=B)
        mk = f32(B, T).rearrange("p (b t) -> p b t", b=B)
        c_hi = bf(KT, TOK).rearrange("p (k t) -> p k t", k=KT)
        c_lo = bf(KT, TOK).rearrange("p (k t) -> p k t", k=KT)
        w0_hi, w0_lo = bf(WCOLS), bf(WCOLS)
        at_lookup = at[0]
        idx = f32(LW).bitcast(I32)
        bit = [f32(LW).bitcast(I32) for _ in range(4)]
        pick = [f32(LW) for _ in range(4)]
        at[0] = at_lookup
        h_hi = bf(MT, CH).rearrange("p (m t) -> p m t", m=MT)
        h_lo = bf(MT, CH).rearrange("p (m t) -> p m t", m=MT)
        assert max(at[0], at_lookup + 9 * LW) <= 3 * HALF

        def w0(w, which, kt, m):
            o = which * GCOLS + kt * INTER + m * P
            return w[:, o:o + P]

        def w0d(w, m):
            n = P if m < MT - 1 else MLAST
            o = 2 * GCOLS + m * T
            return w[0:n, o:o + T]

        SMALL = 5248
        small = sb("small", [P, SMALL])
        small_at = [0]

        def part(shape, dt=F32):
            n = int(np.prod(shape[1:])) * (1 if dt == F32 else 2) // (1 if dt == F32 else 4)
            v = small[:, small_at[0]:small_at[0] + n]
            small_at[0] += n
            assert small_at[0] <= SMALL
            if dt != F32:
                v = v.bitcast(dt)
            names = "abcd"[:len(shape) - 1]
            if len(names) == 1:
                return v
            return v.rearrange(f"p ({' '.join(names)}) -> p {' '.join(names)}", **dict(zip(names, shape[1:])))

        wq1 = sb("wq1", [P, P])
        wq3 = sb("wq3", [P, PAIRS, 2, 4, 16])
        wo1 = sb("wo1", [P, P])
        lutb = sb("lutb", [P, LUT])
        lutd = sb("lutd", [P, LUT // 2])
        nck = sb("nck", [P, KT, B])
        nnck = sb("nnck", [P, KT, B])
        kbias = sb("kbias", [P, KT, B])
        kb = sb("kb", [P, 2, KT])
        xs = part([P, 2, T])
        xm = part([P, 2, T])
        om = part([P, 2, KT, T])
        A = part([P, PAIRS * T], BF16)
        qs = part([P, 2, PAIRS * T], BF16)
        ks = part([P, 2, PAIRS * T], BF16)
        nmax = sb("nmax", [P, PAIRS, 2, KT])
        mcol = part([P, KT, PAIRS, P], BF16)
        probs = sb("probs", [P, 4, 1024])
        vu = sb("vu", [P, 2, KT, H0, DK0 + 1])
        rden = sb("rden", [P, KT, H0])
        cn = sb("cn", [P, KT, H0, DK0])
        cT = sb("cT", [P, T])

        wst = sb("wst", [P, 3, FF])
        sil = wst[:, 0, :].rearrange("p (n t) -> p n t", n=2)
        hf = wst[:, 1, :].rearrange("p (n t) -> p n t", n=2)

        small_at[0] = 0
        wemb = sb("wemb", [P, KT, 2 * T])
        bemb = sb("bemb", [P, 4])
        gnorm = sb("gnorm", [P, KT])
        gcol = sb("gcol", [P, KT, B])
        scol = sb("scol", [P, KT, B])
        wqkv = sb("wqkv", [P, KT, 3 * T])
        gqk = sb("gqk", [P, 2, DK1])
        gg = sb("gg", [P, DK1])
        gb = sb("gb", [P, 1])
        w2 = sb("w2", [P, KT, T + E])
        w2T = sb("w2T", [P, KT, T])
        wr = sb("wr", [P, KT, E])
        br = sb("br", [P, E])
        sqx = sb("sqx", [P, T])
        ssq = sb("ssq", [P, 2])
        rstd = sb("rstd", [P, 2])
        xr = part([P, T])
        xnT = part([P, KT, P])
        sq = part([P, 2 * T])
        msr = sb("msr", [P, 2 * H1])
        ms = sb("ms", [P, 2 * H1])
        rs = sb("rs", [P, 2 * H1])
        qk = part([P, 2, H1, DK1])
        q4 = part([P, H1, 4, DK1], BF16)
        k4 = part([P, H1, 4, DK1], BF16)
        qT = part([P, 1024], BF16)
        kT = part([P, 1024], BF16)
        v1 = sb("v1", [P, 2, H1, DK1 + 1])
        rden1 = sb("rden1", [P, H1])
        on = part([P, H1, DK1])
        oT = part([P, T])
        lg = sb("lg", [P, B, E])
        eps = sb("eps", [P, 1])
        wz = sb("wz", [P, 1])

        lmx = sb("lmx", [P, B])
        oh = sb("oh", [P, B, E])
        taken = sb("taken", [P, B])
        ex = sb("ex", [P, B, E])
        es = sb("es", [P, B])
        tot = sb("tot", [P, E, B])
        run = sb("run", [P, E, B])
        cnt = sb("cnt", [P, E], I32)
        ntile = sb("ntile", [P, E])
        first = sb("first", [P, E])
        place = sb("place", [P, B, E])
        slotf = sb("slotf", [P, B])
        slot = sb("slot", [P, B], I32)
        tef = sb("tef", [P, SLOTS])
        te = sb("te", [P, SLOTS], I32)
        pad = wst[:, 2, 0:ROW]
        small_at[0] = 0
        xin = part([P, 2, T])
        xres = part([P, 2, ROW - T])
        gs, hh = probs[:, 0, :], probs[:, 1, :]
        hT_hi, hT_lo = (probs[:, 2, n * 512:(n + 1) * 512].bitcast(BF16) for n in range(2))
        xT_hi, xT_lo = (probs[:, 3, n * T:(n + 1) * T].bitcast(BF16).rearrange("p (n t) -> p n t", n=2) for n in range(2))
        yo = probs[:, 3, 512:1024].rearrange("p (n t) -> p n t", n=2)
        tokn = sb("tokn", [P, 2], I32)

        S = {}

        def new(*names):
            for n in names:
                S[n] = sem("s_" + n)

        new("x", "mk", "cst", "ck", "wq", "lut", "small3", "wqkv", "idx", "pad", "scat", "ones", "init", "wq3", "kprep",
            "lutd", "bit", "pick", "w0h", "w0l",
            "xm", "om", "pq", "a", "qk", "sa", "max", "mc", "mt", "q2", "st", "ex", "v", "vu", "ctx", "rd", "cn",
            "ct", "ce", "wo", "ch", "cl",
            "g", "sil", "u", "hf", "hh", "hl", "dn", "x1",
            "w2a", "w2r", "w2", "emb", "gcol", "gg", "gb", "gmx",
            "ssq", "rstd", "xr", "xt3", "xnT", "qkv", "sq", "ms", "rs", "qkn", "qg", "h4", "l4", "qT", "qTe", "kTe",
            "s3", "e3", "v1", "c3", "rd3", "on", "oT", "oTe", "t3", "te3", "lg",
            "wst0", "wst1", "wst2", "wsh0", "wsh1", "wsh2", "wsl0", "wsl1", "wsl2",
            "mean", "rv", "var", "r", "rx", "rp", "tok", "te", "slot", "rows",
            "xld0", "xld1", "res0", "res1", "tT", "th", "tl", "gu", "gs", "uu", "hm", "hT", "hTh", "hTl", "y", "yo", "so0", "so1", "idn")

        def unless_first(engine, semaphore, count):
            if not (isinstance(count, int) and count == 0):
                engine.wait_ge(semaphore, count)

        block = ctx.enter_context(nc.Block())
        LAST = B - 1
        U = B // 2

        @block.sync
        def _(sp):
            sp.dma_start(xall, x.rearrange("b d t -> d b t")).then_inc(S["x"], 16)
            sp.dma_start(cst[:], consts).then_inc(S["cst"], 16)
            sp.dma_start(wq1[:], wqT).then_inc(S["wq"], 16)
            sp.dma_start(mk, cond.rearrange("(o b) t -> o b t", o=1).broadcast_to([P, B, T])).then_inc(S["mk"], 16)
            sp.dma_start(wo1[:], woT).then_inc(S["wq"], 16)
            for c in range(LCH):
                if c:
                    sp.wait_ge(S["bit"], 4 * c)
                lo, hi = c * LW, (c + 1) * LW
                g1 = min(hi, 2 * GCOLS)
                n = 0
                if lo < g1:
                    sp.dma_start(idx[:, 0:g1 - lo], idx_gu[:, lo:g1]).then_inc(S["idx"], 16)
                if hi > g1:
                    a0 = max(lo, g1)
                    sp.dma_start(idx[:, a0 - lo:LW], idx_d[:, a0 - 2 * GCOLS:hi - 2 * GCOLS]).then_inc(S["idx"], 16)
            sp.wait_ge(S["x1"], B)
            sp.wait_ge(S["pad"], 16 * SLOTS)

            def weight_pieces(u):
                for n, w in enumerate((w_g, w_u, w_d)):
                    unless_first(sp, S[f"wsl{n}"], u)
                    sp.dma_start(wst[:, n, :], w[:, bass.ds(u * FF, FF)]).then_inc(S[f"wst{n}"], 16)
            weight_pieces(0)
            with sp.Fori(1, U) as u:
                weight_pieces(u)
            sp.wait_ge(S["scat"], 16 * B)
            def load_input(j):
                if j >= 2:
                    sp.wait_ge(S["tT"], j - 1)
                sp.dma_start(xin[:, j % 2, :], routed[j * P:(j + 1) * P, 0:T]).then_inc(S[f"xld{j % 2}"], 16)

            load_input(0)
            for j in range(SLOTS):
                if j + 1 < SLOTS:
                    load_input(j + 1)
                if j >= 2:
                    sp.wait_ge(S["yo"], j - 1)
                    sp.wait_ge(S["idn"], j - 1)
                sp.dma_start(xres[:, j % 2, :], routed[j * P:(j + 1) * P, T:ROW]).then_inc(S[f"res{j % 2}"], 16)

        @block.gpsimd
        def _(pool):
            nc.gpsimd.memset(ones[:], 1.0).then_inc(S["ones"], 1)
            nc.gpsimd.memset(half_neg[:], -0.5).then_inc(S["ones"], 1)
            nc.gpsimd.memset(wz[:], 0.0).then_inc(S["ones"], 1)
            nc.gpsimd.memset(pad, 0.0).then_inc(S["ones"], 1)
            nc.gpsimd.memset(vu[:], 1.0).then_inc(S["ones"], 1)
            nc.gpsimd.memset(v1[:], 1.0).then_inc(S["ones"], 1)
            nc.gpsimd.iota(rows[:, :, ROW - 1:ROW].bitcast(I32), pattern=[[P, B], [0, 1]], base=0,
                           channel_multiplier=1).then_inc(S["tok"], 1)
            nc.gpsimd.memset(eps[:], EPS).then_inc(S["ones"], 1)
            pool.wait_ge(S["ones"], 4)
            nc.gpsimd.memset(pad[:, ROW - 1:ROW].bitcast(I32), DUMMY).then_inc(S["ones"], 1)

            pool.wait_ge(S["x"], 16)
            pool.wait_ge(S["mk"], 16)

            def inputs(b, par):
                pool.wait_ge(S["pq"], 2 * (b - 1))
                pool.wait_ge(S["v"], b - 1)
                pool.wait_ge(S["ex"], 4 * (b - 1))
                first_inputs(b, par)

            def first_inputs(b, par):
                nc.gpsimd.tensor_tensor(xm[:, par, :].unsqueeze(1), xall[:, bass.ds(b, 1), :], mk[:, bass.ds(b, 1), :],
                                        ALU.mult).then_inc(S["xm"], 1)
                nc.gpsimd.tensor_copy(xs[:, par, :].unsqueeze(1), xall[:, bass.ds(b, 1), :]).then_inc(S["xm"], 1)
                nc.gpsimd.tensor_copy(kb[:, par, :].unsqueeze(2), kbias[:, :, bass.ds(b, 1)]).then_inc(S["xm"], 1)

            pool.wait_ge(S["kprep"], 3)
            first_inputs(0, 0)
            first_inputs(1, 1)
            with pool.Fori(1, U) as u:
                inputs(2 * u, 0)
                inputs(2 * u + 1, 1)

            pool.wait_ge(S["ones"], 8)
            for j in range(SLOTS):
                pool.dma_start(routed[j * P:(j + 1) * P, :], pad).then_inc(S["pad"], 16)

            def split(n, dst_hi, dst_lo, u):
                pool.wait_ge(S[f"wst{n}"], 16 * (u + 1))
                o = bass.ds(u * FF, FF)
                nc.gpsimd.tensor_tensor(dst_hi[:, o], wst[:, n, :], wz[:].broadcast_to([P, FF]), ALU.add).then_inc(S[f"wsh{n}"], 1)
                pool.wait_ge(S[f"wsh{n}"], u + 1)
                nc.gpsimd.tensor_tensor(dst_lo[:, o], wst[:, n, :], dst_hi[:, o], ALU.subtract).then_inc(S[f"wsl{n}"], 1)

            def norms(b, par, u, back):
                pool.wait_ge(S["ssq"], b + 1)
                if back:
                    pool.wait_ge(S["xr"], b - 1)
                nc.gpsimd.tensor_tensor(rstd[:, par:par + 1], ssq[:, par:par + 1], eps[:], ALU.add).then_inc(S["var"], 1)
                pool.wait_ge(S["var"], b + 1)
                nc.gpsimd.tensor_tensor(rstd[:, par:par + 1], rstd[:, par:par + 1], half_neg[:, 0:1],
                                        ALU.pow).then_inc(S["rstd"], 1)
                pool.wait_ge(S["ms"], b + 1)
                unless_first(pool, S["qkn"], b)
                nc.gpsimd.tensor_tensor(rs[:], ms[:], half_neg[:, 0:2 * H1], ALU.pow).then_inc(S["rs"], 1)
                pool.wait_ge(S["qkn"], b + 1)
                nc.gpsimd.tensor_tensor(qk[:, 0], qk[:, 0], gg[:].unsqueeze(1).broadcast_to([P, H1, DK1]),
                                        ALU.mult).then_inc(S["qg"], 1)
                if par == 0:
                    split(0, wg_hi, wg_lo, u)
                    split(1, wu_hi, wu_lo, u)
                else:
                    split(2, wd_hi, wd_lo, u)

            pool.wait_ge(S["x1"], B)
            pool.wait_ge(S["gg"], 1)
            norms(0, 0, 0, False)
            norms(1, 1, 0, False)
            with pool.Fori(1, U) as u:
                norms(2 * u, 0, u, True)
                norms(2 * u + 1, 1, u, True)

            pool.wait_ge(S["pad"], 16 * SLOTS)
            pool.wait_ge(S["slot"], 1)
            pool.wait_ge(S["rows"], 1)
            pool.wait_ge(S["tok"], 1)
            for j in range(B):
                pool.indirect_dma_start(routed, bass.IndirectOffsetOnAxis(ap=slot[:, j:j + 1], axis=0),
                                        rows[:, j, :], None).then_inc(S["scat"], 16)
            for j in range(SLOTS):
                pool.wait_ge(S["yo"], j + 1)
                pool.wait_ge(S["idn"], j + 1)
                pool.indirect_dma_start(out, bass.IndirectOffsetOnAxis(ap=tokn[:, j % 2:j % 2 + 1], axis=0),
                                        yo[:, j % 2, :], None, bounds_check=TOK - 1,
                                        oob_is_err=False).then_inc(S[f"so{j % 2}"], 16)
            for j in range(2):
                pool.wait_ge(S[f"so{j}"], 16 * ((SLOTS - j + 1) // 2))

        @block.scalar
        def _(act):
            act.dma_start(ck[:], condT).then_inc(S["ck"], 16)
            act.dma_start(lutb[:], lut.broadcast_to([P, LUT])).then_inc(S["lut"], 16)
            for dst, src in ((wemb[:], w_emb.rearrange("(k p) n -> p k n", p=P)), (bemb[:], b_emb), (gnorm[:], g_norm),
                             (gqk[:, 0, :], g_q.broadcast_to([P, DK1])), (gqk[:, 1, :], g_k.broadcast_to([P, DK1])),
                             (w2[:, :, 0:T], w_out.rearrange("(k p) n -> p k n", p=P)),
                             (w2T[:], w_outT.rearrange("(k p) n -> p k n", p=P)),
                             (wr[:], w_r.rearrange("(k p) n -> p k n", p=P)), (br[:], b_r.broadcast_to([P, E]))):
                act.dma_start(dst, src).then_inc(S["small3"], 16)
            act.dma_start(wqkv[:], w_qkv.rearrange("(k p) n -> p k n", p=P)).then_inc(S["wqkv"], 16)

            def fixed():
                act.wait_ge(S["cst"], 16)

            fixed()

            def round_q(b):
                for n in range(2):
                    act.wait_ge(S["pq"], 2 * b + n + 1)
                    unless_first(act, S["qk"], 4 * b)
                    nc.scalar.activation(A[:, n * 512:(n + 1) * 512], PA[:, n * 512:(n + 1) * 512], ACT.Identity,
                                         bias=cst[:, C_EV:C_EV + 1]).then_inc(S["a"], 1)

            def values(b, par, back):
                act.wait_ge(S["v"], b + 1)
                if back:
                    act.wait_ge(S["ctx"], b - 1)
                nc.scalar.copy(vu[:, par, :, :, 0:DK0], PD[:, 0:T].rearrange("p (k h d) -> p k h d", k=KT, h=H0)
                               ).then_inc(S["vu"], 1)

            def exps(b, par):
                unless_first(act, S["ctx"], b)
                act.wait_ge(S["xm"], 3 * b + 3)
                for c in range(4):
                    act.wait_ge(S["st"], 4 * b + c + 1)
                    nc.scalar.activation(probs[:, c, :], PC[:], ACT.Exp, scale=SCALE0, bias=kb[:, par, c % KT:c % KT + 1]).then_inc(S["ex"], 1)

            def context_out(b):
                act.wait_ge(S["ct"], b + 1)
                unless_first(act, S["wo"], b)
                nc.scalar.copy(cT[:], PD[:, 512:512 + T]).then_inc(S["ce"], 1)
                act.wait_ge(S["wo"], b + 1)
                fixed()
                nc.scalar.copy(c_hi[:, :, bass.ds(b * P, P)],
                               PD[:, 512:512 + T].rearrange("p (k t) -> p k t", k=KT)).then_inc(S["ch"], 1)

            round_q(0)
            act.wait_ge(S["ones"], 6)
            act.wait_ge(S["kprep"], 3)

            def body(i, par, back):
                round_q(i)
                values(i - 1, 1 - par, back)
                exps(i - 1, 1 - par)
                context_out(i - 1)

            body(1, 1, False)
            body(2, 0, False)
            with act.Fori(1, U - 1) as u:
                body(2 * u + 1, 1, True)
                body(2 * u + 2, 0, True)
            body(LAST, 1, True)
            values(LAST, 1, True)
            exps(LAST, 1)
            context_out(LAST)

            def gate_chunk(c):
                for m in range(MT):
                    n = P if m < MT - 1 else MLAST
                    g = PA[0:n, (m % 2) * 512:(m % 2 + 1) * 512]
                    act.wait_ge(S["g"], MT * c + m + 1)
                    if m >= 2:
                        act.wait_ge(S["hf"], MT * c + m - 1)
                    else:
                        unless_first(act, S["hf"], MT * c)
                    nc.scalar.activation(sil[0:n, m % 2, :], g, ACT.Silu).then_inc(S["sil"], 1)
                    act.wait_ge(S["hf"], MT * c + m + 1)
                    unless_first(act, S["dn"], MT * c)
                    nc.scalar.copy(h_hi[0:n, m, :], hf[0:n, m % 2, :]).then_inc(S["hh"], 1)

            gate_chunk(0)
            with act.Fori(1, TOK // CH) as c:
                gate_chunk(c)

            def front(b, par, back):
                act.wait_ge(S["x1"], B)
                unless_first(act, S["ssq"], b)
                if back:
                    act.wait_ge(S["rstd"], b - 1)
                fixed()
                nc.scalar.activation(sqx[:].unsqueeze(1), rows[:, bass.ds(b, 1), T:2 * T], ACT.Square,
                                     scale=T ** -0.5, accum_out=ssq[:, par:par + 1]).then_inc(S["ssq"], 1)

            def squares(b, par, back):
                act.wait_ge(S["qkv"], 2 * b + 1)
                unless_first(act, S["ms"], b)
                nc.scalar.activation(sq, PB[:, 0:512], ACT.Square, scale=DK1 ** -0.5).then_inc(S["sq"], 1)
                act.wait_ge(S["qkv"], 2 * b + 2)
                if back:
                    act.wait_ge(S["c3"], b - 1)
                nc.scalar.copy(v1[:, par, :, 0:DK1], PB[:, 512:512 + T].rearrange("p (h d) -> p h d", h=H1)
                               ).then_inc(S["v1"], 1)

            def high_parts(b):
                act.wait_ge(S["qg"], b + 1)
                unless_first(act, S["qT"], 2 * b)
                unless_first(act, S["l4"], 2 * b)
                nc.scalar.copy(q4[:, :, 0:2, :], qk[:, 0].unsqueeze(2).broadcast_to([P, H1, 2, DK1])).then_inc(S["h4"], 1)
                nc.scalar.copy(k4[:, :, 0::2, :], qk[:, 1].unsqueeze(2).broadcast_to([P, H1, 2, DK1])).then_inc(S["h4"], 1)

            def exps1(b):
                unless_first(act, S["c3"], b)
                for c in range(2):
                    act.wait_ge(S["s3"], 2 * b + c + 1)
                    nc.scalar.activation(probs[:, c, :], PA[:], ACT.Exp, scale=DK1 ** -0.5, bias=gb[:]).then_inc(S["e3"], 1)

            def qT_out(b):
                act.wait_ge(S["qT"], 2 * b + 1)
                unless_first(act, S["s3"], 2 * b)
                nc.scalar.copy(qT, PC[:, 0:512].bitcast(BF16)).then_inc(S["qTe"], 1)

            def result(b):
                act.wait_ge(S["oT"], b + 1)
                unless_first(act, S["t3"], b)
                nc.scalar.copy(oT, PD[:, 512:512 + T]).then_inc(S["oTe"], 1)
                act.wait_ge(S["t3"], b + 1)
                fixed()
                nc.scalar.copy(rows[:, bass.ds(b, 1), 0:T], PD[:, 512:512 + T].unsqueeze(1)).then_inc(S["te3"], 1)

            act.wait_ge(S["gb"], 1)

            def body1(i, par, back):
                front(i, par, back)
                qT_out(i - 1)
                squares(i, par, back)
                exps1(i - 1)
                high_parts(i)
                result(i - 1)

            front(0, 0, False)
            squares(0, 0, False)
            high_parts(0)
            body1(1, 1, False)
            with act.Fori(1, U) as u:
                body1(2 * u, 0, True)
                body1(2 * u + 1, 1, True)
            qT_out(LAST)
            exps1(LAST)
            result(LAST)

            act.wait_ge(S["rx"], 1)
            nc.scalar.activation(ex[:], ex[:], ACT.Exp).then_inc(S["rx"], 1)

            def x_high(j, par):
                act.wait_ge(S["tT"], j + 1)
                nc.scalar.copy(xT_hi[:, par, :], PD[:, 0:T]).then_inc(S["th"], 1)

            def gate(j):
                act.wait_ge(S["gu"], j + 1)
                unless_first(act, S["hm"], j)
                nc.scalar.activation(gs, PA[:], ACT.Silu).then_inc(S["gs"], 1)

            def h_high(j):
                act.wait_ge(S["hT"], j + 1)
                unless_first(act, S["y"], j)
                nc.scalar.copy(hT_hi, PC[:]).then_inc(S["hTh"], 1)

            def tile(j, par, more=True):
                h_high(j - 1)
                gate(j)
                if more:
                    x_high(j + 1, 1 - par)

            x_high(0, 0)
            gate(0)
            x_high(1, 1)
            tile(1, 1)
            tile(2, 0)
            with act.Fori(1, (SLOTS - 2) // 2) as u:
                tile(2 * u + 1, 1)
                tile(2 * u + 2, 0)
            for j in range(SLOTS - 2 + (SLOTS % 2 == 0), SLOTS):
                tile(j, j % 2, j + 1 < SLOTS)
            h_high(SLOTS - 1)

        @block.tensor
        def _(pe):
            mm = nc.tensor.matmul
            pe.wait_ge(S["wq3"], 4)
            pe.wait_ge(S["cst"], 16)
            pe.wait_ge(S["init"], 2)
            pe.wait_ge(S["wq"], 32)

            def project(b, par):
                pe.wait_ge(S["xm"], 3 * b + 3)
                unless_first(pe, S["qk"], 4 * b)
                for pr in range(PAIRS):
                    ins = mm(PA[:, pr * T:(pr + 1) * T], wq3[:, pr].rearrange("p a b c -> p (a b c)"), xm[:, par, :],
                             start=True, stop=True)
                    if pr % 2:
                        ins.then_inc(S["pq"], 1)

            def project_v(b, par):
                unless_first(pe, S["rd"], b)
                unless_first(pe, S["cn"], b)
                for kt in range(KT):
                    ins = mm(PD[:, kt * P:(kt + 1) * P], xs[:, par, kt * P:(kt + 1) * P], wq1[:], start=True, stop=True)
                ins.then_inc(S["v"], 1)

            def scores(b, par, c):
                pe.wait_ge(S["qk"], 4 * b + (2 if c < 2 else 4))
                unless_first(pe, S["max"], 4 * b + c)
                for s in range(2):
                    r = slice(64 * s, 64 * s + 64)
                    for qt in range(KT):
                        ins = mm(PB[:, s * 512 + qt * T:s * 512 + (qt + 1) * T],
                                 qs[r, par, c * T + qt * P:c * T + (qt + 1) * P], ks[r, par, c * T:(c + 1) * T],
                                 start=True, stop=True)
                ins.then_inc(S["sa"], 1)

            def scores_T(b, par, c):
                pp, kt = c // KT, c % KT
                pe.wait_ge(S["q2"], b + 1)
                unless_first(pe, S["ex"], 4 * b + c)
                for s in range(2):
                    r = slice(64 * s, 64 * s + 64)
                    for n in range(2):
                        pr = 2 * pp + n
                        ins = mm(PC[:, s * 512 + n * T:s * 512 + (n + 1) * T],
                                 ks[r, par, pr * T + kt * P:pr * T + (kt + 1) * P], qs[r, par, pr * T:(pr + 1) * T],
                                 start=True, stop=True)
                ins.then_inc(S["st"], 1)

            def contexts(b, par):
                pe.wait_ge(S["vu"], b + 1)
                pe.wait_ge(S["om"], 2 * b + 2)
                W = H0 * (DK0 + 1)
                for qt in range(KT):
                    for kt in range(KT):
                        mm(PD[:, qt * W:(qt + 1) * W], om[:, par, kt, qt * P:(qt + 1) * P],
                           vu[:, par, kt].rearrange("p h d -> p (h d)"), start=(kt == 0), stop=False, skip_group_check=True)
                    pe.wait_ge(S["ex"], 4 * b + 4)
                    for h in range(H0):
                        pr, s = h // 2, h % 2
                        for kt in range(KT):
                            o = s * 512 + (pr % 2) * T + qt * P
                            ins = mm(PD[:, qt * W + h * (DK0 + 1):qt * W + (h + 1) * (DK0 + 1)],
                                     probs[:, (pr // 2) * KT + kt, o:o + P], vu[:, par, kt, h, :],
                                     start=False, stop=(kt == KT - 1), skip_group_check=True)
                ins.then_inc(S["ctx"], 1)

            def max_rows(b):
                pe.wait_ge(S["mc"], 2 * b + 2)
                pe.wait_ge(S["cl"], b - 1)
                first_max_rows(b)

            def first_max_rows(b):
                M = PD[:, 512:1024].bitcast(BF16)
                for pr in range(PAIRS):
                    for qt in range(KT):
                        ins = pe.transpose(M[:, pr * T + qt * P:pr * T + (qt + 1) * P], mcol[:, qt, pr, :], identb[:])
                ins.then_inc(S["mt"], 1)

            def context_T(b, more=True):
                pe.wait_ge(S["cn"], b + 1)
                pe.wait_ge(S["q2"], b + (2 if more else 1))
                for qt in range(KT):
                    ins = pe.transpose(PD[:, 512 + qt * P:512 + (qt + 1) * P], cn[:, qt].rearrange("p h d -> p (h d)"), ident)
                ins.then_inc(S["ct"], 1)
                pe.wait_ge(S["ce"], b + 1)
                for qt in range(KT):
                    ins = mm(PD[:, 512 + qt * P:512 + (qt + 1) * P], cT[:, qt * P:(qt + 1) * P], wo1[:], start=True, stop=True)
                ins.then_inc(S["wo"], 1)

            project(0, 0)
            for c in range(4):
                scores(0, 0, c)
            pe.wait_ge(S["mc"], 2)
            first_max_rows(0)

            def body(i, par, back):
                project(i, par)
                project_v(i - 1, 1 - par)
                for c in range(4):
                    scores_T(i - 1, 1 - par, c)
                    scores(i, par, c)
                contexts(i - 1, 1 - par)
                if back:
                    max_rows(i)
                else:
                    pe.wait_ge(S["mc"], 2 * i + 2)
                    first_max_rows(i)
                context_T(i - 1)

            body(1, 1, False)
            body(2, 0, True)
            with pe.Fori(1, U - 1) as u:
                body(2 * u + 1, 1, True)
                body(2 * u + 2, 0, True)
            body(LAST, 1, True)
            project_v(LAST, 1)
            for c in range(4):
                scores_T(LAST, 1, c)
            contexts(LAST, 1)
            context_T(LAST, False)

            pe.wait_ge(S["w0h"], LCH)
            pe.wait_ge(S["w0l"], LCH)
            pe.wait_ge(S["ch"], B)
            pe.wait_ge(S["cl"], B)
            def chunk(c):
                tok = bass.ds(c * CH, CH)

                def up(m):
                    for which, bank, done in ((0, PA, "g"), (1, PB, "u")):
                        unless_first(pe, S["hf"], MT * c + max(m - 1, 0))
                        o = bank[:, (m % 2) * 512:(m % 2 + 1) * 512]
                        k = 0
                        for kt in range(KT):
                            for w, v in ((w0_hi, c_hi), (w0_hi, c_lo), (w0_lo, c_hi)):
                                ins = mm(o, w0(w, which, kt, m), v[:, kt, tok], start=(k == 0), stop=(k == 3 * KT - 1))
                                k += 1
                        ins.then_inc(S[done], 1)

                def down(m):
                    n = P if m < MT - 1 else MLAST
                    pe.wait_ge(S["hl"], MT * c + m + 1)
                    if m == 0:
                        unless_first(pe, S["x1"], TPC * c)
                    for t in range(TPC):
                        o = (PC, PD)[t // 2][:, (t % 2) * 512:(t % 2) * 512 + T]
                        for k, (v, w) in enumerate(((h_hi, w0_hi), (h_hi, w0_lo), (h_lo, w0_hi))):
                            ins = mm(o, v[0:n, m, t * P:(t + 1) * P], w0d(w, m), start=(m == 0 and k == 0),
                                     stop=(m == MT - 1 and k == 2))
                    ins.then_inc(S["dn"], 1)

                up(0)
                for m in range(1, MT):
                    up(m)
                    down(m - 1)
                down(MT - 1)

            chunk(0)
            with pe.Fori(1, TOK // CH) as c:
                chunk(c)

            pe.wait_ge(S["x1"], B)
            pe.wait_ge(S["small3"], 16 * 9)
            pe.wait_ge(S["ck"], 16)
            for m in range(4):
                for kt in range(KT):
                    ins = mm(PA[:, m * B:(m + 1) * B], wemb[:, kt, m * P:(m + 1) * P], ck[:, kt, :],
                             start=(kt == 0), stop=(kt == KT - 1))
            ins.then_inc(S["emb"], 1)
            pe.wait_ge(S["w2a"], 2 * KT)
            for m in range(KT):
                for kt in range(KT):
                    ins = mm(PB[:, m * E:(m + 1) * E], w2T[:, kt, m * P:(m + 1) * P], wr[:, kt, :],
                             start=(kt == 0), stop=(kt == KT - 1))
            ins.then_inc(S["w2r"], 1)
            pe.wait_ge(S["gcol"], 4)
            pe.wait_ge(S["w2"], 1)
            pe.wait_ge(S["wqkv"], 16)

            def norm_qkv(b):
                pe.wait_ge(S["xr"], b + 1)
                unless_first(pe, S["v1"], b)
                for kt in range(KT):
                    ins = pe.transpose(PB[:, 512 + kt * P:512 + (kt + 1) * P], xr[:, kt * P:(kt + 1) * P], ident)
                ins.then_inc(S["xt3"], 1)

            def qkv(b):
                pe.wait_ge(S["xnT"], 2 * b + 2)
                unless_first(pe, S["qkn"], b)
                for kt in range(KT):
                    ins = mm(PB[:, 0:512], xnT[:, kt, :], wqkv[:, kt, 0:512], start=(kt == 0), stop=(kt == KT - 1))
                ins.then_inc(S["qkv"], 1)
                for kt in range(KT):
                    ins = mm(PB[:, 512:512 + T], xnT[:, kt, :], wqkv[:, kt, 512:768], start=(kt == 0), stop=(kt == KT - 1))
                ins.then_inc(S["qkv"], 1)

            def turn(b):
                pe.wait_ge(S["l4"], 2 * b + 2)
                for n, (src, done) in enumerate(((q4, "qTe"), (k4, "kTe"))):
                    unless_first(pe, S[done], b)
                    bank = PC[:, n * 512:(n + 1) * 512].bitcast(BF16)
                    for pr in range(H1 // 2):
                        ins = pe.transpose(bank[:, pr * P:(pr + 1) * P],
                                           src[:, 2 * pr:2 * pr + 2].rearrange("p h s d -> p (h s d)"), identb[:])
                    ins.then_inc(S["qT"], 1)

            def scores1(b, c):
                pe.wait_ge(S["qTe"], b + 1)
                pe.wait_ge(S["kTe"], b + 1)
                unless_first(pe, S["e3"], 2 * b + c)
                for s in range(2):
                    r = slice(64 * s, 64 * s + 64)
                    for n in range(4):
                        pr = 4 * c + n
                        ins = mm(PA[:, s * 512 + n * P:s * 512 + (n + 1) * P], kT[r, pr * P:(pr + 1) * P],
                                 qT[r, pr * P:(pr + 1) * P], start=True, stop=True)
                ins.then_inc(S["s3"], 1)

            def contexts1(b, par):
                pe.wait_ge(S["v1"], b + 1)
                unless_first(pe, S["on"], b)
                for h in range(H1):
                    if h % 8 == 0:
                        pe.wait_ge(S["e3"], 2 * b + h // 8 + 1)
                    pr, s = h // 2, h % 2
                    o = s * 512 + (pr % 4) * P
                    ins = mm(PD[:, h * (DK1 + 1):(h + 1) * (DK1 + 1)], probs[:, pr // 4, o:o + P], v1[:, par, h, :],
                             start=True, stop=True)
                ins.then_inc(S["c3"], 1)

            def outputs(b):
                pe.wait_ge(S["on"], b + 1)
                unless_first(pe, S["lg"], b)
                unless_first(pe, S["te3"], b)
                for kt in range(KT):
                    ins = pe.transpose(PD[:, 512 + kt * P:512 + (kt + 1) * P],
                                       on.rearrange("p h d -> p (h d)")[:, kt * P:(kt + 1) * P], ident)
                ins.then_inc(S["oT"], 1)
                pe.wait_ge(S["oTe"], b + 1)
                for kt in range(KT):
                    ins = mm(PD[:, 512:512 + T + E], oT[:, kt * P:(kt + 1) * P], w2[:, kt, :], start=(kt == 0), stop=(kt == KT - 1))
                ins.then_inc(S["t3"], 1)

            def body1(i, par):
                norm_qkv(i)
                turn(i - 1)
                qkv(i)
                scores1(i - 1, 0)
                scores1(i - 1, 1)
                contexts1(i - 1, 1 - par)
                outputs(i - 1)

            norm_qkv(0)
            qkv(0)
            body1(1, 1)
            with pe.Fori(1, U) as u:
                body1(2 * u, 0)
                body1(2 * u + 1, 1)
            turn(LAST)
            scores1(LAST, 0)
            scores1(LAST, 1)
            contexts1(LAST, 1)
            outputs(LAST)

            pe.wait_ge(S["r"], 1)
            flat = oh[:].rearrange("p b e -> p (b e)")
            mm(PA[:, 0:B * E], cst[:, C_TRI:C_TRI + P], flat, start=True, stop=True)
            mm(PB[:, 0:B * E], ones[:], flat, start=True, stop=True).then_inc(S["rp"], 1)

            for n in range(3):
                pe.wait_ge(S[f"wsl{n}"], U)
            pe.wait_ge(S["te"], 1)

            def tile_in(j, half, par):
                pe.wait_ge(S[f"xld{par}"], 16 * (half + 1))
                unless_first(pe, S["tl"], j)
                for kt in range(KT):
                    ins = pe.transpose(PD[:, kt * P:(kt + 1) * P], xin[:, par, kt * P:(kt + 1) * P], ident)
                ins.then_inc(S["tT"], 1)

            def gate_up(j, par, e, bank, w_hi, w_lo, free, done):
                pe.wait_ge(S["tl"], j + 1)
                unless_first(pe, S[free], j)
                for n in range(2):
                    k = 0
                    for kt in range(KT):
                        o = bass.ds(e * (KT * FF) + (kt * FF + n * 512), 512)
                        xo = slice(kt * P, (kt + 1) * P)
                        for v, w in ((xT_hi, w_hi), (xT_hi, w_lo), (xT_lo, w_hi)):
                            ins = mm(bank[:, n * 512:(n + 1) * 512], v[:, par, xo], w[:, o], start=(k == 0), stop=(k == 3 * KT - 1))
                            k += 1
                ins.then_inc(S[done], 1)

            def turn_h(j):
                pe.wait_ge(S["hm"], j + 1)
                unless_first(pe, S["hTl"], j)
                for f in range(FT):
                    ins = pe.transpose(PC[:, f * P:(f + 1) * P], hh[:, f * P:(f + 1) * P], ident)
                ins.then_inc(S["hT"], 1)

            def down(j, e):
                pe.wait_ge(S["hTh"], j + 1)
                pe.wait_ge(S["hTl"], j + 1)
                unless_first(pe, S["yo"], j)
                k = 0
                for f in range(FT):
                    o = bass.ds(e * (FT * T) + f * T, T)
                    for v, w in ((hT_hi, wd_hi), (hT_hi, wd_lo), (hT_lo, wd_hi)):
                        ins = mm(PD[:, 512:512 + T], v[:, f * P:(f + 1) * P], w[:, o], start=(k == 0), stop=(k == 3 * FT - 1))
                        k += 1
                ins.then_inc(S["y"], 1)

            def expert_of(j):
                return pe.value_load(te[0:1, bass.ds(j, 1)], min_val=0, max_val=E - 1)

            def tile(j, half, par, more=True):
                gate_up(j, par, expert_of(j), PA, wg_hi, wg_lo, "gs", "gu")
                turn_h(j - 1)
                gate_up(j, par, expert_of(j), PB, wu_hi, wu_lo, "hm", "uu")
                if more:
                    tile_in(j + 1, half + par, 1 - par)
                down(j - 1, expert_of(j - 1))

            tile_in(0, 0, 0)
            gate_up(0, 0, expert_of(0), PA, wg_hi, wg_lo, "gs", "gu")
            gate_up(0, 0, expert_of(0), PB, wu_hi, wu_lo, "hm", "uu")
            tile_in(1, 0, 1)
            tile(1, 0, 1)
            tile(2, 1, 0)
            with pe.Fori(1, (SLOTS - 2) // 2) as u:
                tile(2 * u + 1, u, 1)
                tile(2 * u + 2, u + 1, 0)
            for j in range(SLOTS - 2 + (SLOTS % 2 == 0), SLOTS):
                tile(j, j // 2, j % 2, j + 1 < SLOTS)
            turn_h(SLOTS - 1)
            down(SLOTS - 1, expert_of(SLOTS - 1))

        @block.vector
        def _(dve):
            v = nc.vector
            v.memset(wq3[:], 0.0).then_inc(S["wq3"], 1)
            v.memset(mcol, 0.0).then_inc(S["init"], 1)
            dve.wait_ge(S["cst"], 16)
            v.tensor_copy(identb[:], ident).then_inc(S["init"], 1)
            dve.wait_ge(S["wq"], 32)
            dve.wait_ge(S["wq3"], 1)
            for s in range(3):
                v.tensor_copy(wq3[:, :, :, s, :], wq1[:].rearrange("p (r a d) -> p r a d", r=PAIRS, a=2)).then_inc(S["wq3"], 1)
            dve.wait_ge(S["ck"], 16)
            v.tensor_scalar(nck[:], ck[:], -1.0, 1.0, ALU.mult, ALU.add).then_inc(S["kprep"], 1)
            v.tensor_scalar(nnck[:], ck[:], 1.0, None, ALU.subtract).then_inc(S["kprep"], 1)
            v.tensor_scalar(kbias[:], ck[:], 1.0, NEG, ALU.subtract, ALU.mult).then_inc(S["kprep"], 1)

            dve.wait_ge(S["lut"], 16)
            pairs = lutb[:].rearrange("p (j t) -> p j t", t=2)
            v.tensor_tensor(lutd[:], pairs[:, :, 1], pairs[:, :, 0], ALU.subtract).then_inc(S["lutd"], 1)
            dve.wait_ge(S["lutd"], 1)
            npick = [0]
            loads = 0
            for c in range(LCH):
                lo, hi = c * LW, (c + 1) * LW
                loads += (lo < 2 * GCOLS) + (hi > 2 * GCOLS)
                dve.wait_ge(S["idx"], 16 * loads)
                if c:
                    dve.wait_ge(S["w0l"], c)
                for n in range(4):
                    v.tensor_scalar(bit[n], idx, 1 << n, None, ALU.bitwise_and).then_inc(S["bit"], 1)
                dve.wait_ge(S["bit"], 4 * c + 4)

                def entry(dst, j):
                    v.tensor_scalar(pick[dst], bit[0], lutd[:, j:j + 1], lutb[:, 2 * j:2 * j + 1], ALU.mult, ALU.add
                                    ).then_inc(S["pick"], 1)
                    npick[0] += 1
                    dve.wait_ge(S["pick"], npick[0])

                def choose(dst, other, n):
                    v.copy_predicated(pick[dst], bit[n], pick[other]).then_inc(S["pick"], 1)
                    npick[0] += 1
                    dve.wait_ge(S["pick"], npick[0])

                def tree(dst, j, level):
                    if level == 0:
                        entry(dst, j)
                        return
                    tree(dst, j, level - 1)
                    tree(dst + 1, j + (1 << (level - 1)), level - 1)
                    choose(dst, dst + 1, level)

                tree(0, 0, 3)
                v.tensor_copy(w0_hi[:, lo:hi], pick[0]).then_inc(S["w0h"], 1)
                dve.wait_ge(S["w0h"], c + 1)
                v.tensor_tensor(w0_lo[:, lo:hi], pick[0], w0_hi[:, lo:hi], ALU.subtract).then_inc(S["w0l"], 1)

            def fixed():
                dve.wait_ge(S["mk"], 16)

            dve.wait_ge(S["kprep"], 3)

            def stack(b, par, back):
                if back:
                    dve.wait_ge(S["st"], 4 * (b - 1))
                for n in range(2):
                    dve.wait_ge(S["a"], 2 * b + n + 1)
                    o = slice(n * 512, (n + 1) * 512)
                    for dst, c in ((qs, C_SQ), (ks, C_SK)):
                        v.scalar_tensor_tensor(out=dst[:, par, o], in0=A[:, o], scalar=cst[:, c:c + 1], in1=PA[:, o],
                                               op0=ALU.mult, op1=ALU.add).then_inc(S["qk"], 1)

            def unmasked(b, par, back):
                if back:
                    dve.wait_ge(S["ctx"], b - 1)
                fixed()
                for kt in range(KT):
                    v.tensor_scalar(om[:, par, kt, :].unsqueeze(1), mk[:, bass.ds(b, 1), :],
                                    nnck[:, kt, bass.ds(b, 1)], nck[:, kt, bass.ds(b, 1)],
                                    ALU.mult, ALU.add).then_inc(S["om"], 1)

            def maxima(b):
                for c in range(4):
                    dve.wait_ge(S["sa"], 4 * b + c + 1)
                    if c == 0:
                        unless_first(dve, S["mc"], 2 * b)
                    v.tensor_reduce(nmax[:, c].rearrange("p s q -> p (s q)"), PB[:].rearrange("p (a k) -> p a k", k=T),
                                    AX.X, ALU.max, negate=True).then_inc(S["max"], 1)
                dve.wait_ge(S["max"], 4 * b + 4)
                unless_first(dve, S["mt"], b)
                cols = mcol.rearrange("p q r (s m) -> p r s q m", s=2)
                v.tensor_copy(cols[:, :, :, :, 48], nmax[:]).then_inc(S["mc"], 1)
                dve.wait_ge(S["mc"], 2 * b + 1)
                v.tensor_tensor(cols[:, :, :, :, 49], nmax[:], cols[:, :, :, :, 48], ALU.subtract).then_inc(S["mc"], 1)

            def add_max(b, par):
                dve.wait_ge(S["mt"], b + 1)
                v.tensor_tensor(qs[:, par, :], PD[:, 512:1024].bitcast(BF16), qs[:, par, :], ALU.add).then_inc(S["q2"], 1)

            def normalise(b):
                cx = PD[:, 0:KT * H0 * (DK0 + 1)].rearrange("p (q h d) -> p q h d", q=KT, h=H0)
                dve.wait_ge(S["ctx"], b + 1)
                unless_first(dve, S["ct"], b)
                v.reciprocal(rden[:], cx[:, :, :, DK0]).then_inc(S["rd"], 1)
                dve.wait_ge(S["rd"], b + 1)
                v.tensor_tensor(cn[:].rearrange("p q h d -> p (q h) d"),
                                cx[:, :, :, 0:DK0].rearrange("p q h d -> p (q h) d"),
                                rden[:].rearrange("p q h -> p (q h)").unsqueeze(2).broadcast_to([P, KT * H0, DK0]),
                                ALU.mult).then_inc(S["cn"], 1)

            def low_c(b):
                dve.wait_ge(S["ch"], b + 1)
                o = bass.ds(b * P, P)
                v.tensor_tensor(c_lo[:, :, o], PD[:, 512:512 + T].rearrange("p (k t) -> p k t", k=KT), c_hi[:, :, o],
                                ALU.subtract).then_inc(S["cl"], 1)

            def body(i, par, back):
                stack(i, par, back)
                unmasked(i, par, back)
                maxima(i)
                normalise(i - 1)
                add_max(i, par)
                low_c(i - 1)

            stack(0, 0, False)
            unmasked(0, 0, False)
            maxima(0)
            add_max(0, 0)
            body(1, 1, False)
            body(2, 0, True)
            with dve.Fori(1, U - 1) as u:
                body(2 * u + 1, 1, True)
                body(2 * u + 2, 0, True)
            body(LAST, 1, True)
            normalise(LAST)
            low_c(LAST)

            def hidden_chunk(c):
                for m in range(MT):
                    n = P if m < MT - 1 else MLAST
                    k = MT * c + m
                    dve.wait_ge(S["sil"], k + 1)
                    dve.wait_ge(S["u"], k + 1)
                    unless_first(dve, S["hl"], k if m == 0 else k - 1)
                    v.tensor_tensor(hf[0:n, m % 2, :], PB[0:n, (m % 2) * 512:(m % 2 + 1) * 512], sil[0:n, m % 2, :],
                                    ALU.mult).then_inc(S["hf"], 1)
                    dve.wait_ge(S["hh"], k + 1)
                    v.tensor_tensor(h_lo[0:n, m, :], hf[0:n, m % 2, :], h_hi[0:n, m, :], ALU.subtract).then_inc(S["hl"], 1)
                dve.wait_ge(S["dn"], MT * c + MT)
                for t in range(TPC):
                    b = TPC * c + t
                    v.tensor_tensor(rows[:, bass.ds(b, 1), T:2 * T],
                                    (PC, PD)[t // 2][:, (t % 2) * 512:(t % 2) * 512 + T].unsqueeze(1),
                                    xall[:, bass.ds(b, 1), :], ALU.add).then_inc(S["x1"], 1)

            hidden_chunk(0)
            with dve.Fori(1, TOK // CH) as c:
                hidden_chunk(c)

            dve.wait_ge(S["small3"], 16 * 9)
            for kt in range(KT):
                v.tensor_tensor(w2[:, kt, kt * P:(kt + 1) * P], w2[:, kt, kt * P:(kt + 1) * P], ident, ALU.add
                                ).then_inc(S["w2a"], 1)
                v.tensor_tensor(w2T[:, kt, kt * P:(kt + 1) * P], w2T[:, kt, kt * P:(kt + 1) * P], ident, ALU.add
                                ).then_inc(S["w2a"], 1)
            v.tensor_tensor(gg[:], gqk[:, 0], gqk[:, 1], ALU.mult).then_inc(S["gg"], 1)
            dve.wait_ge(S["gg"], 1)
            v.tensor_reduce(gb[:], gg[:], AX.X, ALU.max, apply_absolute_value=True).then_inc(S["gmx"], 1)
            dve.wait_ge(S["gmx"], 1)
            v.tensor_scalar(gb[:], gb[:], -(DK1 ** 0.5), None, ALU.mult).then_inc(S["gb"], 1)
            dve.wait_ge(S["emb"], 1)
            for kt in range(KT):
                v.tensor_scalar(gcol[:, kt, :], PA[:, kt * B:(kt + 1) * B], bemb[:, kt:kt + 1], 1.0, ALU.add, ALU.add
                                ).then_inc(S["gcol"], 1)
                v.tensor_scalar(scol[:, kt, :], PA[:, (KT + kt) * B:(KT + kt + 1) * B], bemb[:, KT + kt:KT + kt + 1], None,
                                ALU.add).then_inc(S["gcol"], 1)
            dve.wait_ge(S["gcol"], 4)
            for kt in range(KT):
                v.tensor_scalar(gcol[:, kt, :], gcol[:, kt, :], gnorm[:, kt:kt + 1], None, ALU.mult).then_inc(S["gcol"], 1)
            dve.wait_ge(S["w2r"], 1)
            v.tensor_copy(w2[:, :, T:T + E], PB[:, 0:KT * E].rearrange("p (k e) -> p k e", k=KT)).then_inc(S["w2"], 1)
            dve.wait_ge(S["gcol"], 6)

            def scaled(b, par):
                dve.wait_ge(S["rstd"], b + 1)
                unless_first(dve, S["xt3"], b)
                v.tensor_scalar(xr.unsqueeze(1), rows[:, bass.ds(b, 1), T:2 * T], rstd[:, par:par + 1], None, ALU.mult
                                ).then_inc(S["xr"], 1)

            def modulated(b):
                dve.wait_ge(S["xt3"], b + 1)
                unless_first(dve, S["qkv"], 2 * b)
                for kt in range(KT):
                    v.tensor_scalar(xnT[:, kt, :], PB[:, 512 + kt * P:512 + (kt + 1) * P], gcol[:, kt, bass.ds(b, 1)],
                                    scol[:, kt, bass.ds(b, 1)], ALU.mult, ALU.add).then_inc(S["xnT"], 1)

            def kT_out(b):
                dve.wait_ge(S["qT"], 2 * b + 2)
                unless_first(dve, S["s3"], 2 * b)
                v.tensor_copy(kT, PC[:, 512:1024].bitcast(BF16)).then_inc(S["kTe"], 1)

            def qk_norm(b):
                dve.wait_ge(S["sq"], b + 1)
                unless_first(dve, S["rs"], b)
                v.tensor_reduce(msr[:], sq.rearrange("p (h d) -> p h d", d=DK1), AX.X, ALU.add).then_inc(S["mean"], 1)
                dve.wait_ge(S["mean"], b + 1)
                v.tensor_scalar(ms[:], msr[:], EPS, None, ALU.add).then_inc(S["ms"], 1)
                dve.wait_ge(S["rs"], b + 1)
                unless_first(dve, S["h4"], 2 * b)
                unless_first(dve, S["l4"], 2 * b)
                v.tensor_tensor(qk.rearrange("p a h d -> p (a h) d"), PB[:, 0:512].rearrange("p (h d) -> p h d", d=DK1),
                                rs[:].unsqueeze(2).broadcast_to([P, 2 * H1, DK1]), ALU.mult).then_inc(S["qkn"], 1)

            def low_parts(b):
                dve.wait_ge(S["h4"], 2 * b + 1)
                unless_first(dve, S["qT"], 2 * b)
                v.tensor_tensor(q4[:, :, 2:4, :], qk[:, 0].unsqueeze(2).broadcast_to([P, H1, 2, DK1]), q4[:, :, 0:2, :],
                                ALU.subtract).then_inc(S["l4"], 1)
                dve.wait_ge(S["h4"], 2 * b + 2)
                v.tensor_tensor(k4[:, :, 1::2, :], qk[:, 1].unsqueeze(2).broadcast_to([P, H1, 2, DK1]), k4[:, :, 0::2, :],
                                ALU.subtract).then_inc(S["l4"], 1)

            def normalise1(b):
                cx = PD[:, 0:H1 * (DK1 + 1)].rearrange("p (h d) -> p h d", h=H1)
                dve.wait_ge(S["c3"], b + 1)
                unless_first(dve, S["oT"], b)
                v.reciprocal(rden1[:], cx[:, :, DK1]).then_inc(S["rd3"], 1)
                dve.wait_ge(S["rd3"], b + 1)
                v.tensor_tensor(on, cx[:, :, 0:DK1], rden1[:].unsqueeze(2).broadcast_to([P, H1, DK1]), ALU.mult
                                ).then_inc(S["on"], 1)

            def logits(b):
                dve.wait_ge(S["te3"], b + 1)
                v.tensor_tensor(lg[:, bass.ds(b, 1), :], PD[:, 512 + T:512 + T + E].unsqueeze(1), br[:].unsqueeze(1), ALU.add
                                ).then_inc(S["lg"], 1)

            def body1(i, par):
                scaled(i, par)
                modulated(i)
                kT_out(i - 1)
                qk_norm(i)
                normalise1(i - 1)
                low_parts(i)
                logits(i - 1)

            scaled(0, 0)
            modulated(0)
            qk_norm(0)
            low_parts(0)
            body1(1, 1)
            with dve.Fori(1, U) as u:
                body1(2 * u, 0)
                body1(2 * u + 1, 1)
            kT_out(LAST)
            normalise1(LAST)
            logits(LAST)

            n_r = [0]

            def done(ins):
                ins.then_inc(S["rv"], 1)
                n_r[0] += 1
                dve.wait_ge(S["rv"], n_r[0])

            dve.wait_ge(S["lg"], B)
            wide = lmx[:].unsqueeze(2).broadcast_to([P, B, E])
            done(v.tensor_reduce(lmx[:], lg[:], AX.X, ALU.max))
            v.tensor_tensor(ex[:], lg[:], wide, ALU.subtract).then_inc(S["rx"], 1)
            done(v.tensor_tensor(oh[:], lg[:], wide, ALU.is_equal))
            done(v.tensor_copy(taken[:], oh[:, :, 0]))
            for e in range(1, E):
                last = v.tensor_tensor(oh[:, :, e], oh[:, :, e], taken[:], ALU.is_gt)
                if e < E - 1:
                    done(last)
                    done(v.tensor_tensor(taken[:], oh[:, :, e], taken[:], ALU.max))
            last.then_inc(S["r"], 1)
            dve.wait_ge(S["rx"], 2)
            done(v.tensor_reduce(es[:], ex[:], AX.X, ALU.add))
            v.reciprocal(rows[:, :, 2 * T], es[:]).then_inc(S["rows"], 1)
            dve.wait_ge(S["rp"], 1)
            done(v.tensor_copy(tot[:], PB[:, 0:B * E].rearrange("p (b e) -> p e b", e=E)))
            for e in range(E):
                done(v.tensor_tensor_scan(run[:, e, :], ones[:, 0:B], tot[:, e, :], 0.0, ALU.mult, ALU.add))
            done(v.tensor_scalar(cnt[:], run[:, :, B - 1], float(P - 1), None, ALU.add))
            done(v.tensor_scalar(cnt[:], cnt[:], P.bit_length() - 1, None, ALU.arith_shift_right))
            done(v.tensor_copy(ntile[:], cnt[:]))
            done(v.memset(first[:], 0.0))
            for e in range(1, E):
                done(v.tensor_tensor(first[:, e:e + 1], first[:, e - 1:e], ntile[:, e - 1:e], ALU.add))
            tiles = cst[:, C_ROWS:C_ROWS + SLOTS]
            done(v.tensor_scalar(tef[:], tiles, first[:, 1:2], None, ALU.is_ge))
            for e in range(2, E):
                done(v.scalar_tensor_tensor(out=tef[:], in0=tiles, scalar=first[:, e:e + 1], in1=tef[:], op0=ALU.is_ge,
                                            op1=ALU.add))
            v.tensor_copy(te[:], tef[:]).then_inc(S["te"], 1)
            done(v.tensor_tensor(place[:], run[:].rearrange("p e b -> p b e"), tot[:].rearrange("p e b -> p b e"), ALU.subtract))
            done(v.tensor_tensor(place[:], PA[:, 0:B * E].rearrange("p (b e) -> p b e", e=E), place[:], ALU.add))
            done(v.scalar_tensor_tensor(out=place[:], in0=first[:].unsqueeze(1).broadcast_to([P, B, E]), scalar=float(P),
                                        in1=place[:], op0=ALU.mult, op1=ALU.add))
            done(v.tensor_tensor(place[:], place[:], oh[:], ALU.mult))
            done(v.tensor_reduce(slotf[:], place[:], AX.X, ALU.add))
            v.tensor_copy(slot[:], slotf[:]).then_inc(S["slot"], 1)

            def x_low(j, par):
                dve.wait_ge(S["th"], j + 1)
                v.tensor_tensor(xT_lo[:, par, :], PD[:, 0:T], xT_hi[:, par, :], ALU.subtract).then_inc(S["tl"], 1)

            def hidden(j):
                dve.wait_ge(S["gs"], j + 1)
                dve.wait_ge(S["uu"], j + 1)
                unless_first(dve, S["hT"], j)
                v.tensor_tensor(hh, PB[:], gs, ALU.mult).then_inc(S["hm"], 1)

            def h_low(j):
                dve.wait_ge(S["hTh"], j + 1)
                unless_first(dve, S["y"], j)
                v.tensor_tensor(hT_lo, PC[:], hT_hi, ALU.subtract).then_inc(S["hTl"], 1)

            def result(j, par, half, back):
                dve.wait_ge(S["y"], j + 1)
                dve.wait_ge(S[f"res{par}"], 16 * half + 16)
                if back:
                    dve.wait_ge(S[f"so{par}"], 16 * half)
                v.tensor_copy(tokn[:, par:par + 1], xres[:, par, T + 1:T + 2].bitcast(I32)).then_inc(S["idn"], 1)
                v.scalar_tensor_tensor(out=yo[:, par, :], in0=PD[:, 512:512 + T], scalar=xres[:, par, T:T + 1],
                                       in1=xres[:, par, 0:T], op0=ALU.mult, op1=ALU.add).then_inc(S["yo"], 1)

            x_low(0, 0)
            hidden(0)
            x_low(1, 1)

            def tile(j, par, half, back, more=True):
                h_low(j - 1)
                hidden(j)
                if more:
                    x_low(j + 1, 1 - par)
                result(j - 1, 1 - par, half, back)

            tile(1, 1, 0, False)
            tile(2, 0, 0, False)
            with dve.Fori(1, (SLOTS - 2) // 2) as u:
                tile(2 * u + 1, 1, u, True)
                tile(2 * u + 2, 0, u, True)
            for j in range(SLOTS - 2 + (SLOTS % 2 == 0), SLOTS):
                tile(j, j % 2, (j - 1) // 2, True, j + 1 < SLOTS)
            h_low(SLOTS - 1)
            result(SLOTS - 1, (SLOTS - 1) % 2, (SLOTS - 1) // 2, True)


def kernel(x, cond_2048, L0_cond_Wq, L0_cond_Wo, L0_ffn_lut, L0_ffn_gate_idx, L0_ffn_up_idx, L0_ffn_down_idx,
           L1_cond_W_emb, L1_cond_b_emb, L1_cond_g_norm, L1_cond_W_qkv, L1_cond_g_q, L1_cond_g_k, L1_cond_W_out,
           L1_ffn_Wr, L1_ffn_br, L1_ffn_Wg, L1_ffn_Wu, L1_ffn_Wd):
    import concourse.bacc as bacc
    from concourse.bass_utils import run_bass_kernel_spmd

    def by_rows(w):
        w = np.asarray(w)
        return w.reshape(-1, P, w.shape[-1]).transpose(1, 0, 2).reshape(P, -1)

    down = np.asarray(L0_ffn_down_idx).T
    down = np.concatenate([down, np.zeros((MT * P - INTER, T), down.dtype)])
    arrays = {
        "x": x, "cond": cond_2048, "condT": np.asarray(cond_2048).T.reshape(KT, P, B).transpose(1, 0, 2),
        "consts": constants(), "wqT": np.asarray(L0_cond_Wq).T, "woT": np.asarray(L0_cond_Wo).T,
        "lut": np.asarray(L0_ffn_lut).reshape(1, LUT),
        "idx_gu": np.concatenate([by_rows(np.asarray(L0_ffn_gate_idx).T), by_rows(np.asarray(L0_ffn_up_idx).T)], axis=1),
        "idx_d": by_rows(down),
        "w_emb": L1_cond_W_emb, "b_emb": np.asarray(L1_cond_b_emb).reshape(4, P).T,
        "g_norm": np.asarray(L1_cond_g_norm).reshape(KT, P).T, "w_qkv": L1_cond_W_qkv,
        "g_q": np.asarray(L1_cond_g_q).reshape(1, DK1), "g_k": np.asarray(L1_cond_g_k).reshape(1, DK1),
        "w_out": L1_cond_W_out, "w_outT": np.asarray(L1_cond_W_out).T, "w_r": L1_ffn_Wr,
        "b_r": np.asarray(L1_ffn_br).reshape(1, E),
        "w_g": by_rows(np.asarray(L1_ffn_Wg).reshape(E * T, FF)), "w_u": by_rows(np.asarray(L1_ffn_Wu).reshape(E * T, FF)),
        "w_d": by_rows(np.asarray(L1_ffn_Wd).reshape(E * FF, T)),
    }
    arrays = {f"in_{k}": np.ascontiguousarray(a) for k, a in arrays.items()}
    nc = bacc.Bacc("TRN2", target_bir_lowering=False, num_devices=1)
    args = [nc.dram_tensor(k, a.shape, mybir.dt.from_np(a.dtype), kind="ExternalInput").ap() for k, a in arrays.items()]
    out = nc.dram_tensor("out", (TOK, T), F32, kind="ExternalOutput").ap()
    routed = nc.dram_tensor("routed", (SLOTS * P, ROW), F32, kind="Internal").ap()
    program(nc, *args, out, routed)
    got = run_bass_kernel_spmd(nc, [arrays], core_ids=[0]).results[0]["out"]
    return got.reshape(B, D, T)
```

```python
from contextlib import ExitStack

import numpy as np

import concourse.bass as bass
from concourse import mybir

F32 = mybir.dt.float32
BF16 = mybir.dt.bfloat16
I32 = mybir.dt.int32
ALU = mybir.AluOpType
ACT = mybir.ActivationFunctionType
AX = mybir.AxisListType

P = 128
B, D, T = 16, 128, 256
KT = T // P
H0, DK0 = 8, 16
PAIRS = H0 // 2
SCALE0 = DK0 ** -0.5
INTER = 688
MT = -(-INTER // P)
MLAST = INTER - (MT - 1) * P
LUT = 16
H1, DK1 = 16, 16
EPS = 1e-6
E, FF = 4, 1024
FT = FF // P
TOK = B * D
CH = 512
TPC = CH // P
SLOTS = TOK // P + E - 1
ROW = 2 * T + 2
NEG = 1e30
DUMMY = 2 * TOK

GCOLS = KT * INTER
WCOLS = 2 * GCOLS + MT * T
LCH = B
LW = WCOLS // LCH

C_ID, C_TRI, C_SQ, C_SK, C_EV, C_ROWS = 0, P, 2 * P, 2 * P + 1, 2 * P + 2, 2 * P + 3
HS = 32
GROUP = P // HS
GROUPS = H0 // GROUP
C_N = C_ROWS + SLOTS


def constants():
    c = np.zeros((P, C_N), np.float32)
    p = np.arange(P)
    c[:, C_ID:C_ID + P] = np.eye(P)
    c[:, C_TRI:C_TRI + P] = p[:, None] < p[None, :]
    slot, r = p % 64 // 16, p % 64
    c[:, C_SQ] = np.where((slot == 2) | (r == 50), -1, 0)
    c[:, C_SK] = np.where(slot == 1, -1, np.where((r == 48) | (r == 49), 1, 0))
    c[:, C_EV] = (r == 48) | (r == 49)
    c[:, C_ROWS:] = np.arange(SLOTS)
    return c


def program(nc, x, cond, condT, consts, wqT, woT, lut, idx_all, w_emb, b_emb, g_norm, w_qkv, g_q, g_k,
            w_out, w_outT, w_r, b_r, w_g, w_u, w_d, out, routed):
    with ExitStack() as ctx:
        def sb(name, shape, dt=F32):
            return ctx.enter_context(nc.sbuf_tensor(name, shape, dt))

        def sem(name):
            return ctx.enter_context(nc.semaphore(name))

        PA, PB, PC, PD = (ctx.enter_context(nc.psum_tensor(n, [P, 1024], F32)) for n in ("PA", "PB", "PC", "PD"))

        cst = sb("cst", [P, C_N])
        ident = cst[:, C_ID:C_ID + P]
        identb = sb("identb", [P, P], BF16)
        ones = sb("ones", [P, P])
        half_neg = sb("half_neg", [P, 64])
        ck = sb("ck", [P, KT, B])
        rows = sb("rows", [P, B, ROW])

        HALF = E * KT * FF
        arena = sb("arena", [P, 3 * HALF])
        at = [0]

        def f32(*shape):
            n = int(np.prod(shape))
            v = arena[:, at[0]:at[0] + n]
            at[0] += n
            return v

        def bf(*shape):
            n = int(np.prod(shape)) // 2
            v = arena[:, at[0]:at[0] + n].bitcast(BF16)
            at[0] += n
            return v

        def hi_lo(k):
            v = arena[:, k * HALF:(k + 1) * HALF].bitcast(BF16)
            return v[:, 0:HALF], v[:, HALF:2 * HALF]

        (wg_hi, wg_lo), (wu_hi, wu_lo), (wd_hi, wd_lo) = hi_lo(0), hi_lo(1), hi_lo(2)

        xall = f32(B, T).rearrange("p (b t) -> p b t", b=B)
        mk = f32(B, T).rearrange("p (b t) -> p b t", b=B)
        c_hi = bf(KT, TOK).rearrange("p (k t) -> p k t", k=KT)
        c_lo = bf(KT, TOK).rearrange("p (k t) -> p k t", k=KT)
        w0_hi, w0_lo = bf(WCOLS), bf(WCOLS)
        at_lookup = at[0]
        idx = f32(LW).bitcast(I32)
        bit = f32(4, LW).bitcast(I32).rearrange("p (n c) -> p n c", n=4)
        pick = f32(LUT // 2, LW).rearrange("p (n c) -> p n c", n=LUT // 2)
        at[0] = at_lookup
        h_hi = bf(MT, CH).rearrange("p (m t) -> p m t", m=MT)
        h_lo = bf(MT, CH).rearrange("p (m t) -> p m t", m=MT)
        assert max(at[0], at_lookup + (5 + LUT // 2) * LW) <= 3 * HALF

        def w0(w, which, kt, m):
            o = which * GCOLS + kt * INTER + m * P
            return w[:, o:o + P]

        def w0d(w, m):
            n = P if m < MT - 1 else MLAST
            o = 2 * GCOLS + m * T
            return w[0:n, o:o + T]

        SMALL = 5248
        small = sb("small", [P, SMALL])
        small_at = [0]

        def part(shape, dt=F32):
            n = int(np.prod(shape[1:])) * (1 if dt == F32 else 2) // (1 if dt == F32 else 4)
            v = small[:, small_at[0]:small_at[0] + n]
            small_at[0] += n
            assert small_at[0] <= SMALL
            if dt != F32:
                v = v.bitcast(dt)
            names = "abcd"[:len(shape) - 1]
            if len(names) == 1:
                return v
            return v.rearrange(f"p ({' '.join(names)}) -> p {' '.join(names)}", **dict(zip(names, shape[1:])))

        wq1 = sb("wq1", [P, P])
        wq3 = sb("wq3", [P, PAIRS, 2, 4, 16])
        wo2 = sb("wo2", [P, GROUPS, P])
        lutb = sb("lutb", [P, LUT])
        lutd = sb("lutd", [P, LUT // 2])
        absent_row = sb("absent_row", [1, P], BF16)
        nbig = sb("nbig", [P, KT, B])
        xs = part([P, 2, T])
        xm = part([P, 2, T])
        absent = part([P, 2, T], BF16)
        A = part([P, PAIRS * T], BF16)
        qs = part([P, 2, PAIRS * T], BF16)
        ks = part([P, 2, PAIRS * T], BF16)
        nmax = sb("nmax", [P, PAIRS, 2, KT])
        mcol = part([P, KT, PAIRS, P], BF16)
        probs = sb("probs", [P, 4, 1024])
        vu = sb("vu", [P, 2, KT, H0, HS])
        cq = part([P, GROUPS * T])
        wst = sb("wst", [P, 3, FF])
        rden = sb("rden", [P, GROUPS * T // HS])
        cT = wst[:, 1, 0:GROUPS * T].rearrange("p (g t) -> p g t", g=GROUPS)

        sil = wst[:, 0, :].rearrange("p (n t) -> p n t", n=2)
        hf = wst[:, 1, :].rearrange("p (n t) -> p n t", n=2)

        small_at[0] = 0
        wemb = sb("wemb", [P, KT, 2 * T])
        bemb = sb("bemb", [P, 4])
        gnorm = sb("gnorm", [P, KT])
        gcol = sb("gcol", [P, KT, B])
        scol = sb("scol", [P, KT, B])
        wqkv = sb("wqkv", [P, KT, 3 * T])
        gqk = sb("gqk", [P, 2, DK1])
        gg = sb("gg", [P, DK1])
        gb = sb("gb", [P, 1])
        w2 = sb("w2", [P, KT, T + E])
        w2T = sb("w2T", [P, KT, T])
        wr = sb("wr", [P, KT, E])
        br = sb("br", [P, E])
        sqx = sb("sqx", [P, T])
        ssq = sb("ssq", [P, 2])
        rstd = sb("rstd", [P, 2])
        xr = part([P, T])
        xnT = part([P, KT, P])
        sq = part([P, 2 * T])
        msr = sb("msr", [P, 2 * H1])
        ms = sb("ms", [P, 2 * H1])
        rs = sb("rs", [P, 2 * H1])
        qk = part([P, 2, H1, DK1])
        q4 = part([P, H1, 4, DK1], BF16)
        k4 = part([P, H1, 4, DK1], BF16)
        qT = part([P, 1024], BF16)
        kT = part([P, 1024], BF16)
        v1 = sb("v1", [P, 2, H1, DK1 + 1])
        rden1 = sb("rden1", [P, H1])
        on = part([P, H1, DK1])
        oT = part([P, T])
        lg = sb("lg", [P, B, E])
        eps = sb("eps", [P, 1])
        wz = sb("wz", [P, 1])

        lmx = sb("lmx", [P, B])
        oh = sb("oh", [P, B, E])
        taken = sb("taken", [P, B])
        ex = sb("ex", [P, B, E])
        es = sb("es", [P, B])
        tot = sb("tot", [P, E, B])
        run = sb("run", [P, E, B])
        cnt = sb("cnt", [P, E], I32)
        ntile = sb("ntile", [P, E])
        first = sb("first", [P, E])
        place = sb("place", [P, B, E])
        slotf = sb("slotf", [P, B])
        slot = sb("slot", [P, B], I32)
        tef = sb("tef", [P, SLOTS])
        te = sb("te", [P, SLOTS], I32)
        pad = wst[:, 2, 0:ROW]
        small_at[0] = 0
        xin = part([P, 2, T])
        xres = part([P, 2, ROW - T])
        gs, hh = probs[:, 0, :], probs[:, 1, :]
        hT_hi, hT_lo = (probs[:, 2, n * 512:(n + 1) * 512].bitcast(BF16) for n in range(2))
        xT_hi, xT_lo = (probs[:, 3, n * T:(n + 1) * T].bitcast(BF16).rearrange("p (n t) -> p n t", n=2) for n in range(2))
        yo = probs[:, 3, 512:1024].rearrange("p (n t) -> p n t", n=2)
        tokn = sb("tokn", [P, 2], I32)

        S = {}

        def new(*names):
            for n in names:
                S[n] = sem("s_" + n)

        new("x", "mk", "x_rest", "mk_rest", "cst", "ck", "wq", "lut", "small3", "wqkv", "idx", "pad", "scat", "ones", "init", "wq3", "kprep",
            "lutd", "bit", "entry", "pick", "w0h", "w0l",
            "xm", "absent", "pq", "a", "qk", "sa", "max", "mc", "mt", "q2", "st", "ex", "v", "vu", "ctx", "cq", "rd", "cn", "ct",
            "wo", "ch", "cl",
            "g", "sil", "u", "hf", "hh", "hl", "dn", "x1",
            "w2a", "w2r", "w2", "emb", "gcol", "gg", "gb", "gmx",
            "ssq", "rstd", "xr", "xt3", "xnT", "qkv", "sq", "ms", "rs", "qkn", "qg", "h4", "l4", "qT", "qTe", "kTe",
            "s3", "e3", "v1", "c3", "rd3", "on", "oT", "oTe", "t3", "te3", "lg",
            "wst0", "wst1", "wst2", "wsh0", "wsh1", "wsh2", "wsl0", "wsl1", "wsl2",
            "mean", "rv", "var", "r", "rx", "rp", "tok", "te", "slot", "rows",
            "xld0", "xld1", "res0", "res1", "tT", "th", "tl", "gu", "gs", "uu", "hm", "hT", "hTh", "hTl", "y", "yo", "so0", "so1", "idn")

        def unless_first(engine, semaphore, count):
            if not (isinstance(count, int) and count == 0):
                engine.wait_ge(semaphore, count)

        block = ctx.enter_context(nc.Block())
        LAST = B - 1
        U = B // 2

        @block.sync
        def _(sp):
            first, rest = slice(0, 2), slice(2, B)
            masks = cond.rearrange("(o b) t -> o b t", o=1).broadcast_to([P, B, T])
            sp.dma_start(xall[:, first], x[first].rearrange("b d t -> d b t")).then_inc(S["x"], 16)
            sp.dma_start(mk[:, first], masks[:, first]).then_inc(S["mk"], 16)
            sp.dma_start(wq1[:], wqT).then_inc(S["wq"], 16)
            sp.dma_start(cst[:], consts).then_inc(S["cst"], 16)
            sp.dma_start(wo2[:], woT.rearrange("p (g o) -> p g o", g=GROUPS)).then_inc(S["wq"], 16)
            sp.dma_start(xall[:, rest], x[rest].rearrange("b d t -> d b t")).then_inc(S["x_rest"], 16)
            sp.dma_start(mk[:, rest], masks[:, rest]).then_inc(S["mk_rest"], 16)
            sp.dma_start(idx, idx_all[:, 0:LW]).then_inc(S["idx"], 16)
            with sp.Fori(1, LCH) as c:
                sp.wait_ge(S["bit"], 4 * c)
                sp.dma_start(idx, idx_all[:, bass.ds(c * LW, LW)]).then_inc(S["idx"], 16)
            sp.wait_ge(S["x1"], B)
            sp.wait_ge(S["pad"], 16 * SLOTS)

            def weight_pieces(u):
                for n, w in enumerate((w_g, w_u, w_d)):
                    unless_first(sp, S[f"wsl{n}"], u)
                    sp.dma_start(wst[:, n, :], w[:, bass.ds(u * FF, FF)]).then_inc(S[f"wst{n}"], 16)
            weight_pieces(0)
            with sp.Fori(1, U) as u:
                weight_pieces(u)
            sp.wait_ge(S["scat"], 16 * B)
            def load_input(j):
                if j >= 2:
                    sp.wait_ge(S["tT"], j - 1)
                sp.dma_start(xin[:, j % 2, :], routed[j * P:(j + 1) * P, 0:T]).then_inc(S[f"xld{j % 2}"], 16)

            load_input(0)
            for j in range(SLOTS):
                if j + 1 < SLOTS:
                    load_input(j + 1)
                if j >= 2:
                    sp.wait_ge(S["yo"], j - 1)
                    sp.wait_ge(S["idn"], j - 1)
                sp.dma_start(xres[:, j % 2, :], routed[j * P:(j + 1) * P, T:ROW]).then_inc(S[f"res{j % 2}"], 16)

        @block.gpsimd
        def _(pool):
            nc.gpsimd.memset(ones[:], 1.0).then_inc(S["ones"], 1)
            nc.gpsimd.memset(half_neg[:], -0.5).then_inc(S["ones"], 1)
            nc.gpsimd.memset(wz[:], 0.0).then_inc(S["ones"], 1)
            nc.gpsimd.memset(pad, 0.0).then_inc(S["ones"], 1)
            nc.gpsimd.iota(rows[:, :, ROW - 1:ROW].bitcast(I32), pattern=[[P, B], [0, 1]], base=0,
                           channel_multiplier=1).then_inc(S["tok"], 1)
            nc.gpsimd.memset(eps[:], EPS).then_inc(S["ones"], 1)
            pool.wait_ge(S["ones"], 4)
            nc.gpsimd.memset(pad[:, ROW - 1:ROW].bitcast(I32), DUMMY).then_inc(S["ones"], 1)

            def inputs(b, par):
                nc.gpsimd.tensor_tensor(xm[:, par, :].unsqueeze(1), xall[:, bass.ds(b, 1), :], mk[:, bass.ds(b, 1), :],
                                        ALU.mult).then_inc(S["xm"], 1)
                nc.gpsimd.tensor_tensor(absent[0:1, par, :].unsqueeze(1), ones[0:1, 0:1].unsqueeze(1).broadcast_to([1, 1, T]),
                                        mk[0:1, bass.ds(b, 1), :], ALU.subtract).then_inc(S["xm"], 1)
                nc.gpsimd.tensor_copy(xs[:, par, :].unsqueeze(1), xall[:, bass.ds(b, 1), :]).then_inc(S["xm"], 1)

            def turn_inputs(i, par):
                pool.wait_ge(S["pq"], 2 * i)
                pool.wait_ge(S["v"], i)
                inputs(i + 1, par)

            pool.wait_ge(S["x"], 16)
            pool.wait_ge(S["mk"], 16)
            inputs(0, 0)
            nc.gpsimd.memset(vu[:], 1.0).then_inc(S["ones"], 1)
            nc.gpsimd.memset(v1[:], 1.0).then_inc(S["ones"], 1)
            inputs(1, 1)
            pool.wait_ge(S["x_rest"], 16)
            pool.wait_ge(S["mk_rest"], 16)
            turn_inputs(1, 0)
            turn_inputs(2, 1)
            with pool.Fori(1, U - 1) as u:
                turn_inputs(2 * u + 1, 0)
                turn_inputs(2 * u + 2, 1)

            pool.wait_ge(S["ones"], 8)
            for j in range(SLOTS):
                pool.dma_start(routed[j * P:(j + 1) * P, :], pad).then_inc(S["pad"], 16)

            def split(n, dst_hi, dst_lo, u):
                pool.wait_ge(S[f"wst{n}"], 16 * (u + 1))
                o = bass.ds(u * FF, FF)
                nc.gpsimd.tensor_tensor(dst_hi[:, o], wst[:, n, :], wz[:].broadcast_to([P, FF]), ALU.add).then_inc(S[f"wsh{n}"], 1)
                pool.wait_ge(S[f"wsh{n}"], u + 1)
                nc.gpsimd.tensor_tensor(dst_lo[:, o], wst[:, n, :], dst_hi[:, o], ALU.subtract).then_inc(S[f"wsl{n}"], 1)

            def norms(b, par, u, back):
                pool.wait_ge(S["ssq"], b + 1)
                if back:
                    pool.wait_ge(S["xr"], b - 1)
                nc.gpsimd.tensor_tensor(rstd[:, par:par + 1], ssq[:, par:par + 1], eps[:], ALU.add).then_inc(S["var"], 1)
                pool.wait_ge(S["var"], b + 1)
                nc.gpsimd.tensor_tensor(rstd[:, par:par + 1], rstd[:, par:par + 1], half_neg[:, 0:1],
                                        ALU.pow).then_inc(S["rstd"], 1)
                pool.wait_ge(S["ms"], b + 1)
                unless_first(pool, S["qkn"], b)
                nc.gpsimd.tensor_tensor(rs[:], ms[:], half_neg[:, 0:2 * H1], ALU.pow).then_inc(S["rs"], 1)
                pool.wait_ge(S["qkn"], b + 1)
                nc.gpsimd.tensor_tensor(qk[:, 0], qk[:, 0], gg[:].unsqueeze(1).broadcast_to([P, H1, DK1]),
                                        ALU.mult).then_inc(S["qg"], 1)
                if par == 0:
                    split(0, wg_hi, wg_lo, u)
                    split(1, wu_hi, wu_lo, u)
                else:
                    split(2, wd_hi, wd_lo, u)

            pool.wait_ge(S["x1"], B)
            pool.wait_ge(S["gg"], 1)
            norms(0, 0, 0, False)
            norms(1, 1, 0, False)
            with pool.Fori(1, U) as u:
                norms(2 * u, 0, u, True)
                norms(2 * u + 1, 1, u, True)

            pool.wait_ge(S["pad"], 16 * SLOTS)
            pool.wait_ge(S["slot"], 1)
            pool.wait_ge(S["rows"], 1)
            pool.wait_ge(S["tok"], 1)
            for j in range(B):
                pool.indirect_dma_start(routed, bass.IndirectOffsetOnAxis(ap=slot[:, j:j + 1], axis=0),
                                        rows[:, j, :], None).then_inc(S["scat"], 16)
            for j in range(SLOTS):
                pool.wait_ge(S["yo"], j + 1)
                pool.wait_ge(S["idn"], j + 1)
                pool.indirect_dma_start(out, bass.IndirectOffsetOnAxis(ap=tokn[:, j % 2:j % 2 + 1], axis=0),
                                        yo[:, j % 2, :], None, bounds_check=TOK - 1,
                                        oob_is_err=False).then_inc(S[f"so{j % 2}"], 16)
            for j in range(2):
                pool.wait_ge(S[f"so{j}"], 16 * ((SLOTS - j + 1) // 2))

        @block.scalar
        def _(act):
            act.dma_start(ck[:], condT).then_inc(S["ck"], 16)
            act.dma_start(lutb[:], lut.broadcast_to([P, LUT])).then_inc(S["lut"], 16)
            for dst, src in ((wemb[:], w_emb.rearrange("(k p) n -> p k n", p=P)), (bemb[:], b_emb), (gnorm[:], g_norm),
                             (gqk[:, 0, :], g_q.broadcast_to([P, DK1])), (gqk[:, 1, :], g_k.broadcast_to([P, DK1])),
                             (w2[:, :, 0:T], w_out.rearrange("(k p) n -> p k n", p=P)),
                             (w2T[:], w_outT.rearrange("(k p) n -> p k n", p=P)),
                             (wr[:], w_r.rearrange("(k p) n -> p k n", p=P)), (br[:], b_r.broadcast_to([P, E]))):
                act.dma_start(dst, src).then_inc(S["small3"], 16)
            act.dma_start(wqkv[:], w_qkv.rearrange("(k p) n -> p k n", p=P)).then_inc(S["wqkv"], 16)

            def fixed():
                act.wait_ge(S["cst"], 16)

            fixed()

            def round_q(b):
                for n in range(2):
                    act.wait_ge(S["pq"], 2 * b + n + 1)
                    unless_first(act, S["qk"], 4 * b)
                    nc.scalar.activation(A[:, n * 512:(n + 1) * 512], PA[:, n * 512:(n + 1) * 512], ACT.Identity,
                                         bias=cst[:, C_EV:C_EV + 1]).then_inc(S["a"], 1)

            def values(b, par):
                act.wait_ge(S["v"], b + 1)
                if not (isinstance(b, int) and b < 2):
                    act.wait_ge(S["ctx"], b - 1)
                nc.scalar.copy(vu[:, par, :, :, 0:DK0], PD[:, 0:T].rearrange("p (k h d) -> p k h d", k=KT, h=H0)
                               ).then_inc(S["vu"], 1)

            def exps(b, c):
                unless_first(act, S["ctx"], b)
                act.wait_ge(S["st"], 4 * b + c + 1)
                nc.scalar.activation(probs[:, c, :], PC[:], ACT.Exp, scale=SCALE0).then_inc(S["ex"], 1)

            def context_high(b):
                act.wait_ge(S["wo"], b + 1)
                fixed()
                nc.scalar.copy(c_hi[:, :, bass.ds(b * P, P)],
                               PD[:, 512:512 + T].rearrange("p (k t) -> p k t", k=KT)).then_inc(S["ch"], 1)

            def entries(c):
                act.wait_ge(S["bit"], 4 * c + 4)
                unless_first(act, S["w0l"], c)
                for j in range(LUT // 2):
                    nc.scalar.activation(pick[:, j, :], bit[:, 0, :], ACT.Identity, scale=lutd[:, j:j + 1],
                                         bias=lutb[:, 2 * j:2 * j + 1]).then_inc(S["entry"], 1)

            act.wait_ge(S["ones"], 7)
            round_q(0)
            round_q(1)
            act.wait_ge(S["lutd"], 1)
            act.wait_ge(S["lut"], 16)
            entries(0)

            def body(i, par, before=True, after=True):
                exps(i - 1, 0)
                values(i - 1, 1 - par)
                exps(i - 1, 1)
                if before:
                    context_high(i - 2)
                exps(i - 1, 2)
                exps(i - 1, 3)
                if after:
                    round_q(i + 1)
                entries(i)

            body(1, 1, before=False)
            body(2, 0)
            with act.Fori(1, U - 1) as u:
                body(2 * u + 1, 1)
                body(2 * u + 2, 0)
            body(LAST, 1, after=False)
            exps(LAST, 0)
            values(LAST, 1)
            exps(LAST, 1)
            context_high(LAST - 1)
            exps(LAST, 2)
            exps(LAST, 3)
            context_high(LAST)

            def gate_chunk(c):
                for m in range(MT):
                    n = P if m < MT - 1 else MLAST
                    g = PA[0:n, (m % 2) * 512:(m % 2 + 1) * 512]
                    act.wait_ge(S["g"], MT * c + m + 1)
                    if m >= 2:
                        act.wait_ge(S["hf"], MT * c + m - 1)
                    else:
                        unless_first(act, S["hf"], MT * c)
                    nc.scalar.activation(sil[0:n, m % 2, :], g, ACT.Silu).then_inc(S["sil"], 1)
                    act.wait_ge(S["hf"], MT * c + m + 1)
                    unless_first(act, S["dn"], MT * c)
                    nc.scalar.copy(h_hi[0:n, m, :], hf[0:n, m % 2, :]).then_inc(S["hh"], 1)

            gate_chunk(0)
            with act.Fori(1, TOK // CH) as c:
                gate_chunk(c)

            def front(b, par, back):
                act.wait_ge(S["x1"], B)
                unless_first(act, S["ssq"], b)
                if back:
                    act.wait_ge(S["rstd"], b - 1)
                fixed()
                nc.scalar.activation(sqx[:].unsqueeze(1), rows[:, bass.ds(b, 1), T:2 * T], ACT.Square,
                                     scale=T ** -0.5, accum_out=ssq[:, par:par + 1]).then_inc(S["ssq"], 1)

            def squares(b, par, back):
                act.wait_ge(S["qkv"], 2 * b + 1)
                unless_first(act, S["ms"], b)
                nc.scalar.activation(sq, PB[:, 0:512], ACT.Square, scale=DK1 ** -0.5).then_inc(S["sq"], 1)
                act.wait_ge(S["qkv"], 2 * b + 2)
                if back:
                    act.wait_ge(S["c3"], b - 1)
                nc.scalar.copy(v1[:, par, :, 0:DK1], PB[:, 512:512 + T].rearrange("p (h d) -> p h d", h=H1)
                               ).then_inc(S["v1"], 1)

            def high_parts(b):
                act.wait_ge(S["qg"], b + 1)
                unless_first(act, S["qT"], 2 * b)
                unless_first(act, S["l4"], 2 * b)
                nc.scalar.copy(q4[:, :, 0:2, :], qk[:, 0].unsqueeze(2).broadcast_to([P, H1, 2, DK1])).then_inc(S["h4"], 1)
                nc.scalar.copy(k4[:, :, 0::2, :], qk[:, 1].unsqueeze(2).broadcast_to([P, H1, 2, DK1])).then_inc(S["h4"], 1)

            def exps1(b):
                unless_first(act, S["c3"], b)
                for c in range(2):
                    act.wait_ge(S["s3"], 2 * b + c + 1)
                    nc.scalar.activation(probs[:, c, :], PA[:], ACT.Exp, scale=DK1 ** -0.5, bias=gb[:]).then_inc(S["e3"], 1)

            def qT_out(b):
                act.wait_ge(S["qT"], 2 * b + 1)
                unless_first(act, S["s3"], 2 * b)
                nc.scalar.copy(qT, PC[:, 0:512].bitcast(BF16)).then_inc(S["qTe"], 1)

            def result(b):
                act.wait_ge(S["oT"], b + 1)
                unless_first(act, S["t3"], b)
                nc.scalar.copy(oT, PD[:, 512:512 + T]).then_inc(S["oTe"], 1)
                act.wait_ge(S["t3"], b + 1)
                fixed()
                nc.scalar.copy(rows[:, bass.ds(b, 1), 0:T], PD[:, 512:512 + T].unsqueeze(1)).then_inc(S["te3"], 1)

            act.wait_ge(S["gb"], 1)

            def body1(i, par, back):
                front(i, par, back)
                qT_out(i - 1)
                squares(i, par, back)
                exps1(i - 1)
                high_parts(i)
                result(i - 1)

            front(0, 0, False)
            squares(0, 0, False)
            high_parts(0)
            body1(1, 1, False)
            with act.Fori(1, U) as u:
                body1(2 * u, 0, True)
                body1(2 * u + 1, 1, True)
            qT_out(LAST)
            exps1(LAST)
            result(LAST)

            act.wait_ge(S["rx"], 1)
            nc.scalar.activation(ex[:], ex[:], ACT.Exp).then_inc(S["rx"], 1)

            def x_high(j, par):
                act.wait_ge(S["tT"], j + 1)
                nc.scalar.copy(xT_hi[:, par, :], PD[:, 0:T]).then_inc(S["th"], 1)

            def gate(j):
                act.wait_ge(S["gu"], j + 1)
                unless_first(act, S["hm"], j)
                nc.scalar.activation(gs, PA[:], ACT.Silu).then_inc(S["gs"], 1)

            def h_high(j):
                act.wait_ge(S["hT"], j + 1)
                unless_first(act, S["y"], j)
                nc.scalar.copy(hT_hi, PC[:]).then_inc(S["hTh"], 1)

            def tile(j, par, more=True):
                h_high(j - 1)
                gate(j)
                if more:
                    x_high(j + 1, 1 - par)

            x_high(0, 0)
            gate(0)
            x_high(1, 1)
            tile(1, 1)
            tile(2, 0)
            with act.Fori(1, (SLOTS - 2) // 2) as u:
                tile(2 * u + 1, 1)
                tile(2 * u + 2, 0)
            for j in range(SLOTS - 2 + (SLOTS % 2 == 0), SLOTS):
                tile(j, j % 2, j + 1 < SLOTS)
            h_high(SLOTS - 1)

        @block.tensor
        def _(pe):
            mm = nc.tensor.matmul
            pe.wait_ge(S["wq3"], 4)
            pe.wait_ge(S["cst"], 16)
            pe.wait_ge(S["init"], 2)
            pe.wait_ge(S["absent"], 2)
            pe.wait_ge(S["ones"], 7)
            pe.wait_ge(S["wq"], 32)

            def project(b, par):
                pe.wait_ge(S["xm"], 3 * b + 3)
                unless_first(pe, S["qk"], 4 * b)
                for pr in range(PAIRS):
                    mm(PA[:, pr * T:(pr + 1) * T], wq3[:, pr].rearrange("p a b c -> p (a b c)"), xm[:, par, :],
                       start=True, stop=False)
                    ins = mm(PA[:, pr * T:(pr + 1) * T], absent_row[:], absent[0:1, par, :], start=False, stop=True)
                    if pr % 2:
                        ins.then_inc(S["pq"], 1)

            def project_v(b, par):
                unless_first(pe, S["cq"], b)
                for kt in range(KT):
                    ins = mm(PD[:, kt * P:(kt + 1) * P], xs[:, par, kt * P:(kt + 1) * P], wq1[:], start=True, stop=True)
                ins.then_inc(S["v"], 1)

            def scores(b, par, c):
                pe.wait_ge(S["qk"], 4 * b + (2 if c < 2 else 4))
                unless_first(pe, S["max"], 4 * b + c)
                for s in range(2):
                    r = slice(64 * s, 64 * s + 64)
                    for qt in range(KT):
                        ins = mm(PB[:, s * 512 + qt * T:s * 512 + (qt + 1) * T],
                                 qs[r, par, c * T + qt * P:c * T + (qt + 1) * P], ks[r, par, c * T:(c + 1) * T],
                                 start=True, stop=True)
                ins.then_inc(S["sa"], 1)

            def scores_T(b, par, c):
                pp, kt = c // KT, c % KT
                pe.wait_ge(S["q2"], b + 1)
                unless_first(pe, S["ex"], 4 * b + c)
                for s in range(2):
                    r = slice(64 * s, 64 * s + 64)
                    for n in range(2):
                        pr = 2 * pp + n
                        ins = mm(PC[:, s * 512 + n * T:s * 512 + (n + 1) * T],
                                 ks[r, par, pr * T + kt * P:pr * T + (kt + 1) * P], qs[r, par, pr * T:(pr + 1) * T],
                                 start=True, stop=True)
                ins.then_inc(S["st"], 1)

            def contexts(b, par):
                pe.wait_ge(S["vu"], b + 1)
                for g in range(GROUPS):
                    for kt in range(KT):
                        pe.wait_ge(S["ex"], 4 * b + g * KT + kt + 1)
                        for j in range(GROUP):
                            pr, s = (g * GROUP + j) // 2, j % 2
                            o = s * 512 + (pr % 2) * T
                            ins = mm(PD[j * HS:(j + 1) * HS, g * T:(g + 1) * T], vu[:, par, kt, g * GROUP + j, :],
                                     probs[:, g * KT + kt, o:o + T], start=(kt == 0), stop=(kt == KT - 1))
                ins.then_inc(S["ctx"], 1)

            def max_rows(b):
                pe.wait_ge(S["mc"], 3 * b + 3)
                if not (isinstance(b, int) and b < 2):
                    pe.wait_ge(S["cl"], b - 1)
                M = PD[:, 512:1024].bitcast(BF16)
                for pr in range(PAIRS):
                    for qt in range(KT):
                        ins = pe.transpose(M[:, pr * T + qt * P:pr * T + (qt + 1) * P], mcol[:, qt, pr, :], identb[:])
                ins.then_inc(S["mt"], 1)

            def outputs0(b):
                pe.wait_ge(S["ct"], b + 1)
                pe.wait_ge(S["q2"], min(b + 2, B) if isinstance(b, int) else b + 2)
                if isinstance(b, int) and b == LAST:
                    pe.wait_ge(S["cl"], LAST)
                for qt in range(KT):
                    for g in range(GROUPS):
                        ins = mm(PD[:, 512 + qt * P:512 + (qt + 1) * P], cT[:, g, qt * P:(qt + 1) * P], wo2[:, g, :],
                                 start=(g == 0), stop=(g == GROUPS - 1))
                ins.then_inc(S["wo"], 1)

            project(0, 0)
            for c in range(4):
                scores(0, 0, c)
            project(1, 1)
            max_rows(0)

            def body(i, par, before=True, after=True):
                for c in range(4):
                    scores(i, par, c)
                    scores_T(i - 1, 1 - par, c)
                    if c == 0:
                        project_v(i - 1, 1 - par)
                    if c == 1 and before:
                        outputs0(i - 2)
                if after:
                    project(i + 1, 1 - par)
                contexts(i - 1, 1 - par)
                max_rows(i)

            body(1, 1, before=False)
            body(2, 0)
            with pe.Fori(1, U - 1) as u:
                body(2 * u + 1, 1)
                body(2 * u + 2, 0)
            body(LAST, 1, after=False)
            for c in range(4):
                scores_T(LAST, 1, c)
                if c == 0:
                    project_v(LAST, 1)
                if c == 1:
                    outputs0(LAST - 1)
            contexts(LAST, 1)
            outputs0(LAST)

            pe.wait_ge(S["w0h"], LCH)
            pe.wait_ge(S["w0l"], LCH)
            pe.wait_ge(S["ch"], B)
            pe.wait_ge(S["cl"], B)
            def chunk(c):
                tok = bass.ds(c * CH, CH)

                def up(m):
                    for which, bank, done in ((0, PA, "g"), (1, PB, "u")):
                        unless_first(pe, S["hf"], MT * c + max(m - 1, 0))
                        o = bank[:, (m % 2) * 512:(m % 2 + 1) * 512]
                        k = 0
                        for kt in range(KT):
                            for w, v in ((w0_hi, c_hi), (w0_hi, c_lo), (w0_lo, c_hi)):
                                ins = mm(o, w0(w, which, kt, m), v[:, kt, tok], start=(k == 0), stop=(k == 3 * KT - 1))
                                k += 1
                        ins.then_inc(S[done], 1)

                def down(m):
                    n = P if m < MT - 1 else MLAST
                    pe.wait_ge(S["hl"], MT * c + m + 1)
                    if m == 0:
                        unless_first(pe, S["x1"], TPC * c)
                    for t in range(TPC):
                        o = (PC, PD)[t // 2][:, (t % 2) * 512:(t % 2) * 512 + T]
                        for k, (v, w) in enumerate(((h_hi, w0_hi), (h_hi, w0_lo), (h_lo, w0_hi))):
                            ins = mm(o, v[0:n, m, t * P:(t + 1) * P], w0d(w, m), start=(m == 0 and k == 0),
                                     stop=(m == MT - 1 and k == 2))
                    ins.then_inc(S["dn"], 1)

                up(0)
                for m in range(1, MT):
                    up(m)
                    down(m - 1)
                down(MT - 1)

            chunk(0)
            with pe.Fori(1, TOK // CH) as c:
                chunk(c)

            pe.wait_ge(S["x1"], B)
            pe.wait_ge(S["small3"], 16 * 9)
            pe.wait_ge(S["ck"], 16)
            for m in range(4):
                for kt in range(KT):
                    ins = mm(PA[:, m * B:(m + 1) * B], wemb[:, kt, m * P:(m + 1) * P], ck[:, kt, :],
                             start=(kt == 0), stop=(kt == KT - 1))
            ins.then_inc(S["emb"], 1)
            pe.wait_ge(S["w2a"], 2 * KT)
            for m in range(KT):
                for kt in range(KT):
                    ins = mm(PB[:, m * E:(m + 1) * E], w2T[:, kt, m * P:(m + 1) * P], wr[:, kt, :],
                             start=(kt == 0), stop=(kt == KT - 1))
            ins.then_inc(S["w2r"], 1)
            pe.wait_ge(S["gcol"], 4)
            pe.wait_ge(S["w2"], 1)
            pe.wait_ge(S["wqkv"], 16)

            def norm_qkv(b):
                pe.wait_ge(S["xr"], b + 1)
                unless_first(pe, S["v1"], b)
                for kt in range(KT):
                    ins = pe.transpose(PB[:, 512 + kt * P:512 + (kt + 1) * P], xr[:, kt * P:(kt + 1) * P], ident)
                ins.then_inc(S["xt3"], 1)

            def qkv(b):
                pe.wait_ge(S["xnT"], 2 * b + 2)
                unless_first(pe, S["qkn"], b)
                for kt in range(KT):
                    ins = mm(PB[:, 0:512], xnT[:, kt, :], wqkv[:, kt, 0:512], start=(kt == 0), stop=(kt == KT - 1))
                ins.then_inc(S["qkv"], 1)
                for kt in range(KT):
                    ins = mm(PB[:, 512:512 + T], xnT[:, kt, :], wqkv[:, kt, 512:768], start=(kt == 0), stop=(kt == KT - 1))
                ins.then_inc(S["qkv"], 1)

            def turn(b):
                pe.wait_ge(S["l4"], 2 * b + 2)
                for n, (src, done) in enumerate(((q4, "qTe"), (k4, "kTe"))):
                    unless_first(pe, S[done], b)
                    bank = PC[:, n * 512:(n + 1) * 512].bitcast(BF16)
                    for pr in range(H1 // 2):
                        ins = pe.transpose(bank[:, pr * P:(pr + 1) * P],
                                           src[:, 2 * pr:2 * pr + 2].rearrange("p h s d -> p (h s d)"), identb[:])
                    ins.then_inc(S["qT"], 1)

            def scores1(b, c):
                pe.wait_ge(S["qTe"], b + 1)
                pe.wait_ge(S["kTe"], b + 1)
                unless_first(pe, S["e3"], 2 * b + c)
                for s in range(2):
                    r = slice(64 * s, 64 * s + 64)
                    for n in range(4):
                        pr = 4 * c + n
                        ins = mm(PA[:, s * 512 + n * P:s * 512 + (n + 1) * P], kT[r, pr * P:(pr + 1) * P],
                                 qT[r, pr * P:(pr + 1) * P], start=True, stop=True)
                ins.then_inc(S["s3"], 1)

            def contexts1(b, par):
                pe.wait_ge(S["v1"], b + 1)
                unless_first(pe, S["on"], b)
                for h in range(H1):
                    if h % 8 == 0:
                        pe.wait_ge(S["e3"], 2 * b + h // 8 + 1)
                    pr, s = h // 2, h % 2
                    o = s * 512 + (pr % 4) * P
                    ins = mm(PD[:, h * (DK1 + 1):(h + 1) * (DK1 + 1)], probs[:, pr // 4, o:o + P], v1[:, par, h, :],
                             start=True, stop=True)
                ins.then_inc(S["c3"], 1)

            def outputs(b):
                pe.wait_ge(S["on"], b + 1)
                unless_first(pe, S["lg"], b)
                unless_first(pe, S["te3"], b)
                for kt in range(KT):
                    ins = pe.transpose(PD[:, 512 + kt * P:512 + (kt + 1) * P],
                                       on.rearrange("p h d -> p (h d)")[:, kt * P:(kt + 1) * P], ident)
                ins.then_inc(S["oT"], 1)
                pe.wait_ge(S["oTe"], b + 1)
                for kt in range(KT):
                    ins = mm(PD[:, 512:512 + T + E], oT[:, kt * P:(kt + 1) * P], w2[:, kt, :], start=(kt == 0), stop=(kt == KT - 1))
                ins.then_inc(S["t3"], 1)

            def body1(i, par):
                norm_qkv(i)
                turn(i - 1)
                qkv(i)
                scores1(i - 1, 0)
                scores1(i - 1, 1)
                contexts1(i - 1, 1 - par)
                outputs(i - 1)

            norm_qkv(0)
            qkv(0)
            body1(1, 1)
            with pe.Fori(1, U) as u:
                body1(2 * u, 0)
                body1(2 * u + 1, 1)
            turn(LAST)
            scores1(LAST, 0)
            scores1(LAST, 1)
            contexts1(LAST, 1)
            outputs(LAST)

            pe.wait_ge(S["r"], 1)
            flat = oh[:].rearrange("p b e -> p (b e)")
            mm(PA[:, 0:B * E], cst[:, C_TRI:C_TRI + P], flat, start=True, stop=True)
            mm(PB[:, 0:B * E], ones[:], flat, start=True, stop=True).then_inc(S["rp"], 1)

            for n in range(3):
                pe.wait_ge(S[f"wsl{n}"], U)
            pe.wait_ge(S["te"], 1)

            def tile_in(j, half, par):
                pe.wait_ge(S[f"xld{par}"], 16 * (half + 1))
                unless_first(pe, S["tl"], j)
                for kt in range(KT):
                    ins = pe.transpose(PD[:, kt * P:(kt + 1) * P], xin[:, par, kt * P:(kt + 1) * P], ident)
                ins.then_inc(S["tT"], 1)

            def gate_up(j, par, e, bank, w_hi, w_lo, free, done):
                pe.wait_ge(S["tl"], j + 1)
                unless_first(pe, S[free], j)
                for n in range(2):
                    k = 0
                    for kt in range(KT):
                        o = bass.ds(e * (KT * FF) + (kt * FF + n * 512), 512)
                        xo = slice(kt * P, (kt + 1) * P)
                        for v, w in ((xT_hi, w_hi), (xT_hi, w_lo), (xT_lo, w_hi)):
                            ins = mm(bank[:, n * 512:(n + 1) * 512], v[:, par, xo], w[:, o], start=(k == 0), stop=(k == 3 * KT - 1))
                            k += 1
                ins.then_inc(S[done], 1)

            def turn_h(j):
                pe.wait_ge(S["hm"], j + 1)
                unless_first(pe, S["hTl"], j)
                for f in range(FT):
                    ins = pe.transpose(PC[:, f * P:(f + 1) * P], hh[:, f * P:(f + 1) * P], ident)
                ins.then_inc(S["hT"], 1)

            def down(j, e):
                pe.wait_ge(S["hTh"], j + 1)
                pe.wait_ge(S["hTl"], j + 1)
                unless_first(pe, S["yo"], j)
                k = 0
                for f in range(FT):
                    o = bass.ds(e * (FT * T) + f * T, T)
                    for v, w in ((hT_hi, wd_hi), (hT_hi, wd_lo), (hT_lo, wd_hi)):
                        ins = mm(PD[:, 512:512 + T], v[:, f * P:(f + 1) * P], w[:, o], start=(k == 0), stop=(k == 3 * FT - 1))
                        k += 1
                ins.then_inc(S["y"], 1)

            def expert_of(j):
                return pe.value_load(te[0:1, bass.ds(j, 1)], min_val=0, max_val=E - 1)

            def tile(j, half, par, more=True):
                gate_up(j, par, expert_of(j), PA, wg_hi, wg_lo, "gs", "gu")
                turn_h(j - 1)
                gate_up(j, par, expert_of(j), PB, wu_hi, wu_lo, "hm", "uu")
                if more:
                    tile_in(j + 1, half + par, 1 - par)
                down(j - 1, expert_of(j - 1))

            tile_in(0, 0, 0)
            gate_up(0, 0, expert_of(0), PA, wg_hi, wg_lo, "gs", "gu")
            gate_up(0, 0, expert_of(0), PB, wu_hi, wu_lo, "hm", "uu")
            tile_in(1, 0, 1)
            tile(1, 0, 1)
            tile(2, 1, 0)
            with pe.Fori(1, (SLOTS - 2) // 2) as u:
                tile(2 * u + 1, u, 1)
                tile(2 * u + 2, u + 1, 0)
            for j in range(SLOTS - 2 + (SLOTS % 2 == 0), SLOTS):
                tile(j, j // 2, j % 2, j + 1 < SLOTS)
            turn_h(SLOTS - 1)
            down(SLOTS - 1, expert_of(SLOTS - 1))

        @block.vector
        def _(dve):
            v = nc.vector
            v.memset(wq3[:], 0.0).then_inc(S["wq3"], 1)
            v.memset(absent_row[:], 0.0).then_inc(S["absent"], 1)
            v.memset(mcol, 0.0).then_inc(S["init"], 1)
            dve.wait_ge(S["absent"], 1)
            v.memset(absent_row[:, 50::64], 1.0).then_inc(S["absent"], 1)
            dve.wait_ge(S["wq"], 32)
            dve.wait_ge(S["wq3"], 1)
            for s in range(3):
                v.tensor_copy(wq3[:, :, :, s, :], wq1[:].rearrange("p (r a d) -> p r a d", r=PAIRS, a=2)).then_inc(S["wq3"], 1)
            dve.wait_ge(S["cst"], 16)
            v.tensor_copy(identb[:], ident).then_inc(S["init"], 1)
            dve.wait_ge(S["ck"], 16)
            v.tensor_scalar(nbig[:], ck[:], -NEG, None, ALU.mult).then_inc(S["kprep"], 1)
            dve.wait_ge(S["lut"], 16)
            pairs = lutb[:].rearrange("p (j t) -> p j t", t=2)
            v.tensor_tensor(lutd[:], pairs[:, :, 1], pairs[:, :, 0], ALU.subtract).then_inc(S["lutd"], 1)
            dve.wait_ge(S["kprep"], 1)

            def bits(c):
                dve.wait_ge(S["idx"], 16 * c + 16)
                if not (isinstance(c, int) and c == 0):
                    dve.wait_ge(S["pick"], 3 * c)
                    dve.wait_ge(S["entry"], 8 * c)
                for n in range(4):
                    v.tensor_scalar(bit[:, n, :], idx, 1 << n, None, ALU.bitwise_and).then_inc(S["bit"], 1)

            def select(c, n):
                step = 1 << n
                k = (LUT // 2) // step
                tree = pick.rearrange("p (k s) c -> p k s c", k=k)
                v.copy_predicated(tree[:, :, 0, :], bit[:, n, :].unsqueeze(1).broadcast_to([P, k, LW]),
                                  tree[:, :, step // 2, :]).then_inc(S["pick"], 1)

            def selected(c):
                dve.wait_ge(S["pick"], 3 * c + 3)
                o = bass.ds(c * LW, LW)
                v.tensor_copy(w0_hi[:, o], pick[:, 0, :]).then_inc(S["w0h"], 1)
                dve.wait_ge(S["w0h"], c + 1)
                v.tensor_tensor(w0_lo[:, o], pick[:, 0, :], w0_hi[:, o], ALU.subtract).then_inc(S["w0l"], 1)

            def stack(b, par):
                if not (isinstance(b, int) and b < 2):
                    dve.wait_ge(S["st"], 4 * (b - 1))
                for n in range(2):
                    dve.wait_ge(S["a"], 2 * b + n + 1)
                    o = slice(n * 512, (n + 1) * 512)
                    for dst, c in ((qs, C_SQ), (ks, C_SK)):
                        v.scalar_tensor_tensor(out=dst[:, par, o], in0=A[:, o], scalar=cst[:, c:c + 1], in1=PA[:, o],
                                               op0=ALU.mult, op1=ALU.add).then_inc(S["qk"], 1)

            def maxima(b, piece=None):
                for c in range(4):
                    if piece is not None:
                        if c == 0:
                            dve.wait_ge(S["entry"], 8 * piece + 8)
                        elif c < 3:
                            dve.wait_ge(S["pick"], 3 * piece + c)
                    dve.wait_ge(S["sa"], 4 * b + c + 1)
                    if c == 0:
                        unless_first(dve, S["mc"], 3 * b)
                    v.tensor_reduce(nmax[:, c].rearrange("p s q -> p (s q)"), PB[:].rearrange("p (a k) -> p a k", k=T),
                                    AX.X, ALU.max, negate=True).then_inc(S["max"], 1)
                    if piece is not None and c < 3:
                        select(piece, c + 1)
                dve.wait_ge(S["max"], 4 * b + 4)
                unless_first(dve, S["mt"], b)
                cols = mcol.rearrange("p q r (s m) -> p r s q m", s=2)
                v.tensor_copy(cols[:, :, :, :, 48], nmax[:]).then_inc(S["mc"], 1)
                dve.wait_ge(S["mc"], 3 * b + 1)
                v.tensor_tensor(cols[:, :, :, :, 49], nmax[:], cols[:, :, :, :, 48], ALU.subtract).then_inc(S["mc"], 1)
                v.tensor_copy(mcol[:, :, :, 50::64].rearrange("p q r s -> p q (r s)"),
                              nbig[:, :, bass.ds(b, 1)].broadcast_to([P, KT, 2 * PAIRS])).then_inc(S["mc"], 1)

            def add_max(b, par):
                dve.wait_ge(S["mt"], b + 1)
                v.tensor_tensor(qs[:, par, :], PD[:, 512:1024].bitcast(BF16), qs[:, par, :], ALU.add).then_inc(S["q2"], 1)

            def normalise(b):
                cx = cq.rearrange("p (n d) -> p n d", d=HS)
                v.transpose(cq, PD[:, 0:GROUPS * T]).then_inc(S["cq"], 1)
                dve.wait_ge(S["cq"], b + 1)
                v.reciprocal(rden[:], cx[:, :, DK0]).then_inc(S["rd"], 1)
                dve.wait_ge(S["rd"], b + 1)
                v.tensor_tensor(cx[:, :, 0:DK0], cx[:, :, 0:DK0], rden[:].unsqueeze(2).broadcast_to([P, GROUPS * T // HS, DK0]),
                                ALU.mult).then_inc(S["cn"], 1)
                unless_first(dve, S["wo"], b)
                dve.wait_ge(S["cn"], b + 1)
                v.transpose(cT.rearrange("p g t -> p (g t)"), cq).then_inc(S["ct"], 1)

            def low_c(b):
                dve.wait_ge(S["ch"], b + 1)
                o = bass.ds(b * P, P)
                v.tensor_tensor(c_lo[:, :, o], PD[:, 512:512 + T].rearrange("p (k t) -> p k t", k=KT), c_hi[:, :, o],
                                ALU.subtract).then_inc(S["cl"], 1)

            def body(i, par, before=True, after=True):
                maxima(i, i - 1)
                if before:
                    low_c(i - 2)
                selected(i - 1)
                bits(i)
                if after:
                    stack(i + 1, 1 - par)
                dve.wait_ge(S["ctx"], i)
                add_max(i, par)
                normalise(i - 1)

            stack(0, 0)
            maxima(0)
            bits(0)
            stack(1, 1)
            add_max(0, 0)
            body(1, 1, before=False)
            body(2, 0)
            with dve.Fori(1, U - 1) as u:
                body(2 * u + 1, 1)
                body(2 * u + 2, 0)
            body(LAST, 1, after=False)
            dve.wait_ge(S["entry"], 8 * B)
            for n in range(1, 4):
                if n > 1:
                    dve.wait_ge(S["pick"], 3 * LAST + n - 1)
                select(LAST, n)
            selected(LAST)
            low_c(LAST - 1)
            dve.wait_ge(S["ctx"], B)
            normalise(LAST)
            low_c(LAST)

            def hidden_chunk(c):
                for m in range(MT):
                    n = P if m < MT - 1 else MLAST
                    k = MT * c + m
                    dve.wait_ge(S["sil"], k + 1)
                    dve.wait_ge(S["u"], k + 1)
                    unless_first(dve, S["hl"], k if m == 0 else k - 1)
                    v.tensor_tensor(hf[0:n, m % 2, :], PB[0:n, (m % 2) * 512:(m % 2 + 1) * 512], sil[0:n, m % 2, :],
                                    ALU.mult).then_inc(S["hf"], 1)
                    dve.wait_ge(S["hh"], k + 1)
                    v.tensor_tensor(h_lo[0:n, m, :], hf[0:n, m % 2, :], h_hi[0:n, m, :], ALU.subtract).then_inc(S["hl"], 1)
                dve.wait_ge(S["dn"], MT * c + MT)
                for t in range(TPC):
                    b = TPC * c + t
                    v.tensor_tensor(rows[:, bass.ds(b, 1), T:2 * T],
                                    (PC, PD)[t // 2][:, (t % 2) * 512:(t % 2) * 512 + T].unsqueeze(1),
                                    xall[:, bass.ds(b, 1), :], ALU.add).then_inc(S["x1"], 1)

            hidden_chunk(0)
            with dve.Fori(1, TOK // CH) as c:
                hidden_chunk(c)

            dve.wait_ge(S["small3"], 16 * 9)
            for kt in range(KT):
                v.tensor_tensor(w2[:, kt, kt * P:(kt + 1) * P], w2[:, kt, kt * P:(kt + 1) * P], ident, ALU.add
                                ).then_inc(S["w2a"], 1)
                v.tensor_tensor(w2T[:, kt, kt * P:(kt + 1) * P], w2T[:, kt, kt * P:(kt + 1) * P], ident, ALU.add
                                ).then_inc(S["w2a"], 1)
            v.tensor_tensor(gg[:], gqk[:, 0], gqk[:, 1], ALU.mult).then_inc(S["gg"], 1)
            dve.wait_ge(S["gg"], 1)
            v.tensor_reduce(gb[:], gg[:], AX.X, ALU.max, apply_absolute_value=True).then_inc(S["gmx"], 1)
            dve.wait_ge(S["gmx"], 1)
            v.tensor_scalar(gb[:], gb[:], -(DK1 ** 0.5), None, ALU.mult).then_inc(S["gb"], 1)
            dve.wait_ge(S["emb"], 1)
            for kt in range(KT):
                v.tensor_scalar(gcol[:, kt, :], PA[:, kt * B:(kt + 1) * B], bemb[:, kt:kt + 1], 1.0, ALU.add, ALU.add
                                ).then_inc(S["gcol"], 1)
                v.tensor_scalar(scol[:, kt, :], PA[:, (KT + kt) * B:(KT + kt + 1) * B], bemb[:, KT + kt:KT + kt + 1], None,
                                ALU.add).then_inc(S["gcol"], 1)
            dve.wait_ge(S["gcol"], 4)
            for kt in range(KT):
                v.tensor_scalar(gcol[:, kt, :], gcol[:, kt, :], gnorm[:, kt:kt + 1], None, ALU.mult).then_inc(S["gcol"], 1)
            dve.wait_ge(S["w2r"], 1)
            v.tensor_copy(w2[:, :, T:T + E], PB[:, 0:KT * E].rearrange("p (k e) -> p k e", k=KT)).then_inc(S["w2"], 1)
            dve.wait_ge(S["gcol"], 6)

            def scaled(b, par):
                dve.wait_ge(S["rstd"], b + 1)
                unless_first(dve, S["xt3"], b)
                v.tensor_scalar(xr.unsqueeze(1), rows[:, bass.ds(b, 1), T:2 * T], rstd[:, par:par + 1], None, ALU.mult
                                ).then_inc(S["xr"], 1)

            def modulated(b):
                dve.wait_ge(S["xt3"], b + 1)
                unless_first(dve, S["qkv"], 2 * b)
                for kt in range(KT):
                    v.tensor_scalar(xnT[:, kt, :], PB[:, 512 + kt * P:512 + (kt + 1) * P], gcol[:, kt, bass.ds(b, 1)],
                                    scol[:, kt, bass.ds(b, 1)], ALU.mult, ALU.add).then_inc(S["xnT"], 1)

            def kT_out(b):
                dve.wait_ge(S["qT"], 2 * b + 2)
                unless_first(dve, S["s3"], 2 * b)
                v.tensor_copy(kT, PC[:, 512:1024].bitcast(BF16)).then_inc(S["kTe"], 1)

            def qk_norm(b):
                dve.wait_ge(S["sq"], b + 1)
                unless_first(dve, S["rs"], b)
                v.tensor_reduce(msr[:], sq.rearrange("p (h d) -> p h d", d=DK1), AX.X, ALU.add).then_inc(S["mean"], 1)
                dve.wait_ge(S["mean"], b + 1)
                v.tensor_scalar(ms[:], msr[:], EPS, None, ALU.add).then_inc(S["ms"], 1)
                dve.wait_ge(S["rs"], b + 1)
                unless_first(dve, S["h4"], 2 * b)
                unless_first(dve, S["l4"], 2 * b)
                v.tensor_tensor(qk.rearrange("p a h d -> p (a h) d"), PB[:, 0:512].rearrange("p (h d) -> p h d", d=DK1),
                                rs[:].unsqueeze(2).broadcast_to([P, 2 * H1, DK1]), ALU.mult).then_inc(S["qkn"], 1)

            def low_parts(b):
                dve.wait_ge(S["h4"], 2 * b + 1)
                unless_first(dve, S["qT"], 2 * b)
                v.tensor_tensor(q4[:, :, 2:4, :], qk[:, 0].unsqueeze(2).broadcast_to([P, H1, 2, DK1]), q4[:, :, 0:2, :],
                                ALU.subtract).then_inc(S["l4"], 1)
                dve.wait_ge(S["h4"], 2 * b + 2)
                v.tensor_tensor(k4[:, :, 1::2, :], qk[:, 1].unsqueeze(2).broadcast_to([P, H1, 2, DK1]), k4[:, :, 0::2, :],
                                ALU.subtract).then_inc(S["l4"], 1)

            def normalise1(b):
                cx = PD[:, 0:H1 * (DK1 + 1)].rearrange("p (h d) -> p h d", h=H1)
                dve.wait_ge(S["c3"], b + 1)
                unless_first(dve, S["oT"], b)
                v.reciprocal(rden1[:], cx[:, :, DK1]).then_inc(S["rd3"], 1)
                dve.wait_ge(S["rd3"], b + 1)
                v.tensor_tensor(on, cx[:, :, 0:DK1], rden1[:].unsqueeze(2).broadcast_to([P, H1, DK1]), ALU.mult
                                ).then_inc(S["on"], 1)

            def logits(b):
                dve.wait_ge(S["te3"], b + 1)
                v.tensor_tensor(lg[:, bass.ds(b, 1), :], PD[:, 512 + T:512 + T + E].unsqueeze(1), br[:].unsqueeze(1), ALU.add
                                ).then_inc(S["lg"], 1)

            def body1(i, par):
                scaled(i, par)
                modulated(i)
                kT_out(i - 1)
                qk_norm(i)
                normalise1(i - 1)
                low_parts(i)
                logits(i - 1)

            scaled(0, 0)
            modulated(0)
            qk_norm(0)
            low_parts(0)
            body1(1, 1)
            with dve.Fori(1, U) as u:
                body1(2 * u, 0)
                body1(2 * u + 1, 1)
            kT_out(LAST)
            normalise1(LAST)
            logits(LAST)

            n_r = [0]

            def done(ins):
                ins.then_inc(S["rv"], 1)
                n_r[0] += 1
                dve.wait_ge(S["rv"], n_r[0])

            dve.wait_ge(S["lg"], B)
            wide = lmx[:].unsqueeze(2).broadcast_to([P, B, E])
            done(v.tensor_reduce(lmx[:], lg[:], AX.X, ALU.max))
            v.tensor_tensor(ex[:], lg[:], wide, ALU.subtract).then_inc(S["rx"], 1)
            done(v.tensor_tensor(oh[:], lg[:], wide, ALU.is_equal))
            done(v.tensor_copy(taken[:], oh[:, :, 0]))
            for e in range(1, E):
                last = v.tensor_tensor(oh[:, :, e], oh[:, :, e], taken[:], ALU.is_gt)
                if e < E - 1:
                    done(last)
                    done(v.tensor_tensor(taken[:], oh[:, :, e], taken[:], ALU.max))
            last.then_inc(S["r"], 1)
            dve.wait_ge(S["rx"], 2)
            done(v.tensor_reduce(es[:], ex[:], AX.X, ALU.add))
            v.reciprocal(rows[:, :, 2 * T], es[:]).then_inc(S["rows"], 1)
            dve.wait_ge(S["rp"], 1)
            done(v.tensor_copy(tot[:], PB[:, 0:B * E].rearrange("p (b e) -> p e b", e=E)))
            for e in range(E):
                done(v.tensor_tensor_scan(run[:, e, :], ones[:, 0:B], tot[:, e, :], 0.0, ALU.mult, ALU.add))
            done(v.tensor_scalar(cnt[:], run[:, :, B - 1], float(P - 1), None, ALU.add))
            done(v.tensor_scalar(cnt[:], cnt[:], P.bit_length() - 1, None, ALU.arith_shift_right))
            done(v.tensor_copy(ntile[:], cnt[:]))
            done(v.memset(first[:], 0.0))
            for e in range(1, E):
                done(v.tensor_tensor(first[:, e:e + 1], first[:, e - 1:e], ntile[:, e - 1:e], ALU.add))
            tiles = cst[:, C_ROWS:C_ROWS + SLOTS]
            done(v.tensor_scalar(tef[:], tiles, first[:, 1:2], None, ALU.is_ge))
            for e in range(2, E):
                done(v.scalar_tensor_tensor(out=tef[:], in0=tiles, scalar=first[:, e:e + 1], in1=tef[:], op0=ALU.is_ge,
                                            op1=ALU.add))
            v.tensor_copy(te[:], tef[:]).then_inc(S["te"], 1)
            done(v.tensor_tensor(place[:], run[:].rearrange("p e b -> p b e"), tot[:].rearrange("p e b -> p b e"), ALU.subtract))
            done(v.tensor_tensor(place[:], PA[:, 0:B * E].rearrange("p (b e) -> p b e", e=E), place[:], ALU.add))
            done(v.scalar_tensor_tensor(out=place[:], in0=first[:].unsqueeze(1).broadcast_to([P, B, E]), scalar=float(P),
                                        in1=place[:], op0=ALU.mult, op1=ALU.add))
            done(v.tensor_tensor(place[:], place[:], oh[:], ALU.mult))
            done(v.tensor_reduce(slotf[:], place[:], AX.X, ALU.add))
            v.tensor_copy(slot[:], slotf[:]).then_inc(S["slot"], 1)

            def x_low(j, par):
                dve.wait_ge(S["th"], j + 1)
                v.tensor_tensor(xT_lo[:, par, :], PD[:, 0:T], xT_hi[:, par, :], ALU.subtract).then_inc(S["tl"], 1)

            def hidden(j):
                dve.wait_ge(S["gs"], j + 1)
                dve.wait_ge(S["uu"], j + 1)
                unless_first(dve, S["hT"], j)
                v.tensor_tensor(hh, PB[:], gs, ALU.mult).then_inc(S["hm"], 1)

            def h_low(j):
                dve.wait_ge(S["hTh"], j + 1)
                unless_first(dve, S["y"], j)
                v.tensor_tensor(hT_lo, PC[:], hT_hi, ALU.subtract).then_inc(S["hTl"], 1)

            def result(j, par, half, back):
                dve.wait_ge(S["y"], j + 1)
                dve.wait_ge(S[f"res{par}"], 16 * half + 16)
                if back:
                    dve.wait_ge(S[f"so{par}"], 16 * half)
                v.tensor_copy(tokn[:, par:par + 1], xres[:, par, T + 1:T + 2].bitcast(I32)).then_inc(S["idn"], 1)
                v.scalar_tensor_tensor(out=yo[:, par, :], in0=PD[:, 512:512 + T], scalar=xres[:, par, T:T + 1],
                                       in1=xres[:, par, 0:T], op0=ALU.mult, op1=ALU.add).then_inc(S["yo"], 1)

            x_low(0, 0)
            hidden(0)
            x_low(1, 1)

            def tile(j, par, half, back, more=True):
                h_low(j - 1)
                hidden(j)
                if more:
                    x_low(j + 1, 1 - par)
                result(j - 1, 1 - par, half, back)

            tile(1, 1, 0, False)
            tile(2, 0, 0, False)
            with dve.Fori(1, (SLOTS - 2) // 2) as u:
                tile(2 * u + 1, 1, u, True)
                tile(2 * u + 2, 0, u, True)
            for j in range(SLOTS - 2 + (SLOTS % 2 == 0), SLOTS):
                tile(j, j % 2, (j - 1) // 2, True, j + 1 < SLOTS)
            h_low(SLOTS - 1)
            result(SLOTS - 1, (SLOTS - 1) % 2, (SLOTS - 1) // 2, True)


def kernel(x, cond_2048, L0_cond_Wq, L0_cond_Wo, L0_ffn_lut, L0_ffn_gate_idx, L0_ffn_up_idx, L0_ffn_down_idx,
           L1_cond_W_emb, L1_cond_b_emb, L1_cond_g_norm, L1_cond_W_qkv, L1_cond_g_q, L1_cond_g_k, L1_cond_W_out,
           L1_ffn_Wr, L1_ffn_br, L1_ffn_Wg, L1_ffn_Wu, L1_ffn_Wd):
    import concourse.bacc as bacc
    from concourse.bass_utils import run_bass_kernel_spmd

    def by_rows(w):
        w = np.asarray(w)
        return w.reshape(-1, P, w.shape[-1]).transpose(1, 0, 2).reshape(P, -1)

    down = np.asarray(L0_ffn_down_idx).T
    down = np.concatenate([down, np.zeros((MT * P - INTER, T), down.dtype)])
    wo = np.zeros((GROUPS, GROUP, HS, P), np.float32)
    wo[:, :, 0:DK0] = np.asarray(L0_cond_Wo).T.reshape(GROUPS, GROUP, DK0, P)
    arrays = {
        "x": x, "cond": cond_2048, "condT": np.asarray(cond_2048).T.reshape(KT, P, B).transpose(1, 0, 2),
        "consts": constants(), "wqT": np.asarray(L0_cond_Wq).T, "woT": by_rows(wo.reshape(GROUPS * P, P)),
        "lut": np.asarray(L0_ffn_lut).reshape(1, LUT),
        "idx_all": np.concatenate([by_rows(np.asarray(L0_ffn_gate_idx).T), by_rows(np.asarray(L0_ffn_up_idx).T),
                                   by_rows(down)], axis=1),
        "w_emb": L1_cond_W_emb, "b_emb": np.asarray(L1_cond_b_emb).reshape(4, P).T,
        "g_norm": np.asarray(L1_cond_g_norm).reshape(KT, P).T, "w_qkv": L1_cond_W_qkv,
        "g_q": np.asarray(L1_cond_g_q).reshape(1, DK1), "g_k": np.asarray(L1_cond_g_k).reshape(1, DK1),
        "w_out": L1_cond_W_out, "w_outT": np.asarray(L1_cond_W_out).T, "w_r": L1_ffn_Wr,
        "b_r": np.asarray(L1_ffn_br).reshape(1, E),
        "w_g": by_rows(np.asarray(L1_ffn_Wg).reshape(E * T, FF)), "w_u": by_rows(np.asarray(L1_ffn_Wu).reshape(E * T, FF)),
        "w_d": by_rows(np.asarray(L1_ffn_Wd).reshape(E * FF, T)),
    }
    arrays = {f"in_{k}": np.ascontiguousarray(a) for k, a in arrays.items()}
    nc = bacc.Bacc("TRN2", target_bir_lowering=False, num_devices=1)
    args = [nc.dram_tensor(k, a.shape, mybir.dt.from_np(a.dtype), kind="ExternalInput").ap() for k, a in arrays.items()]
    out = nc.dram_tensor("out", (TOK, T), F32, kind="ExternalOutput").ap()
    routed = nc.dram_tensor("routed", (SLOTS * P, ROW), F32, kind="Internal").ap()
    program(nc, *args, out, routed)
    got = run_bass_kernel_spmd(nc, [arrays], core_ids=[0]).results[0]["out"]
    return got.reshape(B, D, T)
```

```python
from contextlib import ExitStack

import numpy as np

import concourse.bass as bass
from concourse import mybir

F32 = mybir.dt.float32
BF16 = mybir.dt.bfloat16
I32 = mybir.dt.int32
ALU = mybir.AluOpType
ACT = mybir.ActivationFunctionType
AX = mybir.AxisListType

P = 128
B, D, T = 16, 128, 256
KT = T // P
H0, DK0 = 8, 16
PAIRS = H0 // 2
SCALE0 = DK0 ** -0.5
INTER = 688
MT = -(-INTER // P)
MLAST = INTER - (MT - 1) * P
LUT = 16
H1, DK1 = 16, 16
EPS = 1e-6
E, FF = 4, 1024
FT = FF // P
TOK = B * D
CH = 512
TPC = CH // P
SLOTS = TOK // P + E - 1
ROW = 2 * T + 2
NEG = 1e30
DUMMY = 2 * TOK

GCOLS = KT * INTER
WCOLS = 2 * GCOLS + MT * T
LCH = B
LW = WCOLS // LCH

C_ID, C_TRI, C_SQ, C_SK, C_EV, C_ROWS = 0, P, 2 * P, 2 * P + 1, 2 * P + 2, 2 * P + 3
HS = 32
GROUP = P // HS
RSQRT = 0x5f3759df
NEWTON = 3
C_N = C_ROWS + SLOTS


def constants():
    c = np.zeros((P, C_N), np.float32)
    p = np.arange(P)
    c[:, C_ID:C_ID + P] = np.eye(P)
    c[:, C_TRI:C_TRI + P] = p[:, None] < p[None, :]
    slot, r = p % 64 // 16, p % 64
    c[:, C_SQ] = np.where((slot == 2) | (r == 50), -1, 0)
    c[:, C_SK] = np.where(slot == 1, -1, np.where((r == 48) | (r == 49), 1, 0))
    c[:, C_EV] = (r == 48) | (r == 49)
    c[:, C_ROWS:] = np.arange(SLOTS)
    return c


def program(nc, x, cond, condT, consts, wqT, woT, lut, idx_all, w_emb, b_emb, g_norm, w_qkv, g_q, g_k,
            w_out, w_outT, w_r, b_r, w_g, w_u, w_d, out, routed):
    with ExitStack() as ctx:
        def sb(name, shape, dt=F32):
            return ctx.enter_context(nc.sbuf_tensor(name, shape, dt))

        def sem(name):
            return ctx.enter_context(nc.semaphore(name))

        PA, PB, PC, PD = (ctx.enter_context(nc.psum_tensor(n, [P, 1024], F32)) for n in ("PA", "PB", "PC", "PD"))

        cst = sb("cst", [P, C_N])
        ident = cst[:, C_ID:C_ID + P]
        identb = sb("identb", [P, P], BF16)
        ones = sb("ones", [P, P])
        ck = sb("ck", [P, KT, B])
        rows = sb("rows", [P, B, ROW])

        HALF = E * KT * FF
        arena = sb("arena", [P, 3 * HALF])
        at = [0]

        def f32(*shape):
            n = int(np.prod(shape))
            v = arena[:, at[0]:at[0] + n]
            at[0] += n
            return v

        def bf(*shape):
            n = int(np.prod(shape)) // 2
            v = arena[:, at[0]:at[0] + n].bitcast(BF16)
            at[0] += n
            return v

        def hi_lo(k):
            v = arena[:, k * HALF:(k + 1) * HALF].bitcast(BF16)
            return v[:, 0:HALF], v[:, HALF:2 * HALF]

        (wg_hi, wg_lo), (wu_hi, wu_lo), (wd_hi, wd_lo) = hi_lo(0), hi_lo(1), hi_lo(2)

        xall = f32(B, T).rearrange("p (b t) -> p b t", b=B)
        mk = f32(B, T).rearrange("p (b t) -> p b t", b=B)
        c_hi = bf(KT, TOK).rearrange("p (k t) -> p k t", k=KT)
        c_lo = bf(KT, TOK).rearrange("p (k t) -> p k t", k=KT)
        w0_hi, w0_lo = bf(WCOLS), bf(WCOLS)
        at_lookup = at[0]
        idx = f32(LW).bitcast(I32)
        bit = f32(2, 4, LW).bitcast(I32).rearrange("p (a n c) -> p a n c", a=2, n=4)
        pick = f32(2, LUT // 2, LW).rearrange("p (a n c) -> p a n c", a=2, n=LUT // 2)
        at[0] = at_lookup
        h_hi = bf(MT, CH).rearrange("p (m t) -> p m t", m=MT)
        h_lo = bf(MT, CH).rearrange("p (m t) -> p m t", m=MT)
        assert max(at[0], at_lookup + (9 + LUT) * LW) <= 3 * HALF

        def w0(w, which, kt, m):
            o = which * GCOLS + kt * INTER + m * P
            return w[:, o:o + P]

        def w0d(w, m):
            n = P if m < MT - 1 else MLAST
            o = 2 * GCOLS + m * T
            return w[0:n, o:o + T]

        SMALL = 5248
        small = sb("small", [P, SMALL])
        small_at = [0]

        def part(shape, dt=F32):
            n = int(np.prod(shape[1:])) * (1 if dt == F32 else 2) // (1 if dt == F32 else 4)
            v = small[:, small_at[0]:small_at[0] + n]
            small_at[0] += n
            assert small_at[0] <= SMALL
            if dt != F32:
                v = v.bitcast(dt)
            names = "abcd"[:len(shape) - 1]
            if len(names) == 1:
                return v
            return v.rearrange(f"p ({' '.join(names)}) -> p {' '.join(names)}", **dict(zip(names, shape[1:])))

        wq1 = sb("wq1", [P, P])
        wq3 = sb("wq3", [P, PAIRS, 2, 4, 16])
        wo1 = sb("wo1", [P, P])
        lutb = sb("lutb", [P, LUT])
        lutd = sb("lutd", [P, LUT // 2])
        absent_row = sb("absent_row", [1, P], BF16)
        nbig = sb("nbig", [P, KT, B])
        xs = part([P, 2, T])
        xm = part([P, 2, T])
        absent = part([P, 2, T], BF16)
        A = part([P, PAIRS * T], BF16)
        qs = part([P, 2, PAIRS * T], BF16)
        ks = part([P, 2, PAIRS * T], BF16)
        nmax = sb("nmax", [P, PAIRS, 2, KT])
        mcol = part([P, KT, PAIRS, P], BF16)
        probs = sb("probs", [P, 4, 1024])
        vu = sb("vu", [P, 2, KT, H0, HS])
        cq = part([P, 2 * T])
        cn = part([P, T])
        wst = sb("wst", [P, 3, FF])
        rden = sb("rden", [P, 2 * T // HS])
        cT = wst[:, 2, ROW:ROW + T]
        q32 = wst[:, 0, :]
        c_out = wst[:, 1, FF - T:FF]

        sil = wst[:, 0, :].rearrange("p (n t) -> p n t", n=2)
        hf = wst[:, 1, :].rearrange("p (n t) -> p n t", n=2)

        small_at[0] = 0
        wemb = sb("wemb", [P, KT, 2 * T])
        bemb = sb("bemb", [P, 4])
        gnorm = sb("gnorm", [P, KT])
        gcol = sb("gcol", [P, KT, B])
        scol = sb("scol", [P, KT, B])
        wqkv = sb("wqkv", [P, KT, 3 * T])
        gqk = sb("gqk", [P, 2, DK1])
        gg = sb("gg", [P, DK1])
        gb = sb("gb", [P, 1])
        w2 = sb("w2", [P, KT, T + E])
        w2T = sb("w2T", [P, KT, T])
        wr = sb("wr", [P, KT, E])
        br = sb("br", [P, E])
        sqx = sb("sqx", [P, T])
        ssq = sb("ssq", [P, B])
        rstd = sb("rstd", [P, B])
        newt = sb("newt", [P, 2 * H1])
        xr = part([P, T])
        xnT = part([P, KT, P])
        sq = part([P, 2 * T])
        ms = sb("ms", [P, 2 * H1])
        rs = sb("rs", [P, 2 * H1])
        qk_raw = part([P, 2, H1, DK1])
        qk = part([P, 2, H1, DK1])
        q4 = part([P, H1, 4, DK1], BF16)
        k4 = part([P, H1, 4, DK1], BF16)
        qT = part([P, 1024], BF16)
        kT = part([P, 1024], BF16)
        v1 = vu[:].rearrange("p a k h d -> p a (k h) d")
        rden1 = sb("rden1", [P, H1])
        cq1 = part([P, H1 * HS])
        cn1 = part([P, T])
        oT = part([P, KT, P])
        lg = sb("lg", [P, B, E])
        wz = sb("wz", [P, 1])

        lmx = sb("lmx", [P, B])
        oh = sb("oh", [P, B, E])
        taken = sb("taken", [P, B])
        ex = sb("ex", [P, B, E])
        es = sb("es", [P, B])
        tot = sb("tot", [P, E, B])
        run = sb("run", [P, E, B])
        cnt = sb("cnt", [P, E], I32)
        ntile = sb("ntile", [P, E])
        first = sb("first", [P, E])
        place = sb("place", [P, B, E])
        slotf = sb("slotf", [P, B])
        slot = sb("slot", [P, B], I32)
        tef = sb("tef", [P, SLOTS])
        te = sb("te", [P, SLOTS], I32)
        pad = wst[:, 2, 0:ROW]
        small_at[0] = 0
        xin = part([P, 2, T])
        xres = part([P, 2, ROW - T])
        gs, hh = probs[:, 0, :], probs[:, 1, :]
        hT_hi, hT_lo = (probs[:, 2, n * 512:(n + 1) * 512].bitcast(BF16) for n in range(2))
        xT_hi, xT_lo = (probs[:, 3, n * T:(n + 1) * T].bitcast(BF16).rearrange("p (n t) -> p n t", n=2) for n in range(2))
        yo = probs[:, 3, 512:1024].rearrange("p (n t) -> p n t", n=2)
        tokn = sb("tokn", [P, 2], I32)

        S = {}

        def new(*names):
            for n in names:
                S[n] = sem("s_" + n)

        new("x", "mk", "x_rest", "mk_rest", "cst", "ck", "wq", "lut", "small3", "wqkv", "idx", "pad", "scat", "ones", "init", "wq3", "kprep",
            "lutd", "bit", "entry", "pick", "w0h", "w0l",
            "xm", "xs0", "xs1", "absent", "pq", "a", "q32", "qk", "kh", "kk", "sa", "max", "mc", "mt", "q2", "st", "ex", "v", "vu", "ctx", "cq", "rd", "cn", "ct",
            "wo", "c", "ch", "cl",
            "g", "sil", "u", "hf", "hh", "hl", "dn", "x1",
            "w2a", "w2r", "w2", "emb", "gcol", "gg", "gb", "gmx",
            "ssq", "rstd", "nwx", "xr", "xt3", "xnT", "qkv", "sq", "raw", "mean", "ms", "nw", "qkn", "qg", "h4", "l4",
            "qT", "qTe", "kTe", "s3", "e3", "v1", "c3", "cq1", "rd3", "on", "oT", "t3", "te3", "lg",
            "wst0", "wst1", "wst2", "wsh0", "wsh1", "wsh2", "wsl0", "wsl1", "wsl2",
            "rv", "r", "rx", "rp", "tok", "te", "slot", "rows",
            "xld0", "xld1", "res0", "res1", "tT", "th", "tl", "gu", "gs", "uu", "hm", "hT", "hTh", "hTl", "y", "yo", "so0", "so1", "idn")

        def unless_first(engine, semaphore, count):
            if not (isinstance(count, int) and count <= 0):
                engine.wait_ge(semaphore, count)

        block = ctx.enter_context(nc.Block())
        LAST = B - 1
        U = B // 2

        @block.sync
        def _(sp):
            first, rest = slice(0, 2), slice(2, B)
            masks = cond.rearrange("(o b) t -> o b t", o=1).broadcast_to([P, B, T])
            sp.dma_start(xall[:, first], x[first].rearrange("b d t -> d b t")).then_inc(S["x"], 16)
            sp.dma_start(mk[:, first], masks[:, first]).then_inc(S["mk"], 16)
            sp.dma_start(wq1[:], wqT).then_inc(S["wq"], 16)
            sp.dma_start(cst[:], consts).then_inc(S["cst"], 16)
            sp.dma_start(wo1[:], woT).then_inc(S["wq"], 16)
            sp.dma_start(xall[:, rest], x[rest].rearrange("b d t -> d b t")).then_inc(S["x_rest"], 16)
            sp.dma_start(mk[:, rest], masks[:, rest]).then_inc(S["mk_rest"], 16)
            def load_x(b, par):
                sp.dma_start(xs[:, par, :], x[bass.ds(b, 1)].rearrange("b d t -> d (b t)")).then_inc(S[f"xs{par}"], 16)

            def load_index(i):
                sp.wait_ge(S["bit"], 4 * i)
                sp.dma_start(idx, idx_all[:, bass.ds(i * LW, LW)]).then_inc(S["idx"], 16)

            def load_next(i, par):
                load_index(i + 1)
                sp.wait_ge(S["v"], i)
                load_x(i + 1, 1 - par)

            sp.dma_start(idx, idx_all[:, 0:LW]).then_inc(S["idx"], 16)
            load_x(0, 0)
            load_x(1, 1)
            load_index(1)
            with sp.Fori(1, U) as u:
                load_next(2 * u - 1, 1)
                load_next(2 * u, 0)
            sp.wait_ge(S["x1"], B)
            sp.wait_ge(S["pad"], 16 * SLOTS)

            def weight_pieces(u):
                for n, w in enumerate((w_g, w_u, w_d)):
                    unless_first(sp, S[f"wsl{n}"], u)
                    sp.dma_start(wst[:, n, :], w[:, bass.ds(u * FF, FF)]).then_inc(S[f"wst{n}"], 16)
            weight_pieces(0)
            with sp.Fori(1, U) as u:
                weight_pieces(u)
            sp.wait_ge(S["scat"], 16 * B)
            def load_input(j):
                if j >= 2:
                    sp.wait_ge(S["tT"], j - 1)
                sp.dma_start(xin[:, j % 2, :], routed[j * P:(j + 1) * P, 0:T]).then_inc(S[f"xld{j % 2}"], 16)

            load_input(0)
            for j in range(SLOTS):
                if j + 1 < SLOTS:
                    load_input(j + 1)
                if j >= 2:
                    sp.wait_ge(S["yo"], j - 1)
                    sp.wait_ge(S["idn"], j - 1)
                sp.dma_start(xres[:, j % 2, :], routed[j * P:(j + 1) * P, T:ROW]).then_inc(S[f"res{j % 2}"], 16)

        @block.gpsimd
        def _(pool):
            nc.gpsimd.memset(ones[:], 1.0).then_inc(S["ones"], 1)
            nc.gpsimd.memset(wz[:], 0.0).then_inc(S["ones"], 1)
            nc.gpsimd.memset(pad, 0.0).then_inc(S["ones"], 1)
            nc.gpsimd.iota(rows[:, :, ROW - 1:ROW].bitcast(I32), pattern=[[P, B], [0, 1]], base=0,
                           channel_multiplier=1).then_inc(S["tok"], 1)
            pool.wait_ge(S["ones"], 3)
            nc.gpsimd.memset(pad[:, ROW - 1:ROW].bitcast(I32), DUMMY).then_inc(S["ones"], 1)

            def table_parts(c, par):
                pool.wait_ge(S["pick"], 3 * c + 3)
                o = bass.ds(c * LW, LW)
                nc.gpsimd.tensor_tensor(w0_hi[:, o], pick[:, par, 0, :], wz[:].broadcast_to([P, LW]), ALU.add).then_inc(S["w0h"], 1)
                pool.wait_ge(S["w0h"], c + 1)
                nc.gpsimd.tensor_tensor(w0_lo[:, o], pick[:, par, 0, :], w0_hi[:, o], ALU.subtract).then_inc(S["w0l"], 1)

            def context_parts(b):
                pool.wait_ge(S["c"], b + 1)
                o = bass.ds(b * P, P)
                c32 = c_out.rearrange("p (k t) -> p k t", k=KT)
                nc.gpsimd.tensor_tensor(c_hi[:, :, o], c32, wz[:].unsqueeze(2).broadcast_to([P, KT, P]), ALU.add
                                        ).then_inc(S["ch"], 1)
                pool.wait_ge(S["ch"], b + 1)
                nc.gpsimd.tensor_tensor(c_lo[:, :, o], c32, c_hi[:, :, o], ALU.subtract).then_inc(S["cl"], 1)

            def projected(b, par):
                nc.gpsimd.tensor_tensor(xm[:, par, :].unsqueeze(1), xall[:, bass.ds(b, 1), :], mk[:, bass.ds(b, 1), :],
                                        ALU.mult).then_inc(S["xm"], 1)
                nc.gpsimd.tensor_tensor(absent[0:1, par, :].unsqueeze(1), ones[0:1, 0:1].unsqueeze(1).broadcast_to([1, 1, T]),
                                        mk[0:1, bass.ds(b, 1), :], ALU.subtract).then_inc(S["xm"], 1)

            def keys(b, par, n):
                if n == 0 and not (isinstance(b, int) and b < 2):
                    pool.wait_ge(S["st"], 8 * (b - 1))
                o = slice(n * 512, (n + 1) * 512)
                pool.wait_ge(S["a"], 2 * b + n + 1)
                nc.gpsimd.tensor_tensor(ks[:, par, o], A[:, o], cst[:, C_SK:C_SK + 1].broadcast_to([P, 512]), ALU.mult
                                        ).then_inc(S["kh"], 1)
                pool.wait_ge(S["q32"], 2 * b + n + 1)
                pool.wait_ge(S["kh"], 2 * b + n + 1)
                nc.gpsimd.tensor_tensor(ks[:, par, o], ks[:, par, o], q32[:, o], ALU.add).then_inc(S["kk"], 1)

            def body(i, par, before=True, after=2):
                if after >= 2:
                    pool.wait_ge(S["pq"], 2 * i + 2)
                    projected(i + 2, par)
                if after >= 1:
                    keys(i + 1, 1 - par, 0)
                if before:
                    context_parts(i - 2)
                table_parts(i - 1, 1 - par)
                if after >= 1:
                    keys(i + 1, 1 - par, 1)

            pool.wait_ge(S["x"], 16)
            pool.wait_ge(S["mk"], 16)
            projected(0, 0)
            nc.gpsimd.memset(vu[:], 1.0).then_inc(S["ones"], 1)
            projected(1, 1)
            pool.wait_ge(S["cst"], 16)
            keys(0, 0, 0)
            keys(0, 0, 1)
            pool.wait_ge(S["x_rest"], 16)
            pool.wait_ge(S["mk_rest"], 16)
            projected(2, 0)
            keys(1, 1, 0)
            keys(1, 1, 1)
            body(1, 1, before=False)
            body(2, 0)
            with pool.Fori(1, U - 2) as u:
                body(2 * u + 1, 1)
                body(2 * u + 2, 0)
            body(LAST - 2, 1)
            body(LAST - 1, 0, after=1)
            body(LAST, 1, after=0)
            context_parts(LAST - 1)
            table_parts(LAST, 1)
            context_parts(LAST)

            pool.wait_ge(S["ones"], 5)
            for j in range(SLOTS):
                pool.dma_start(routed[j * P:(j + 1) * P, :], pad).then_inc(S["pad"], 16)

            def split(n, dst_hi, dst_lo, u):
                pool.wait_ge(S[f"wst{n}"], 16 * (u + 1))
                o = bass.ds(u * FF, FF)
                nc.gpsimd.tensor_tensor(dst_hi[:, o], wst[:, n, :], wz[:].broadcast_to([P, FF]), ALU.add).then_inc(S[f"wsh{n}"], 1)
                pool.wait_ge(S[f"wsh{n}"], u + 1)
                nc.gpsimd.tensor_tensor(dst_lo[:, o], wst[:, n, :], dst_hi[:, o], ALU.subtract).then_inc(S[f"wsl{n}"], 1)

            pool.wait_ge(S["x1"], B)
            with pool.Fori(0, U) as u:
                split(0, wg_hi, wg_lo, u)
                split(1, wu_hi, wu_lo, u)
                split(2, wd_hi, wd_lo, u)

            pool.wait_ge(S["pad"], 16 * SLOTS)
            pool.wait_ge(S["slot"], 1)
            pool.wait_ge(S["rows"], 1)
            pool.wait_ge(S["tok"], 1)
            for j in range(B):
                pool.indirect_dma_start(routed, bass.IndirectOffsetOnAxis(ap=slot[:, j:j + 1], axis=0),
                                        rows[:, j, :], None).then_inc(S["scat"], 16)
            for j in range(SLOTS):
                pool.wait_ge(S["yo"], j + 1)
                pool.wait_ge(S["idn"], j + 1)
                pool.indirect_dma_start(out, bass.IndirectOffsetOnAxis(ap=tokn[:, j % 2:j % 2 + 1], axis=0),
                                        yo[:, j % 2, :], None, bounds_check=TOK - 1,
                                        oob_is_err=False).then_inc(S[f"so{j % 2}"], 16)
            for j in range(2):
                pool.wait_ge(S[f"so{j}"], 16 * ((SLOTS - j + 1) // 2))

        @block.scalar
        def _(act):
            act.dma_start(ck[:], condT).then_inc(S["ck"], 16)
            act.dma_start(lutb[:], lut.broadcast_to([P, LUT])).then_inc(S["lut"], 16)
            for dst, src in ((wemb[:], w_emb.rearrange("(k p) n -> p k n", p=P)), (bemb[:], b_emb), (gnorm[:], g_norm),
                             (gqk[:, 0, :], g_q.broadcast_to([P, DK1])), (gqk[:, 1, :], g_k.broadcast_to([P, DK1])),
                             (w2[:, :, 0:T], w_out.rearrange("(k p) n -> p k n", p=P)),
                             (w2T[:], w_outT.rearrange("(k p) n -> p k n", p=P)),
                             (wr[:], w_r.rearrange("(k p) n -> p k n", p=P)), (br[:], b_r.broadcast_to([P, E]))):
                act.dma_start(dst, src).then_inc(S["small3"], 16)
            act.dma_start(wqkv[:], w_qkv.rearrange("(k p) n -> p k n", p=P)).then_inc(S["wqkv"], 16)

            def fixed():
                act.wait_ge(S["cst"], 16)

            fixed()

            def round_q(b, n):
                o = slice(n * 512, (n + 1) * 512)
                act.wait_ge(S["pq"], 2 * b + n + 1)
                unless_first(act, S["qk"], 2 * b)
                unless_first(act, S["kk"], 2 * b)
                nc.scalar.activation(A[:, o], PA[:, o], ACT.Identity, bias=cst[:, C_EV:C_EV + 1]).then_inc(S["a"], 1)
                nc.scalar.copy(q32[:, o], PA[:, o]).then_inc(S["q32"], 1)

            def values(b, par):
                act.wait_ge(S["v"], b + 1)
                if not (isinstance(b, int) and b < 2):
                    act.wait_ge(S["ctx"], b - 1)
                nc.scalar.copy(vu[:, par, :, :, 0:DK0], PD[:, 0:T].rearrange("p (k h d) -> p k h d", k=KT, h=H0)
                               ).then_inc(S["vu"], 1)

            def exps(b, c):
                unless_first(act, S["ctx"], b)
                for s in range(2):
                    act.wait_ge(S["st"], 8 * b + 2 * c + s + 1)
                    o = slice(s * 512, (s + 1) * 512)
                    nc.scalar.activation(probs[:, c, o], PC[:, o], ACT.Exp, scale=SCALE0).then_inc(S["ex"], 1)

            def context_out(b):
                act.wait_ge(S["wo"], b + 1)
                unless_first(act, S["cl"], b)
                nc.scalar.copy(c_out, PD[:, 512:512 + T]).then_inc(S["c"], 1)

            def entries(c, par, part):
                act.wait_ge(S["bit"], 4 * c + 4)
                if not (isinstance(c, int) and c < 2):
                    act.wait_ge(S["w0l"], c - 1)
                for j in range(2 * part, 2 * part + 2):
                    nc.scalar.activation(pick[:, par, j, :], bit[:, par, 0, :], ACT.Identity, scale=lutd[:, j:j + 1],
                                         bias=lutb[:, 2 * j:2 * j + 1]).then_inc(S["entry"], 1)

            act.wait_ge(S["ones"], 5)
            for b in range(2):
                for n in range(2):
                    round_q(b, n)
            act.wait_ge(S["lutd"], 1)
            act.wait_ge(S["lut"], 16)
            for part_ in range(4):
                entries(0, 0, part_)

            def body(i, par, before=True, after=True):
                exps(i - 1, 0)
                values(i - 1, 1 - par)
                entries(i, par, 0)
                exps(i - 1, 1)
                entries(i, par, 1)
                if after:
                    round_q(i + 1, 0)
                exps(i - 1, 2)
                if before:
                    context_out(i - 2)
                entries(i, par, 2)
                exps(i - 1, 3)
                if after:
                    round_q(i + 1, 1)
                entries(i, par, 3)

            body(1, 1, before=False)
            body(2, 0)
            with act.Fori(1, U - 1) as u:
                body(2 * u + 1, 1)
                body(2 * u + 2, 0)
            body(LAST, 1, after=False)
            exps(LAST, 0)
            values(LAST, 1)
            exps(LAST, 1)
            context_out(LAST - 1)
            exps(LAST, 2)
            exps(LAST, 3)
            context_out(LAST)

            def sum_squares(b):
                act.wait_ge(S["x1"], b + 1)
                unless_first(act, S["ssq"], b)
                fixed()
                nc.scalar.activation(sqx[:].unsqueeze(1), rows[:, bass.ds(b, 1), T:2 * T], ACT.Square,
                                     scale=T ** -0.5, accum_out=ssq[:, bass.ds(b, 1)]).then_inc(S["ssq"], 1)

            def gate_chunk(c, before=True):
                for m in range(MT):
                    if m == MT // 2 and before:
                        for t in range(TPC):
                            sum_squares(TPC * (c - 1) + t)
                    n = P if m < MT - 1 else MLAST
                    g = PA[0:n, (m % 2) * 512:(m % 2 + 1) * 512]
                    act.wait_ge(S["g"], MT * c + m + 1)
                    if m >= 2:
                        act.wait_ge(S["hf"], MT * c + m - 1)
                    else:
                        unless_first(act, S["hf"], MT * c)
                    nc.scalar.activation(sil[0:n, m % 2, :], g, ACT.Silu).then_inc(S["sil"], 1)
                    act.wait_ge(S["hf"], MT * c + m + 1)
                    unless_first(act, S["dn"], MT * c)
                    nc.scalar.copy(h_hi[0:n, m, :], hf[0:n, m % 2, :]).then_inc(S["hh"], 1)

            gate_chunk(0, before=False)
            with act.Fori(1, TOK // CH) as c:
                gate_chunk(c)
            for t in range(TPC):
                sum_squares(B - TPC + t)

            def scaled(b):
                unless_first(act, S["xt3"], b)
                fixed()
                nc.scalar.activation(xr.unsqueeze(1), rows[:, bass.ds(b, 1), T:2 * T], ACT.Copy, scale=rstd[:, bass.ds(b, 1)]
                                     ).then_inc(S["xr"], 1)

            def modulated(b):
                act.wait_ge(S["xt3"], b + 1)
                unless_first(act, S["qkv"], 2 * b)
                fixed()
                for kt in range(KT):
                    nc.scalar.activation(xnT[:, kt, :], PB[:, 512 + kt * P:512 + (kt + 1) * P], ACT.Identity,
                                         scale=gcol[:, kt, bass.ds(b, 1)], bias=scol[:, kt, bass.ds(b, 1)]).then_inc(S["xnT"], 1)

            def squares(b):
                act.wait_ge(S["qkv"], 2 * b + 1)
                unless_first(act, S["mean"], b)
                nc.scalar.activation(sq, PB[:, 0:512], ACT.Square, scale=DK1 ** -0.5).then_inc(S["sq"], 1)
                unless_first(act, S["qkn"], 2 * b)
                nc.scalar.copy(qk_raw.rearrange("p a h d -> p (a h d)"), PB[:, 0:512]).then_inc(S["raw"], 1)

            def values1(b, par):
                act.wait_ge(S["qkv"], 2 * b + 2)
                if not (isinstance(b, int) and b < 2):
                    act.wait_ge(S["c3"], b - 1)
                nc.scalar.copy(v1[:, par, :, 0:DK1], PB[:, 512:512 + T].rearrange("p (h d) -> p h d", h=H1)
                               ).then_inc(S["v1"], 1)

            def high_parts(b):
                act.wait_ge(S["qg"], b + 1)
                unless_first(act, S["qT"], 2 * b)
                unless_first(act, S["l4"], 2 * b)
                nc.scalar.copy(q4[:, :, 0:2, :], qk[:, 0].unsqueeze(2).broadcast_to([P, H1, 2, DK1])).then_inc(S["h4"], 1)
                act.wait_ge(S["qkn"], 2 * b + 2)
                nc.scalar.copy(k4[:, :, 0::2, :], qk[:, 1].unsqueeze(2).broadcast_to([P, H1, 2, DK1])).then_inc(S["h4"], 1)

            def exps1(b, par, c):
                act.wait_ge(S["s3"], 2 * b + c + 1)
                if not (isinstance(b, int) and b < 2):
                    act.wait_ge(S["c3"], b - 1)
                nc.scalar.activation(probs[:, 2 * par + c, :], PA[:], ACT.Exp, scale=DK1 ** -0.5, bias=gb[:]
                                     ).then_inc(S["e3"], 1)

            def qT_out(b):
                act.wait_ge(S["qT"], 2 * b + 1)
                unless_first(act, S["s3"], 2 * b)
                nc.scalar.copy(qT, PC[:, 0:512].bitcast(BF16)).then_inc(S["qTe"], 1)

            def result(b):
                act.wait_ge(S["t3"], b + 1)
                fixed()
                nc.scalar.copy(rows[:, bass.ds(b, 1), 0:T], PD[:, 512:512 + T].unsqueeze(1)).then_inc(S["te3"], 1)

            act.wait_ge(S["gb"], 1)
            act.wait_ge(S["gcol"], 6)
            act.wait_ge(S["rstd"], 2 + 3 * NEWTON)

            def body1(i, par, before=True, after=2):
                if before:
                    result(i - 2)
                if after:
                    squares(i + 1)
                qT_out(i)
                if after >= 2:
                    scaled(i + 2)
                exps1(i, par, 0)
                if after:
                    values1(i + 1, 1 - par)
                if after >= 2:
                    modulated(i + 2)
                exps1(i, par, 1)
                if after:
                    high_parts(i + 1)

            scaled(0)
            modulated(0)
            scaled(1)
            squares(0)
            values1(0, 0)
            modulated(1)
            high_parts(0)
            body1(0, 0, before=False)
            body1(1, 1, before=False)
            with act.Fori(1, U - 1) as u:
                body1(2 * u, 0)
                body1(2 * u + 1, 1)
            body1(LAST - 1, 0, after=1)
            body1(LAST, 1, after=0)
            result(LAST - 1)
            result(LAST)

            act.wait_ge(S["rx"], 1)
            nc.scalar.activation(ex[:], ex[:], ACT.Exp).then_inc(S["rx"], 1)

            def x_high(j, par):
                act.wait_ge(S["tT"], j + 1)
                nc.scalar.copy(xT_hi[:, par, :], PD[:, 0:T]).then_inc(S["th"], 1)

            def gate(j):
                act.wait_ge(S["gu"], j + 1)
                unless_first(act, S["hm"], j)
                nc.scalar.activation(gs, PA[:], ACT.Silu).then_inc(S["gs"], 1)

            def h_high(j):
                act.wait_ge(S["hT"], j + 1)
                unless_first(act, S["y"], j)
                nc.scalar.copy(hT_hi, PC[:]).then_inc(S["hTh"], 1)

            def tile(j, par, more=True):
                h_high(j - 1)
                gate(j)
                if more:
                    x_high(j + 1, 1 - par)

            x_high(0, 0)
            gate(0)
            x_high(1, 1)
            tile(1, 1)
            tile(2, 0)
            with act.Fori(1, (SLOTS - 2) // 2) as u:
                tile(2 * u + 1, 1)
                tile(2 * u + 2, 0)
            for j in range(SLOTS - 2 + (SLOTS % 2 == 0), SLOTS):
                tile(j, j % 2, j + 1 < SLOTS)
            h_high(SLOTS - 1)

        @block.tensor
        def _(pe):
            mm = nc.tensor.matmul
            pe.wait_ge(S["wq3"], 4)
            pe.wait_ge(S["cst"], 16)
            pe.wait_ge(S["init"], 2)
            pe.wait_ge(S["absent"], 2)
            pe.wait_ge(S["ones"], 5)
            pe.wait_ge(S["wq"], 32)

            def project(b, par, pr):
                if pr == 0:
                    pe.wait_ge(S["xm"], 2 * b + 2)
                    unless_first(pe, S["q32"], 2 * b)
                mm(PA[:, pr * T:(pr + 1) * T], wq3[:, pr].rearrange("p a b c -> p (a b c)"), xm[:, par, :], start=True, stop=False)
                ins = mm(PA[:, pr * T:(pr + 1) * T], absent_row[:], absent[0:1, par, :], start=False, stop=True)
                if pr % 2:
                    ins.then_inc(S["pq"], 1)

            def project_v(b, par, half):
                pe.wait_ge(S[f"xs{par}"], 16 * (half + 1))
                unless_first(pe, S["cq"], b)
                for kt in range(KT):
                    ins = mm(PD[:, kt * P:(kt + 1) * P], xs[:, par, kt * P:(kt + 1) * P], wq1[:], start=True, stop=True)
                ins.then_inc(S["v"], 1)

            def scores(b, par, c, s):
                pe.wait_ge(S["qk"], 2 * b + 1 + c // 2)
                pe.wait_ge(S["kk"], 2 * b + 1 + c // 2)
                unless_first(pe, S["max"], 8 * b + 2 * c + s - 1)
                r = slice(64 * s, 64 * s + 64)
                for qt in range(KT):
                    ins = mm(PB[:, s * 512 + qt * T:s * 512 + (qt + 1) * T],
                             qs[r, par, c * T + qt * P:c * T + (qt + 1) * P], ks[r, par, c * T:(c + 1) * T],
                             start=True, stop=True)
                ins.then_inc(S["sa"], 1)

            def scores_T(b, par, c, s):
                pp, kt = c // KT, c % KT
                pe.wait_ge(S["q2"], b + 1)
                unless_first(pe, S["ex"], 8 * b + 2 * c + s - 1)
                r = slice(64 * s, 64 * s + 64)
                for n in range(2):
                    pr = 2 * pp + n
                    ins = mm(PC[:, s * 512 + n * T:s * 512 + (n + 1) * T],
                             ks[r, par, pr * T + kt * P:pr * T + (kt + 1) * P], qs[r, par, pr * T:(pr + 1) * T],
                             start=True, stop=True)
                ins.then_inc(S["st"], 1)

            def contexts(b, par):
                pe.wait_ge(S["vu"], b + 1)
                pe.wait_ge(S["ex"], 8 * b + 8)
                for s in range(2):
                    for kt in range(KT):
                        for pr in range(PAIRS):
                            o = s * 512 + (pr % 2) * T
                            ins = mm(PD[pr * HS:(pr + 1) * HS, s * T:(s + 1) * T], vu[:, par, kt, 2 * pr + s, :],
                                     probs[:, (pr // 2) * KT + kt, o:o + T], start=(kt == 0), stop=(kt == KT - 1))
                ins.then_inc(S["ctx"], 1)

            def max_rows(b):
                pe.wait_ge(S["mc"], 3 * b + 3)
                if not (isinstance(b, int) and b < 2):
                    pe.wait_ge(S["c"], b - 1)
                M = PD[:, 512:1024].bitcast(BF16)
                for pr in range(PAIRS):
                    for qt in range(KT):
                        ins = pe.transpose(M[:, pr * T + qt * P:pr * T + (qt + 1) * P], mcol[:, qt, pr, :], identb[:])
                ins.then_inc(S["mt"], 1)

            def outputs0(b):
                pe.wait_ge(S["ct"], b + 1)
                pe.wait_ge(S["q2"], min(b + 2, B) if isinstance(b, int) else b + 2)
                if isinstance(b, int) and b == LAST:
                    pe.wait_ge(S["c"], LAST)
                for qt in range(KT):
                    ins = mm(PD[:, 512 + qt * P:512 + (qt + 1) * P], cT[:, qt * P:(qt + 1) * P], wo1[:], start=True, stop=True)
                ins.then_inc(S["wo"], 1)

            for pr in range(PAIRS):
                project(0, 0, pr)
            for c in range(4):
                for s in range(2):
                    scores(0, 0, c, s)
                project(1, 1, c)
            max_rows(0)

            def body(i, par, half, before=True, after=True):
                for c in range(4):
                    for s in range(2):
                        scores(i, par, c, s)
                        scores_T(i - 1, 1 - par, c, s)
                    if after:
                        project(i + 1, 1 - par, c)
                    if c == 0:
                        project_v(i - 1, 1 - par, half)
                    if c == 2 and before:
                        outputs0(i - 2)
                max_rows(i)
                contexts(i - 1, 1 - par)

            body(1, 1, 0, before=False)
            body(2, 0, 0)
            with pe.Fori(1, U - 1) as u:
                body(2 * u + 1, 1, u)
                body(2 * u + 2, 0, u)
            body(LAST, 1, U - 1, after=False)
            for c in range(4):
                for s in range(2):
                    scores_T(LAST, 1, c, s)
                if c == 0:
                    project_v(LAST, 1, U - 1)
                if c == 1:
                    outputs0(LAST - 1)
            contexts(LAST, 1)

            def norm_and_router():
                pe.wait_ge(S["small3"], 16 * 9)
                pe.wait_ge(S["ck"], 16)
                pe.wait_ge(S["ex"], 8 * B)
                for m in range(4):
                    for kt in range(KT):
                        ins = mm(PC[:, m * B:(m + 1) * B], wemb[:, kt, m * P:(m + 1) * P], ck[:, kt, :],
                                 start=(kt == 0), stop=(kt == KT - 1))
                ins.then_inc(S["emb"], 1)
                pe.wait_ge(S["w2a"], 2 * KT)
                for m in range(KT):
                    for kt in range(KT):
                        ins = mm(PC[:, 512 + m * E:512 + (m + 1) * E], w2T[:, kt, m * P:(m + 1) * P], wr[:, kt, :],
                                 start=(kt == 0), stop=(kt == KT - 1))
                ins.then_inc(S["w2r"], 1)

            pe.wait_ge(S["w0h"], -(-2 * GCOLS // LW))
            pe.wait_ge(S["w0l"], -(-2 * GCOLS // LW))

            def chunk(c):
                pe.wait_ge(S["ch"], TPC * c + TPC)
                pe.wait_ge(S["cl"], TPC * c + TPC)
                tok = bass.ds(c * CH, CH)

                def up(m):
                    for which, bank, done in ((0, PA, "g"), (1, PB, "u")):
                        unless_first(pe, S["hf"], MT * c + max(m - 1, 0))
                        o = bank[:, (m % 2) * 512:(m % 2 + 1) * 512]
                        k = 0
                        for kt in range(KT):
                            for w, v in ((w0_hi, c_hi), (w0_hi, c_lo), (w0_lo, c_hi)):
                                ins = mm(o, w0(w, which, kt, m), v[:, kt, tok], start=(k == 0), stop=(k == 3 * KT - 1))
                                k += 1
                        ins.then_inc(S[done], 1)

                def down(m):
                    n = P if m < MT - 1 else MLAST
                    pe.wait_ge(S["hl"], MT * c + m + 1)
                    if m == 0 and isinstance(c, int):
                        pe.wait_ge(S["w0h"], LCH)
                        pe.wait_ge(S["w0l"], LCH)
                        pe.wait_ge(S["c"], B)
                        pe.wait_ge(S["gcol"], 4)
                        pe.wait_ge(S["w2"], 1)
                    elif m == 0:
                        pe.wait_ge(S["x1"], TPC * c)
                    for t in range(TPC):
                        o = (PC, PD)[t // 2][:, (t % 2) * 512:(t % 2) * 512 + T]
                        for k, (v, w) in enumerate(((h_hi, w0_hi), (h_hi, w0_lo), (h_lo, w0_hi))):
                            ins = mm(o, v[0:n, m, t * P:(t + 1) * P], w0d(w, m), start=(m == 0 and k == 0),
                                     stop=(m == MT - 1 and k == 2))
                    ins.then_inc(S["dn"], 1)

                up(0)
                if isinstance(c, int):
                    outputs0(LAST)
                    norm_and_router()
                for m in range(1, MT):
                    up(m)
                    down(m - 1)
                down(MT - 1)

            chunk(0)
            with pe.Fori(1, TOK // CH) as c:
                chunk(c)

            pe.wait_ge(S["w2"], 1)
            pe.wait_ge(S["wqkv"], 16)

            def turn_x(b):
                pe.wait_ge(S["xr"], b + 1)
                unless_first(pe, S["v1"], b)
                for kt in range(KT):
                    ins = pe.transpose(PB[:, 512 + kt * P:512 + (kt + 1) * P], xr[:, kt * P:(kt + 1) * P], ident)
                ins.then_inc(S["xt3"], 1)

            def queries_keys(b):
                pe.wait_ge(S["xnT"], 2 * b + 2)
                unless_first(pe, S["raw"], b)
                for kt in range(KT):
                    ins = mm(PB[:, 0:512], xnT[:, kt, :], wqkv[:, kt, 0:512], start=(kt == 0), stop=(kt == KT - 1))
                ins.then_inc(S["qkv"], 1)

            def values1(b):
                pe.wait_ge(S["xnT"], 2 * b + 2)
                for kt in range(KT):
                    ins = mm(PB[:, 512:512 + T], xnT[:, kt, :], wqkv[:, kt, 512:768], start=(kt == 0), stop=(kt == KT - 1))
                ins.then_inc(S["qkv"], 1)

            def turn(b):
                for n, (src, done) in enumerate(((q4, "qTe"), (k4, "kTe"))):
                    pe.wait_ge(S["l4"], 2 * b + n + 1)
                    unless_first(pe, S[done], b)
                    bank = PC[:, n * 512:(n + 1) * 512].bitcast(BF16)
                    for pr in range(H1 // 2):
                        ins = pe.transpose(bank[:, pr * P:(pr + 1) * P],
                                           src[:, 2 * pr:2 * pr + 2].rearrange("p h s d -> p (h s d)"), identb[:])
                    ins.then_inc(S["qT"], 1)

            def scores1(b, c):
                pe.wait_ge(S["qTe"], b + 1)
                pe.wait_ge(S["kTe"], b + 1)
                unless_first(pe, S["e3"], 2 * b + c)
                for s in range(2):
                    r = slice(64 * s, 64 * s + 64)
                    for n in range(4):
                        pr = 4 * c + n
                        ins = mm(PA[:, s * 512 + n * P:s * 512 + (n + 1) * P], kT[r, pr * P:(pr + 1) * P],
                                 qT[r, pr * P:(pr + 1) * P], start=True, stop=True)
                ins.then_inc(S["s3"], 1)

            def contexts1(b, par):
                pe.wait_ge(S["v1"], b + 1)
                unless_first(pe, S["cq1"], b)
                pe.wait_ge(S["e3"], 2 * b + 2)
                for c in range(2):
                    for s in range(2):
                        for n in range(GROUP):
                            o = s * 512 + n * P
                            ins = mm(PD[n * HS:(n + 1) * HS, (2 * s + c) * P:(2 * s + c + 1) * P],
                                     v1[:, par, 8 * c + 2 * n + s, :], probs[:, 2 * par + c, o:o + P], start=True, stop=True)
                ins.then_inc(S["c3"], 1)

            def outputs(b):
                pe.wait_ge(S["oT"], b + 1)
                unless_first(pe, S["lg"], b)
                unless_first(pe, S["te3"], b)
                for kt in range(KT):
                    ins = mm(PD[:, 512:512 + T + E], oT[:, kt, :], w2[:, kt, :], start=(kt == 0), stop=(kt == KT - 1))
                ins.then_inc(S["t3"], 1)

            def body1(i, par, before=True, after=2):
                if after >= 1:
                    queries_keys(i + 1)
                turn(i)
                if before:
                    contexts1(i - 1, 1 - par)
                scores1(i, 0)
                if after >= 1:
                    values1(i + 1)
                if after >= 2:
                    turn_x(i + 2)
                scores1(i, 1)
                if before:
                    outputs(i - 1)

            turn_x(0)
            queries_keys(0)
            values1(0)
            turn_x(1)
            body1(0, 0, before=False)
            body1(1, 1)
            with pe.Fori(1, U - 1) as u:
                body1(2 * u, 0)
                body1(2 * u + 1, 1)
            body1(LAST - 1, 0, after=1)
            body1(LAST, 1, after=0)
            contexts1(LAST, 1)
            outputs(LAST)

            pe.wait_ge(S["r"], 1)
            flat = oh[:].rearrange("p b e -> p (b e)")
            mm(PA[:, 0:B * E], cst[:, C_TRI:C_TRI + P], flat, start=True, stop=True)
            mm(PB[:, 0:B * E], ones[:], flat, start=True, stop=True).then_inc(S["rp"], 1)

            for n in range(3):
                pe.wait_ge(S[f"wsl{n}"], U)
            pe.wait_ge(S["te"], 1)

            def tile_in(j, half, par):
                pe.wait_ge(S[f"xld{par}"], 16 * (half + 1))
                unless_first(pe, S["tl"], j)
                for kt in range(KT):
                    ins = pe.transpose(PD[:, kt * P:(kt + 1) * P], xin[:, par, kt * P:(kt + 1) * P], ident)
                ins.then_inc(S["tT"], 1)

            def gate_up(j, par, e, bank, w_hi, w_lo, free, done):
                pe.wait_ge(S["tl"], j + 1)
                unless_first(pe, S[free], j)
                for n in range(2):
                    k = 0
                    for kt in range(KT):
                        o = bass.ds(e * (KT * FF) + (kt * FF + n * 512), 512)
                        xo = slice(kt * P, (kt + 1) * P)
                        for v, w in ((xT_hi, w_hi), (xT_hi, w_lo), (xT_lo, w_hi)):
                            ins = mm(bank[:, n * 512:(n + 1) * 512], v[:, par, xo], w[:, o], start=(k == 0), stop=(k == 3 * KT - 1))
                            k += 1
                ins.then_inc(S[done], 1)

            def turn_h(j):
                pe.wait_ge(S["hm"], j + 1)
                unless_first(pe, S["hTl"], j)
                for f in range(FT):
                    ins = pe.transpose(PC[:, f * P:(f + 1) * P], hh[:, f * P:(f + 1) * P], ident)
                ins.then_inc(S["hT"], 1)

            def down(j, e):
                pe.wait_ge(S["hTh"], j + 1)
                pe.wait_ge(S["hTl"], j + 1)
                unless_first(pe, S["yo"], j)
                k = 0
                for f in range(FT):
                    o = bass.ds(e * (FT * T) + f * T, T)
                    for v, w in ((hT_hi, wd_hi), (hT_hi, wd_lo), (hT_lo, wd_hi)):
                        ins = mm(PD[:, 512:512 + T], v[:, f * P:(f + 1) * P], w[:, o], start=(k == 0), stop=(k == 3 * FT - 1))
                        k += 1
                ins.then_inc(S["y"], 1)

            def expert_of(j):
                return pe.value_load(te[0:1, bass.ds(j, 1)], min_val=0, max_val=E - 1)

            def tile(j, half, par, more=True):
                gate_up(j, par, expert_of(j), PA, wg_hi, wg_lo, "gs", "gu")
                turn_h(j - 1)
                gate_up(j, par, expert_of(j), PB, wu_hi, wu_lo, "hm", "uu")
                if more:
                    tile_in(j + 1, half + par, 1 - par)
                down(j - 1, expert_of(j - 1))

            tile_in(0, 0, 0)
            gate_up(0, 0, expert_of(0), PA, wg_hi, wg_lo, "gs", "gu")
            gate_up(0, 0, expert_of(0), PB, wu_hi, wu_lo, "hm", "uu")
            tile_in(1, 0, 1)
            tile(1, 0, 1)
            tile(2, 1, 0)
            with pe.Fori(1, (SLOTS - 2) // 2) as u:
                tile(2 * u + 1, u, 1)
                tile(2 * u + 2, u + 1, 0)
            for j in range(SLOTS - 2 + (SLOTS % 2 == 0), SLOTS):
                tile(j, j // 2, j % 2, j + 1 < SLOTS)
            turn_h(SLOTS - 1)
            down(SLOTS - 1, expert_of(SLOTS - 1))

        @block.vector
        def _(dve):
            v = nc.vector
            v.memset(wq3[:], 0.0).then_inc(S["wq3"], 1)
            v.memset(absent_row[:], 0.0).then_inc(S["absent"], 1)
            v.memset(mcol, 0.0).then_inc(S["init"], 1)
            dve.wait_ge(S["absent"], 1)
            v.memset(absent_row[:, 50::64], 1.0).then_inc(S["absent"], 1)
            dve.wait_ge(S["wq"], 32)
            dve.wait_ge(S["wq3"], 1)
            for s in range(3):
                v.tensor_copy(wq3[:, :, :, s, :], wq1[:].rearrange("p (r a d) -> p r a d", r=PAIRS, a=2)).then_inc(S["wq3"], 1)
            dve.wait_ge(S["cst"], 16)
            v.tensor_copy(identb[:], ident).then_inc(S["init"], 1)
            dve.wait_ge(S["ck"], 16)
            v.tensor_scalar(nbig[:], ck[:], -NEG, None, ALU.mult).then_inc(S["kprep"], 1)
            dve.wait_ge(S["lut"], 16)
            pairs = lutb[:].rearrange("p (j t) -> p j t", t=2)
            v.tensor_tensor(lutd[:], pairs[:, :, 1], pairs[:, :, 0], ALU.subtract).then_inc(S["lutd"], 1)
            dve.wait_ge(S["kprep"], 1)

            def bits(c, par):
                dve.wait_ge(S["idx"], 16 * c + 16)
                if not (isinstance(c, int) and c < 2):
                    dve.wait_ge(S["pick"], 3 * (c - 1))
                    dve.wait_ge(S["entry"], 8 * (c - 1))
                for n in range(4):
                    v.tensor_scalar(bit[:, par, n, :], idx, 1 << n, None, ALU.bitwise_and).then_inc(S["bit"], 1)

            def select(par, n):
                step = 1 << n
                k = (LUT // 2) // step
                tree = pick[:, par].rearrange("p (k s) c -> p k s c", k=k)
                v.copy_predicated(tree[:, :, 0, :], bit[:, par, n, :].unsqueeze(1).broadcast_to([P, k, LW]),
                                  tree[:, :, step // 2, :]).then_inc(S["pick"], 1)

            def stack(b, par):
                if not (isinstance(b, int) and b < 2):
                    dve.wait_ge(S["st"], 8 * (b - 1))
                for n in range(2):
                    dve.wait_ge(S["q32"], 2 * b + n + 1)
                    o = slice(n * 512, (n + 1) * 512)
                    v.scalar_tensor_tensor(out=qs[:, par, o], in0=A[:, o], scalar=cst[:, C_SQ:C_SQ + 1], in1=q32[:, o],
                                           op0=ALU.mult, op1=ALU.add).then_inc(S["qk"], 1)

            def maxima(b, piece=None, par=0, before=False):
                for c in range(4):
                    for s in range(2):
                        if piece is not None and s == 1:
                            if c == 0:
                                dve.wait_ge(S["entry"], 8 * piece + 8)
                            elif c < 3:
                                dve.wait_ge(S["pick"], 3 * piece + c)
                        dve.wait_ge(S["sa"], 8 * b + 2 * c + s + 1)
                        if c == s == 0:
                            unless_first(dve, S["mc"], 3 * b)
                        v.tensor_reduce(nmax[:, c, s, :], PB[:, s * 512:(s + 1) * 512].rearrange("p (a k) -> p a k", k=T),
                                        AX.X, ALU.max, negate=True).then_inc(S["max"], 1)
                        if before and 2 * c + s < 3:
                            normalise(b - 2, 2 * c + s + 1)
                    if piece is not None and c < 3:
                        select(par, c + 1)
                dve.wait_ge(S["max"], 8 * b + 8)
                unless_first(dve, S["mt"], b)
                cols = mcol.rearrange("p q r (s m) -> p r s q m", s=2)
                v.tensor_copy(cols[:, :, :, :, 48], nmax[:]).then_inc(S["mc"], 1)
                dve.wait_ge(S["mc"], 3 * b + 1)
                v.tensor_tensor(cols[:, :, :, :, 49], nmax[:], cols[:, :, :, :, 48], ALU.subtract).then_inc(S["mc"], 1)
                v.tensor_copy(mcol[:, :, :, 50::64].rearrange("p q r s -> p q (r s)"),
                              nbig[:, :, bass.ds(b, 1)].broadcast_to([P, KT, 2 * PAIRS])).then_inc(S["mc"], 1)

            def add_max(b, par):
                dve.wait_ge(S["mt"], b + 1)
                v.tensor_tensor(qs[:, par, :], PD[:, 512:1024].bitcast(BF16), qs[:, par, :], ALU.add).then_inc(S["q2"], 1)

            def normalise(b, step):
                if step == 0:
                    dve.wait_ge(S["ctx"], b + 1)
                    v.transpose(cq, PD[:, 0:2 * T]).then_inc(S["cq"], 1)
                elif step == 1:
                    dve.wait_ge(S["cq"], b + 1)
                    v.reciprocal(rden[:], cq.rearrange("p (n d) -> p n d", d=HS)[:, :, DK0]).then_inc(S["rd"], 1)
                elif step == 2:
                    dve.wait_ge(S["rd"], b + 1)
                    v.tensor_tensor(cn.rearrange("p (n s d) -> p s n d", s=2, d=DK0),
                                    cq.rearrange("p (s n d) -> p s n d", s=2, d=HS)[:, :, :, 0:DK0],
                                    rden[:].rearrange("p (s n) -> p s n", s=2).unsqueeze(3).broadcast_to([P, 2, T // HS, DK0]),
                                    ALU.mult).then_inc(S["cn"], 1)
                else:
                    dve.wait_ge(S["cn"], b + 1)
                    unless_first(dve, S["wo"], b)
                    v.transpose(cT, cn).then_inc(S["ct"], 1)

            def body(i, par, before=True, after=True):
                if before:
                    normalise(i - 2, 0)
                maxima(i, i - 1, 1 - par, before)
                if after:
                    bits(i + 1, 1 - par)
                    stack(i + 1, 1 - par)
                add_max(i, par)

            stack(0, 0)
            bits(0, 0)
            maxima(0)
            stack(1, 1)
            bits(1, 1)
            add_max(0, 0)
            body(1, 1, before=False)
            body(2, 0)
            with dve.Fori(1, U - 1) as u:
                body(2 * u + 1, 1)
                body(2 * u + 2, 0)
            body(LAST, 1, after=False)
            for n in range(4):
                normalise(LAST - 1, n)
            dve.wait_ge(S["entry"], 8 * B)
            for n in range(1, 4):
                if n > 1:
                    dve.wait_ge(S["pick"], 3 * LAST + n - 1)
                select(1, n)
            for n in range(4):
                normalise(LAST, n)

            dve.wait_ge(S["small3"], 16 * 9)
            for kt in range(KT):
                v.tensor_tensor(w2[:, kt, kt * P:(kt + 1) * P], w2[:, kt, kt * P:(kt + 1) * P], ident, ALU.add
                                ).then_inc(S["w2a"], 1)
                v.tensor_tensor(w2T[:, kt, kt * P:(kt + 1) * P], w2T[:, kt, kt * P:(kt + 1) * P], ident, ALU.add
                                ).then_inc(S["w2a"], 1)
            v.tensor_tensor(gg[:], gqk[:, 0], gqk[:, 1], ALU.mult).then_inc(S["gg"], 1)
            dve.wait_ge(S["gg"], 1)
            v.tensor_reduce(gb[:], gg[:], AX.X, ALU.max, apply_absolute_value=True).then_inc(S["gmx"], 1)
            dve.wait_ge(S["gmx"], 1)
            v.tensor_scalar(gb[:], gb[:], -(DK1 ** 0.5), None, ALU.mult).then_inc(S["gb"], 1)
            dve.wait_ge(S["emb"], 1)
            for kt in range(KT):
                v.tensor_scalar(gcol[:, kt, :], PC[:, kt * B:(kt + 1) * B], bemb[:, kt:kt + 1], 1.0, ALU.add, ALU.add
                                ).then_inc(S["gcol"], 1)
                v.tensor_scalar(scol[:, kt, :], PC[:, (KT + kt) * B:(KT + kt + 1) * B], bemb[:, KT + kt:KT + kt + 1], None,
                                ALU.add).then_inc(S["gcol"], 1)
            dve.wait_ge(S["gcol"], 4)
            for kt in range(KT):
                v.tensor_scalar(gcol[:, kt, :], gcol[:, kt, :], gnorm[:, kt:kt + 1], None, ALU.mult).then_inc(S["gcol"], 1)
            dve.wait_ge(S["w2r"], 1)
            v.tensor_copy(w2[:, :, T:T + E], PC[:, 512:512 + KT * E].rearrange("p (k e) -> p k e", k=KT)).then_inc(S["w2"], 1)
            dve.wait_ge(S["gcol"], 6)

            def hidden_chunk(c):
                for m in range(MT):
                    n = P if m < MT - 1 else MLAST
                    k = MT * c + m
                    if isinstance(c, int) and m == 1:
                        dve.wait_ge(S["cl"], B)
                    dve.wait_ge(S["sil"], k + 1)
                    dve.wait_ge(S["u"], k + 1)
                    unless_first(dve, S["hl"], k if m == 0 else k - 1)
                    v.tensor_tensor(hf[0:n, m % 2, :], PB[0:n, (m % 2) * 512:(m % 2 + 1) * 512], sil[0:n, m % 2, :],
                                    ALU.mult).then_inc(S["hf"], 1)
                    dve.wait_ge(S["hh"], k + 1)
                    v.tensor_tensor(h_lo[0:n, m, :], hf[0:n, m % 2, :], h_hi[0:n, m, :], ALU.subtract).then_inc(S["hl"], 1)
                dve.wait_ge(S["dn"], MT * c + MT)
                for t in range(TPC):
                    b = TPC * c + t
                    v.tensor_tensor(rows[:, bass.ds(b, 1), T:2 * T],
                                    (PC, PD)[t // 2][:, (t % 2) * 512:(t % 2) * 512 + T].unsqueeze(1),
                                    xall[:, bass.ds(b, 1), :], ALU.add).then_inc(S["x1"], 1)

            hidden_chunk(0)
            with dve.Fori(1, TOK // CH) as c:
                hidden_chunk(c)

            def guess(y, x):
                return v.tensor_scalar(y.bitcast(I32), x.bitcast(I32), 1, None, ALU.arith_shift_right)

            def guess_end(y):
                return v.tensor_scalar(y.bitcast(I32), y.bitcast(I32), -1.0, float(RSQRT), ALU.mult, ALU.add)

            def square(t, y):
                return v.scalar_tensor_tensor(out=t, in0=y, scalar=-0.5, in1=y, op0=ALU.mult, op1=ALU.mult)

            def times(t, x):
                return v.tensor_tensor(t, t, x, ALU.mult)

            def better(y, t):
                return v.scalar_tensor_tensor(out=y, in0=t, scalar=1.5, in1=y, op0=ALU.add, op1=ALU.mult)

            dve.wait_ge(S["ssq"], B)
            v.tensor_scalar(ssq[:], ssq[:], EPS, None, ALU.add).then_inc(S["nwx"], 1)
            dve.wait_ge(S["nwx"], 1)
            guess(rstd[:], ssq[:]).then_inc(S["rstd"], 1)
            dve.wait_ge(S["rstd"], 1)
            guess_end(rstd[:]).then_inc(S["rstd"], 1)
            for n in range(NEWTON):
                dve.wait_ge(S["rstd"], 3 * n + 2)
                square(newt[:, 0:B], rstd[:]).then_inc(S["rstd"], 1)
                dve.wait_ge(S["rstd"], 3 * n + 3)
                times(newt[:, 0:B], ssq[:]).then_inc(S["rstd"], 1)
                dve.wait_ge(S["rstd"], 3 * n + 4)
                better(rstd[:], newt[:, 0:B]).then_inc(S["rstd"], 1)
            dve.wait_ge(S["rstd"], 2 + 3 * NEWTON)

            def kT_out(b):
                dve.wait_ge(S["qT"], 2 * b + 2)
                unless_first(dve, S["s3"], 2 * b)
                v.tensor_copy(kT, PC[:, 512:1024].bitcast(BF16)).then_inc(S["kTe"], 1)

            STEPS = 2 + 3 * NEWTON

            def mean_squares(b):
                dve.wait_ge(S["sq"], b + 1)
                v.tensor_reduce(ms[:], sq.rearrange("p (h d) -> p h d", d=DK1), AX.X, ALU.add).then_inc(S["mean"], 1)
                dve.wait_ge(S["mean"], b + 1)
                v.tensor_scalar(ms[:], ms[:], EPS, None, ALU.add).then_inc(S["ms"], 1)

            def factors(b, k):
                if k == 0:
                    dve.wait_ge(S["ms"], b + 1)
                else:
                    dve.wait_ge(S["nw"], STEPS * b + k)
                if k == 0:
                    step = guess(rs[:], ms[:])
                elif k == 1:
                    step = guess_end(rs[:])
                elif k % 3 == 2:
                    step = square(newt[:], rs[:])
                elif k % 3 == 0:
                    step = times(newt[:], ms[:])
                else:
                    step = better(rs[:], newt[:])
                step.then_inc(S["nw"], 1)

            def scaled_qk(b):
                dve.wait_ge(S["raw"], b + 1)
                dve.wait_ge(S["nw"], STEPS * b + STEPS)
                unless_first(dve, S["h4"], 2 * b)
                unless_first(dve, S["l4"], 2 * b)
                for n in range(2):
                    v.tensor_tensor(qk[:, n], qk_raw[:, n],
                                    rs[:, n * H1:(n + 1) * H1].unsqueeze(2).broadcast_to([P, H1, DK1]), ALU.mult
                                    ).then_inc(S["qkn"], 1)
                dve.wait_ge(S["qkn"], 2 * b + 1)
                v.tensor_tensor(qk[:, 0], qk[:, 0], gg[:].unsqueeze(1).broadcast_to([P, H1, DK1]), ALU.mult
                                ).then_inc(S["qg"], 1)

            def low_parts(b):
                dve.wait_ge(S["h4"], 2 * b + 1)
                v.tensor_tensor(q4[:, :, 2:4, :], qk[:, 0].unsqueeze(2).broadcast_to([P, H1, 2, DK1]), q4[:, :, 0:2, :],
                                ALU.subtract).then_inc(S["l4"], 1)
                dve.wait_ge(S["h4"], 2 * b + 2)
                v.tensor_tensor(k4[:, :, 1::2, :], qk[:, 1].unsqueeze(2).broadcast_to([P, H1, 2, DK1]), k4[:, :, 0::2, :],
                                ALU.subtract).then_inc(S["l4"], 1)

            def contexts_by_token(b):
                dve.wait_ge(S["c3"], b + 1)
                v.transpose(cq1, PD[:, 0:H1 * HS]).then_inc(S["cq1"], 1)

            def denominators(b):
                dve.wait_ge(S["cq1"], b + 1)
                v.reciprocal(rden1[:], cq1.rearrange("p (n d) -> p n d", d=HS)[:, :, DK1]).then_inc(S["rd3"], 1)

            def quotients(b):
                dve.wait_ge(S["rd3"], b + 1)
                v.tensor_tensor(cn1.rearrange("p (n s d) -> p s n d", s=2, d=DK1),
                                cq1.rearrange("p (s n d) -> p s n d", s=2, d=HS)[:, :, :, 0:DK1],
                                rden1[:].rearrange("p (s n) -> p s n", s=2).unsqueeze(3).broadcast_to([P, 2, H1 // 2, DK1]),
                                ALU.mult).then_inc(S["on"], 1)

            def quotients_by_column(b):
                dve.wait_ge(S["on"], b + 1)
                unless_first(dve, S["t3"], b)
                v.transpose(oT.rearrange("p k t -> p (k t)"), cn1).then_inc(S["oT"], 1)

            def logits(b):
                dve.wait_ge(S["te3"], b + 1)
                v.tensor_tensor(lg[:, bass.ds(b, 1), :], PD[:, 512 + T:512 + T + E].unsqueeze(1), br[:].unsqueeze(1), ALU.add
                                ).then_inc(S["lg"], 1)

            def body1(i, results=True, before=True, after=True):
                if after:
                    mean_squares(i + 1)
                kT_out(i)
                if after:
                    factors(i + 1, 0)
                if results:
                    logits(i - 2)
                if after:
                    factors(i + 1, 1)
                if before:
                    contexts_by_token(i - 1)
                if after:
                    factors(i + 1, 2)
                if before:
                    denominators(i - 1)
                if after:
                    factors(i + 1, 3)
                if after:
                    factors(i + 1, 4)
                if before:
                    quotients(i - 1)
                if after:
                    factors(i + 1, 5)
                    factors(i + 1, 6)
                if before:
                    quotients_by_column(i - 1)
                if after:
                    factors(i + 1, 7)
                    factors(i + 1, 8)
                    factors(i + 1, 9)
                    factors(i + 1, 10)
                    scaled_qk(i + 1)
                    low_parts(i + 1)

            mean_squares(0)
            for k in range(STEPS):
                factors(0, k)
            scaled_qk(0)
            low_parts(0)
            body1(0, results=False, before=False)
            body1(1, results=False)
            with dve.Fori(1, U - 1) as u:
                body1(2 * u)
                body1(2 * u + 1)
            body1(LAST - 1)
            body1(LAST, after=False)
            logits(LAST - 1)
            contexts_by_token(LAST)
            denominators(LAST)
            quotients(LAST)
            quotients_by_column(LAST)
            logits(LAST)

            n_r = [0]

            def done(ins):
                ins.then_inc(S["rv"], 1)
                n_r[0] += 1
                dve.wait_ge(S["rv"], n_r[0])

            dve.wait_ge(S["lg"], B)
            wide = lmx[:].unsqueeze(2).broadcast_to([P, B, E])
            done(v.tensor_reduce(lmx[:], lg[:], AX.X, ALU.max))
            v.tensor_tensor(ex[:], lg[:], wide, ALU.subtract).then_inc(S["rx"], 1)
            done(v.tensor_tensor(oh[:], lg[:], wide, ALU.is_equal))
            done(v.tensor_copy(taken[:], oh[:, :, 0]))
            for e in range(1, E):
                last = v.tensor_tensor(oh[:, :, e], oh[:, :, e], taken[:], ALU.is_gt)
                if e < E - 1:
                    done(last)
                    done(v.tensor_tensor(taken[:], oh[:, :, e], taken[:], ALU.max))
            last.then_inc(S["r"], 1)
            dve.wait_ge(S["rx"], 2)
            done(v.tensor_reduce(es[:], ex[:], AX.X, ALU.add))
            v.reciprocal(rows[:, :, 2 * T], es[:]).then_inc(S["rows"], 1)
            dve.wait_ge(S["rp"], 1)
            done(v.tensor_copy(tot[:], PB[:, 0:B * E].rearrange("p (b e) -> p e b", e=E)))
            for e in range(E):
                done(v.tensor_tensor_scan(run[:, e, :], ones[:, 0:B], tot[:, e, :], 0.0, ALU.mult, ALU.add))
            done(v.tensor_scalar(cnt[:], run[:, :, B - 1], float(P - 1), None, ALU.add))
            done(v.tensor_scalar(cnt[:], cnt[:], P.bit_length() - 1, None, ALU.arith_shift_right))
            done(v.tensor_copy(ntile[:], cnt[:]))
            done(v.memset(first[:], 0.0))
            for e in range(1, E):
                done(v.tensor_tensor(first[:, e:e + 1], first[:, e - 1:e], ntile[:, e - 1:e], ALU.add))
            done(v.tensor_tensor(place[:], run[:].rearrange("p e b -> p b e"), tot[:].rearrange("p e b -> p b e"), ALU.subtract))
            done(v.tensor_tensor(place[:], PA[:, 0:B * E].rearrange("p (b e) -> p b e", e=E), place[:], ALU.add))
            done(v.scalar_tensor_tensor(out=place[:], in0=first[:].unsqueeze(1).broadcast_to([P, B, E]), scalar=float(P),
                                        in1=place[:], op0=ALU.mult, op1=ALU.add))
            done(v.tensor_tensor(place[:], place[:], oh[:], ALU.mult))
            done(v.tensor_reduce(slotf[:], place[:], AX.X, ALU.add))
            v.tensor_copy(slot[:], slotf[:]).then_inc(S["slot"], 1)
            tiles = cst[:, C_ROWS:C_ROWS + SLOTS]
            done(v.tensor_scalar(tef[:], tiles, first[:, 1:2], None, ALU.is_ge))
            for e in range(2, E):
                done(v.scalar_tensor_tensor(out=tef[:], in0=tiles, scalar=first[:, e:e + 1], in1=tef[:], op0=ALU.is_ge,
                                            op1=ALU.add))
            v.tensor_copy(te[:], tef[:]).then_inc(S["te"], 1)

            def x_low(j, par):
                dve.wait_ge(S["th"], j + 1)
                v.tensor_tensor(xT_lo[:, par, :], PD[:, 0:T], xT_hi[:, par, :], ALU.subtract).then_inc(S["tl"], 1)

            def hidden(j):
                dve.wait_ge(S["gs"], j + 1)
                dve.wait_ge(S["uu"], j + 1)
                unless_first(dve, S["hT"], j)
                v.tensor_tensor(hh, PB[:], gs, ALU.mult).then_inc(S["hm"], 1)

            def h_low(j):
                dve.wait_ge(S["hTh"], j + 1)
                unless_first(dve, S["y"], j)
                v.tensor_tensor(hT_lo, PC[:], hT_hi, ALU.subtract).then_inc(S["hTl"], 1)

            def result(j, par, half, back):
                dve.wait_ge(S["y"], j + 1)
                dve.wait_ge(S[f"res{par}"], 16 * half + 16)
                if back:
                    dve.wait_ge(S[f"so{par}"], 16 * half)
                v.tensor_copy(tokn[:, par:par + 1], xres[:, par, T + 1:T + 2].bitcast(I32)).then_inc(S["idn"], 1)
                v.scalar_tensor_tensor(out=yo[:, par, :], in0=PD[:, 512:512 + T], scalar=xres[:, par, T:T + 1],
                                       in1=xres[:, par, 0:T], op0=ALU.mult, op1=ALU.add).then_inc(S["yo"], 1)

            x_low(0, 0)
            hidden(0)
            x_low(1, 1)

            def tile(j, par, half, back, more=True):
                h_low(j - 1)
                hidden(j)
                if more:
                    x_low(j + 1, 1 - par)
                result(j - 1, 1 - par, half, back)

            tile(1, 1, 0, False)
            tile(2, 0, 0, False)
            with dve.Fori(1, (SLOTS - 2) // 2) as u:
                tile(2 * u + 1, 1, u, True)
                tile(2 * u + 2, 0, u, True)
            for j in range(SLOTS - 2 + (SLOTS % 2 == 0), SLOTS):
                tile(j, j % 2, (j - 1) // 2, True, j + 1 < SLOTS)
            h_low(SLOTS - 1)
            result(SLOTS - 1, (SLOTS - 1) % 2, (SLOTS - 1) // 2, True)


def kernel(x, cond_2048, L0_cond_Wq, L0_cond_Wo, L0_ffn_lut, L0_ffn_gate_idx, L0_ffn_up_idx, L0_ffn_down_idx,
           L1_cond_W_emb, L1_cond_b_emb, L1_cond_g_norm, L1_cond_W_qkv, L1_cond_g_q, L1_cond_g_k, L1_cond_W_out,
           L1_ffn_Wr, L1_ffn_br, L1_ffn_Wg, L1_ffn_Wu, L1_ffn_Wd):
    import concourse.bacc as bacc
    from concourse.bass_utils import run_bass_kernel_spmd

    def by_rows(w):
        w = np.asarray(w)
        return w.reshape(-1, P, w.shape[-1]).transpose(1, 0, 2).reshape(P, -1)

    down = np.asarray(L0_ffn_down_idx).T
    down = np.concatenate([down, np.zeros((MT * P - INTER, T), down.dtype)])
    arrays = {
        "x": x, "cond": cond_2048, "condT": np.asarray(cond_2048).T.reshape(KT, P, B).transpose(1, 0, 2),
        "consts": constants(), "wqT": np.asarray(L0_cond_Wq).T, "woT": np.asarray(L0_cond_Wo).T,
        "lut": np.asarray(L0_ffn_lut).reshape(1, LUT),
        "idx_all": np.concatenate([by_rows(np.asarray(L0_ffn_gate_idx).T), by_rows(np.asarray(L0_ffn_up_idx).T),
                                   by_rows(down)], axis=1),
        "w_emb": L1_cond_W_emb, "b_emb": np.asarray(L1_cond_b_emb).reshape(4, P).T,
        "g_norm": np.asarray(L1_cond_g_norm).reshape(KT, P).T, "w_qkv": L1_cond_W_qkv,
        "g_q": np.asarray(L1_cond_g_q).reshape(1, DK1), "g_k": np.asarray(L1_cond_g_k).reshape(1, DK1),
        "w_out": L1_cond_W_out, "w_outT": np.asarray(L1_cond_W_out).T, "w_r": L1_ffn_Wr,
        "b_r": np.asarray(L1_ffn_br).reshape(1, E),
        "w_g": by_rows(np.asarray(L1_ffn_Wg).reshape(E * T, FF)), "w_u": by_rows(np.asarray(L1_ffn_Wu).reshape(E * T, FF)),
        "w_d": by_rows(np.asarray(L1_ffn_Wd).reshape(E * FF, T)),
    }
    arrays = {f"in_{k}": np.ascontiguousarray(a) for k, a in arrays.items()}
    nc = bacc.Bacc("TRN2", target_bir_lowering=False, num_devices=1)
    args = [nc.dram_tensor(k, a.shape, mybir.dt.from_np(a.dtype), kind="ExternalInput").ap() for k, a in arrays.items()]
    out = nc.dram_tensor("out", (TOK, T), F32, kind="ExternalOutput").ap()
    routed = nc.dram_tensor("routed", (SLOTS * P, ROW), F32, kind="Internal").ap()
    program(nc, *args, out, routed)
    got = run_bass_kernel_spmd(nc, [arrays], core_ids=[0]).results[0]["out"]
    return got.reshape(B, D, T)
```
